# Optimizing a Trainium2 kernel written in Bass

```python
import numpy as np
import jax
import jax.numpy as jnp

def _softmax(x, axis=-1):
    return jax.nn.softmax(x, axis=axis)

def _gelu(x):
    return jax.nn.gelu(x, approximate=True)

def _silu(x):
    return jax.nn.silu(x)

def _sigmoid(x):
    return jax.nn.sigmoid(x)

def _layernorm(x, axis=-1, eps=1e-05):
    m = jnp.mean(x, axis=axis, keepdims=True)
    v = jnp.var(x, axis=axis, keepdims=True)
    return (x - m) / jnp.sqrt(v + eps)

def _scatter_add(tgt, idx, src, axis=0):
    return tgt.at[idx].add(src)

def _segment_sum(src, seg, n):
    return jax.ops.segment_sum(src, seg, n)
kernel_name = 'mk_hybrid_d1_jaxref_r8_afb619'

def setup_inputs(seed: int=0):
    np.random.seed(seed)
    _w = jnp.asarray

    def _L0_attn_a_setup():
        import jax, jax.numpy as jnp
        import numpy as np
        D_MODEL = 128
        D_STATE = 16
        D_CONV = 8
        EXPAND = 1
        D_INNER = EXPAND * D_MODEL
        DT_RANK = (D_MODEL + 15) // 16
        FFN_HID = 4 * D_MODEL

        def _layernorm(x, g, b, eps=1e-05):
            mu = jnp.mean(x, axis=-1, keepdims=True)
            var = jnp.var(x, axis=-1, keepdims=True)
            return (x - mu) * jax.lax.rsqrt(var + eps) * g + b

        def _mamba(x, in_proj_w, conv_w, conv_b, x_proj_w, dt_proj_w, dt_proj_b, A_log, D_param, out_proj_w):
            B, T, _ = x.shape
            xz = jnp.einsum('btd,ed->bte', x, in_proj_w)
            xin, z = jnp.split(xz, 2, axis=-1)
            xp = jnp.pad(xin, ((0, 0), (D_CONV - 1, 0), (0, 0)))
            xc = sum((xp[:, k:k + T, :] * conv_w[:, k] for k in range(D_CONV))) + conv_b
            xc = jax.nn.silu(xc)
            dbl = jnp.einsum('btd,ed->bte', xc, x_proj_w)
            dt = dbl[..., :DT_RANK]
            Bmat = dbl[..., DT_RANK:DT_RANK + D_STATE]
            Cmat = dbl[..., DT_RANK + D_STATE:]
            delta = jax.nn.softplus(jnp.einsum('btr,dr->btd', dt, dt_proj_w) + dt_proj_b)
            A = -jnp.exp(A_log)
            dA = jnp.exp(delta[..., None] * A)
            dBx = delta[..., None] * Bmat[:, :, None, :] * xc[..., None]

            def step(h, inp):
                dA_t, dBx_t, C_t = inp
                h = h * dA_t + dBx_t
                y = jnp.einsum('bdn,bn->bd', h, C_t)
                return (h, y)
            h0 = jnp.zeros((B, D_INNER, D_STATE), x.dtype)
            _, ys = jax.lax.scan(step, h0, (dA.transpose(1, 0, 2, 3), dBx.transpose(1, 0, 2, 3), Cmat.transpose(1, 0, 2)))
            y = ys.transpose(1, 0, 2) + xc * D_param
            y = y * jax.nn.silu(z)
            return jnp.einsum('btd,ed->bte', y, out_proj_w)
        key = jax.random.key(seed)
        ks = jax.random.split(key, 16)
        s = lambda *shape: 0.02
        x = jax.random.normal(ks[0], (2, 512, D_MODEL), dtype=jnp.float32)
        in_proj_w = jax.random.normal(ks[1], (2 * D_INNER, D_MODEL), dtype=jnp.float32) * 0.02
        conv_w = jax.random.normal(ks[2], (D_INNER, D_CONV), dtype=jnp.float32) * 0.1
        conv_b = jnp.zeros((D_INNER,), jnp.float32)
        x_proj_w = jax.random.normal(ks[3], (DT_RANK + 2 * D_STATE, D_INNER), dtype=jnp.float32) * 0.02
        dt_proj_w = jax.random.normal(ks[4], (D_INNER, DT_RANK), dtype=jnp.float32) * 0.02
        dt_proj_b = jax.random.uniform(ks[5], (D_INNER,), jnp.float32, -4.0, -2.0)
        A_log = jnp.log(jnp.tile(jnp.arange(1, D_STATE + 1, dtype=jnp.float32)[None, :], (D_INNER, 1)))
        D_param = jnp.ones((D_INNER,), jnp.float32)
        out_proj_w = jax.random.normal(ks[6], (D_MODEL, D_INNER), dtype=jnp.float32) * 0.02
        ln1_g = jnp.ones((D_MODEL,), jnp.float32)
        ln1_b = jnp.zeros((D_MODEL,), jnp.float32)
        ln2_g = jnp.ones((D_MODEL,), jnp.float32)
        ln2_b = jnp.zeros((D_MODEL,), jnp.float32)
        w1 = jax.random.normal(ks[7], (FFN_HID, D_MODEL), dtype=jnp.float32) * 0.02
        b1 = jnp.zeros((FFN_HID,), jnp.float32)
        w2 = jax.random.normal(ks[8], (D_MODEL, FFN_HID), dtype=jnp.float32) * 0.02
        b2 = jnp.zeros((D_MODEL,), jnp.float32)
        return dict(x=x, in_proj_w=in_proj_w, conv_w=conv_w, conv_b=conv_b, x_proj_w=x_proj_w, dt_proj_w=dt_proj_w, dt_proj_b=dt_proj_b, A_log=A_log, D_param=D_param, out_proj_w=out_proj_w, ln1_g=ln1_g, ln1_b=ln1_b, ln2_g=ln2_g, ln2_b=ln2_b, w1=w1, b1=b1, w2=w2, b2=b2)
    _L0_attn_a_in = _L0_attn_a_setup()

    def _L0_attn_b_setup():
        import jax, jax.numpy as jnp
        import numpy as np
        import math
        D_MODEL = 128
        NUM_HEADS = 16
        HEAD_DIM = D_MODEL // NUM_HEADS
        LN_EPS = 1e-05

        def _layer_norm(x, g, b):
            mu = jnp.mean(x, axis=-1, keepdims=True)
            var = jnp.mean(jnp.square(x - mu), axis=-1, keepdims=True)
            return (x - mu) * jax.lax.rsqrt(var + LN_EPS) * g + b

        def _rope_tables(seq_len, dim, dtype):
            inv_freq = 1.0 / 10000.0 ** (jnp.arange(0, dim, 2, dtype=jnp.float32) / dim)
            t = jnp.arange(seq_len, dtype=jnp.float32)
            freqs = t[:, None] * inv_freq[None, :]
            emb = jnp.concatenate([freqs, freqs], axis=-1)
            return (jnp.cos(emb).astype(dtype), jnp.sin(emb).astype(dtype))

        def _rotate_half(x):
            x1, x2 = jnp.split(x, 2, axis=-1)
            return jnp.concatenate([-x2, x1], axis=-1)
        key = jax.random.key(seed)
        ks = jax.random.split(key, 8)
        B, S, D = (2, 256, D_MODEL)
        s_in = 1.0 / math.sqrt(D)
        return {'x': jax.random.normal(ks[0], (B, S, D), jnp.float32), 'ln1_g': jnp.ones((D,), jnp.float32), 'ln1_b': jnp.zeros((D,), jnp.float32), 'Wqkv': jax.random.normal(ks[1], (D, 3 * D), jnp.float32) * s_in, 'bqkv': jnp.zeros((3 * D,), jnp.float32), 'Wo': jax.random.normal(ks[2], (D, D), jnp.float32) * s_in, 'bo': jnp.zeros((D,), jnp.float32), 'ln2_g': jnp.ones((D,), jnp.float32), 'ln2_b': jnp.zeros((D,), jnp.float32), 'W1': jax.random.normal(ks[3], (D, 4 * D), jnp.float32) * s_in, 'b1': jnp.zeros((4 * D,), jnp.float32), 'W2': jax.random.normal(ks[4], (4 * D, D), jnp.float32) / math.sqrt(4 * D), 'b2': jnp.zeros((D,), jnp.float32)}
    _L0_attn_b_in = _L0_attn_b_setup()

    def _L0_ffn_setup():
        import jax, jax.numpy as jnp
        import numpy as np
        from jax import lax
        D_MODEL = 128
        D_FF = 512
        NUM_EXPERTS = 24
        TOP_K = 2
        key = jax.random.key(seed)
        ks = jax.random.split(key, 7)
        s1 = 1.0 / np.sqrt(D_MODEL)
        s2 = 1.0 / np.sqrt(D_FF)
        x = jax.random.normal(ks[0], (2, 128, D_MODEL), dtype=jnp.float32)
        gate_w = jax.random.uniform(ks[1], (D_MODEL, NUM_EXPERTS), jnp.float32, -s1, s1)
        gate_b = jax.random.uniform(ks[2], (NUM_EXPERTS,), jnp.float32, -s1, s1)
        w1 = jax.random.uniform(ks[3], (NUM_EXPERTS, D_MODEL, D_FF), jnp.float32, -s1, s1)
        b1 = jax.random.uniform(ks[4], (NUM_EXPERTS, D_FF), jnp.float32, -s1, s1)
        w2 = jax.random.uniform(ks[5], (NUM_EXPERTS, D_FF, D_MODEL), jnp.float32, -s2, s2)
        b2 = jax.random.uniform(ks[6], (NUM_EXPERTS, D_MODEL), jnp.float32, -s2, s2)
        return {'x': x, 'gate_w': gate_w, 'gate_b': gate_b, 'w1': w1, 'b1': b1, 'w2': w2, 'b2': b2}
    _L0_ffn_in = _L0_ffn_setup()
    _d = {'L0_attn_a_x': _L0_attn_a_in['x'], 'L0_attn_a_in_proj_w': _L0_attn_a_in['in_proj_w'], 'L0_attn_a_conv_w': _L0_attn_a_in['conv_w'], 'L0_attn_a_conv_b': _L0_attn_a_in['conv_b'], 'L0_attn_a_x_proj_w': _L0_attn_a_in['x_proj_w'], 'L0_attn_a_dt_proj_w': _L0_attn_a_in['dt_proj_w'], 'L0_attn_a_dt_proj_b': _L0_attn_a_in['dt_proj_b'], 'L0_attn_a_A_log': _L0_attn_a_in['A_log'], 'L0_attn_a_D_param': _L0_attn_a_in['D_param'], 'L0_attn_a_out_proj_w': _L0_attn_a_in['out_proj_w'], 'L0_attn_a_ln1_g': _L0_attn_a_in['ln1_g'], 'L0_attn_a_ln1_b': _L0_attn_a_in['ln1_b'], 'L0_attn_a_ln2_g': _L0_attn_a_in['ln2_g'], 'L0_attn_a_ln2_b': _L0_attn_a_in['ln2_b'], 'L0_attn_a_w1': _L0_attn_a_in['w1'], 'L0_attn_a_b1': _L0_attn_a_in['b1'], 'L0_attn_a_w2': _L0_attn_a_in['w2'], 'L0_attn_a_b2': _L0_attn_a_in['b2'], 'L0_attn_b_ln1_g': _L0_attn_b_in['ln1_g'], 'L0_attn_b_ln1_b': _L0_attn_b_in['ln1_b'], 'L0_attn_b_Wqkv': _L0_attn_b_in['Wqkv'], 'L0_attn_b_bqkv': _L0_attn_b_in['bqkv'], 'L0_attn_b_Wo': _L0_attn_b_in['Wo'], 'L0_attn_b_bo': _L0_attn_b_in['bo'], 'L0_attn_b_ln2_g': _L0_attn_b_in['ln2_g'], 'L0_attn_b_ln2_b': _L0_attn_b_in['ln2_b'], 'L0_attn_b_W1': _L0_attn_b_in['W1'], 'L0_attn_b_b1': _L0_attn_b_in['b1'], 'L0_attn_b_W2': _L0_attn_b_in['W2'], 'L0_attn_b_b2': _L0_attn_b_in['b2'], 'L0_ffn_gate_w': _L0_ffn_in['gate_w'], 'L0_ffn_gate_b': _L0_ffn_in['gate_b'], 'L0_ffn_w1': _L0_ffn_in['w1'], 'L0_ffn_b1': _L0_ffn_in['b1'], 'L0_ffn_w2': _L0_ffn_in['w2'], 'L0_ffn_b2': _L0_ffn_in['b2']}
    _x0 = _d['L0_attn_a_x']
    _d['L0_attn_a_x'] = jax.random.normal(jax.random.fold_in(jax.random.key(seed), 1), (4, 512, 128), dtype=_x0.dtype)
    del _x0
    return _d

def reference(L0_attn_a_x, L0_attn_a_in_proj_w, L0_attn_a_conv_w, L0_attn_a_conv_b, L0_attn_a_x_proj_w, L0_attn_a_dt_proj_w, L0_attn_a_dt_proj_b, L0_attn_a_A_log, L0_attn_a_D_param, L0_attn_a_out_proj_w, L0_attn_a_ln1_g, L0_attn_a_ln1_b, L0_attn_a_ln2_g, L0_attn_a_ln2_b, L0_attn_a_w1, L0_attn_a_b1, L0_attn_a_w2, L0_attn_a_b2, L0_attn_b_ln1_g, L0_attn_b_ln1_b, L0_attn_b_Wqkv, L0_attn_b_bqkv, L0_attn_b_Wo, L0_attn_b_bo, L0_attn_b_ln2_g, L0_attn_b_ln2_b, L0_attn_b_W1, L0_attn_b_b1, L0_attn_b_W2, L0_attn_b_b2, L0_ffn_gate_w, L0_ffn_gate_b, L0_ffn_w1, L0_ffn_b1, L0_ffn_w2, L0_ffn_b2):

    def _L0_attn_a_ref(x, in_proj_w, conv_w, conv_b, x_proj_w, dt_proj_w, dt_proj_b, A_log, D_param, out_proj_w, ln1_g, ln1_b, ln2_g, ln2_b, w1, b1, w2, b2):
        import jax, jax.numpy as jnp
        import numpy as np
        D_MODEL = 128
        D_STATE = 16
        D_CONV = 8
        EXPAND = 1
        D_INNER = EXPAND * D_MODEL
        DT_RANK = (D_MODEL + 15) // 16
        FFN_HID = 4 * D_MODEL

        def _layernorm(x, g, b, eps=1e-05):
            mu = jnp.mean(x, axis=-1, keepdims=True)
            var = jnp.var(x, axis=-1, keepdims=True)
            return (x - mu) * jax.lax.rsqrt(var + eps) * g + b

        def _mamba(x, in_proj_w, conv_w, conv_b, x_proj_w, dt_proj_w, dt_proj_b, A_log, D_param, out_proj_w):
            B, T, _ = x.shape
            xz = jnp.einsum('btd,ed->bte', x, in_proj_w)
            xin, z = jnp.split(xz, 2, axis=-1)
            xp = jnp.pad(xin, ((0, 0), (D_CONV - 1, 0), (0, 0)))
            xc = sum((xp[:, k:k + T, :] * conv_w[:, k] for k in range(D_CONV))) + conv_b
            xc = jax.nn.silu(xc)
            dbl = jnp.einsum('btd,ed->bte', xc, x_proj_w)
            dt = dbl[..., :DT_RANK]
            Bmat = dbl[..., DT_RANK:DT_RANK + D_STATE]
            Cmat = dbl[..., DT_RANK + D_STATE:]
            delta = jax.nn.softplus(jnp.einsum('btr,dr->btd', dt, dt_proj_w) + dt_proj_b)
            A = -jnp.exp(A_log)
            dA = jnp.exp(delta[..., None] * A)
            dBx = delta[..., None] * Bmat[:, :, None, :] * xc[..., None]

            def step(h, inp):
                dA_t, dBx_t, C_t = inp
                h = h * dA_t + dBx_t
                y = jnp.einsum('bdn,bn->bd', h, C_t)
                return (h, y)
            h0 = jnp.zeros((B, D_INNER, D_STATE), x.dtype)
            _, ys = jax.lax.scan(step, h0, (dA.transpose(1, 0, 2, 3), dBx.transpose(1, 0, 2, 3), Cmat.transpose(1, 0, 2)))
            y = ys.transpose(1, 0, 2) + xc * D_param
            y = y * jax.nn.silu(z)
            return jnp.einsum('btd,ed->bte', y, out_proj_w)
        x = x + _mamba(_layernorm(x, ln1_g, ln1_b), in_proj_w, conv_w, conv_b, x_proj_w, dt_proj_w, dt_proj_b, A_log, D_param, out_proj_w)
        h = _layernorm(x, ln2_g, ln2_b)
        h = jax.nn.relu(jnp.einsum('btd,hd->bth', h, w1) + b1)
        x = x + jnp.einsum('bth,dh->btd', h, w2) + b2
        return x

    def _L0_attn_b_ref(x, ln1_g, ln1_b, Wqkv, bqkv, Wo, bo, ln2_g, ln2_b, W1, b1, W2, b2):
        import jax, jax.numpy as jnp
        import numpy as np
        import math
        D_MODEL = 128
        NUM_HEADS = 16
        HEAD_DIM = D_MODEL // NUM_HEADS
        LN_EPS = 1e-05

        def _layer_norm(x, g, b):
            mu = jnp.mean(x, axis=-1, keepdims=True)
            var = jnp.mean(jnp.square(x - mu), axis=-1, keepdims=True)
            return (x - mu) * jax.lax.rsqrt(var + LN_EPS) * g + b

        def _rope_tables(seq_len, dim, dtype):
            inv_freq = 1.0 / 10000.0 ** (jnp.arange(0, dim, 2, dtype=jnp.float32) / dim)
            t = jnp.arange(seq_len, dtype=jnp.float32)
            freqs = t[:, None] * inv_freq[None, :]
            emb = jnp.concatenate([freqs, freqs], axis=-1)
            return (jnp.cos(emb).astype(dtype), jnp.sin(emb).astype(dtype))

        def _rotate_half(x):
            x1, x2 = jnp.split(x, 2, axis=-1)
            return jnp.concatenate([-x2, x1], axis=-1)
        B, S, D = x.shape
        H, hd = (NUM_HEADS, HEAD_DIM)
        normed = _layer_norm(x, ln1_g, ln1_b)
        qkv = (normed @ Wqkv + bqkv).reshape(B, S, 3, H, hd)
        qkv = jnp.transpose(qkv, (2, 0, 3, 1, 4))
        q, k, v = (qkv[0], qkv[1], qkv[2])
        cos, sin = _rope_tables(S, hd, q.dtype)
        cos = cos[None, None, :, :]
        sin = sin[None, None, :, :]
        q = q * cos + _rotate_half(q) * sin
        k = k * cos + _rotate_half(k) * sin
        scores = jnp.einsum('bhqd,bhkd->bhqk', q, k) / math.sqrt(hd)
        causal = jnp.triu(jnp.ones((S, S), dtype=bool), k=1)
        scores = jnp.where(causal[None, None], -jnp.inf, scores)
        attn = jax.nn.softmax(scores, axis=-1)
        attn_out = jnp.einsum('bhqk,bhkd->bhqd', attn, v)
        attn_out = jnp.transpose(attn_out, (0, 2, 1, 3)).reshape(B, S, D)
        attn_out = attn_out @ Wo + bo
        x = x + attn_out
        h = _layer_norm(x, ln2_g, ln2_b)
        h = jax.nn.gelu(h @ W1 + b1, approximate=False) @ W2 + b2
        return x + h

    def _L0_ffn_ref(x, gate_w, gate_b, w1, b1, w2, b2):
        import jax, jax.numpy as jnp
        import numpy as np
        from jax import lax
        D_MODEL = 128
        D_FF = 512
        NUM_EXPERTS = 24
        TOP_K = 2
        gate_scores = jnp.einsum('bsd,de->bse', x, gate_w) + gate_b
        topk_val, topk_idx = lax.top_k(gate_scores, TOP_K)
        sparse_gates = jax.nn.softmax(topk_val, axis=-1)
        combine = jnp.sum(jax.nn.one_hot(topk_idx, NUM_EXPERTS, dtype=x.dtype) * sparse_gates[..., None], axis=-2)
        h = jax.nn.gelu(jnp.einsum('bsd,edf->besf', x, w1) + b1[None, :, None, :], approximate=False)
        y = jnp.einsum('besf,efd->besd', h, w2) + b2[None, :, None, :]
        out = jnp.einsum('bse,besd->bsd', combine, y)
        return out + x
    x = L0_attn_a_x
    x = x + _L0_attn_a_ref(_layernorm(x, axis=-1), L0_attn_a_in_proj_w, L0_attn_a_conv_w, L0_attn_a_conv_b, L0_attn_a_x_proj_w, L0_attn_a_dt_proj_w, L0_attn_a_dt_proj_b, L0_attn_a_A_log, L0_attn_a_D_param, L0_attn_a_out_proj_w, L0_attn_a_ln1_g, L0_attn_a_ln1_b, L0_attn_a_ln2_g, L0_attn_a_ln2_b, L0_attn_a_w1, L0_attn_a_b1, L0_attn_a_w2, L0_attn_a_b2)
    x = x + _L0_ffn_ref(_layernorm(x, axis=-1), L0_ffn_gate_w, L0_ffn_gate_b, L0_ffn_w1, L0_ffn_b1, L0_ffn_w2, L0_ffn_b2)
    x = x + _L0_attn_b_ref(_layernorm(x, axis=-1), L0_attn_b_ln1_g, L0_attn_b_ln1_b, L0_attn_b_Wqkv, L0_attn_b_bqkv, L0_attn_b_Wo, L0_attn_b_bo, L0_attn_b_ln2_g, L0_attn_b_ln2_b, L0_attn_b_W1, L0_attn_b_b1, L0_attn_b_W2, L0_attn_b_b2)
    x = x + _L0_ffn_ref(_layernorm(x, axis=-1), L0_ffn_gate_w, L0_ffn_gate_b, L0_ffn_w1, L0_ffn_b1, L0_ffn_w2, L0_ffn_b2)
    return x

_drawn_inputs = setup_inputs


def setup_inputs(seed=0):
    import zlib

    import numpy as np

    out = dict(_drawn_inputs(seed))
    spreads = {'L0_attn_a_conv_b': (0.0, 0.8),
     'L0_attn_a_D_param': (1.0, 0.6),
     'L0_attn_a_ln1_g': (1.0, 0.6),
     'L0_attn_a_ln1_b': (0.0, 0.8),
     'L0_attn_a_ln2_g': (1.0, 0.6),
     'L0_attn_a_ln2_b': (0.0, 2.0),
     'L0_attn_a_b1': (0.0, 2.0),
     'L0_attn_a_b2': (0.0, 0.8),
     'L0_attn_b_ln1_g': (1.0, 0.6),
     'L0_attn_b_ln1_b': (0.0, 0.8),
     'L0_attn_b_bqkv': (0.0, 0.8),
     'L0_attn_b_bo': (0.0, 0.8),
     'L0_attn_b_ln2_g': (1.0, 0.6),
     'L0_attn_b_ln2_b': (0.0, 2.0),
     'L0_attn_b_b1': (0.0, 2.0),
     'L0_attn_b_b2': (0.0, 2.0)}
    factors = {'L0_attn_a_in_proj_w': 8.0,
     'L0_attn_a_conv_w': 8.0,
     'L0_attn_a_x_proj_w': 8.0,
     'L0_attn_a_dt_proj_w': 8.0,
     'L0_attn_a_dt_proj_b': 8.0,
     'L0_attn_a_A_log': 8.0,
     'L0_attn_a_out_proj_w': 8.0,
     'L0_ffn_gate_b': 23.536,
     'L0_ffn_b1': 64.0,
     'L0_ffn_b2': 47.344,
     'L0_attn_a_w1': 8.0,
     'L0_attn_a_w2': 8.0,
     'L0_attn_b_Wqkv': 2.87,
     'L0_attn_b_Wo': 2.688,
     'L0_ffn_gate_w': 4.959,
     'L0_ffn_w1': 6.889,
     'L0_ffn_w2': 5.527}
    for name, (base, spread) in spreads.items():
        noise = np.random.default_rng([zlib.crc32(name.encode()), seed]).standard_normal(out[name].shape)
        drawn = base * np.exp(spread * noise) if base else spread * noise
        out[name] = jnp.asarray(drawn.astype(out[name].dtype))
    for name, factor in factors.items():
        out[name] = (out[name] * factor).astype(out[name].dtype)
    return out
```

```python
from contextlib import ExitStack

import numpy as np

import concourse.bass as bass
from concourse import mybir

P = 128
D = 128
NB = 4
T = 512
TT = T // P
NT = NB * TT
NS = 16
NCONV = 8
RANK = 8
FF = 512
FB = FF // P
NE = 24
TOPK = 2
SLOT_TILES = (NB * T * TOPK - NE) // P + NE
SLOT_TILES += SLOT_TILES % 2
NH = 16
HD = 8
EPS = 1e-5
LOAD_EXPERTS = 4
LEAD = 4
FAR = -1.0e30

F32 = mybir.dt.float32
BF16 = mybir.dt.bfloat16
I32 = mybir.dt.int32
U32 = mybir.dt.uint32
ACT = mybir.ActivationFunctionType
ALU = mybir.AluOpType
AX_X = mybir.AxisListType.X



class Core:

    def __init__(self, nc, ctx, io):
        self.nc, self.ctx, self.io = nc, ctx, io
        self.retired = []
        self.bank = ctx.enter_context(nc.psum_tensor("bank", [P, 8, T], F32))
        self.X = self.sb("X", [P, NT, D])
        self.ident = self.sb("ident", [P, P])
        self.identb = self.sb("identb", [P, P], BF16)
        self.half = self.sb("half", [P, TT])
        self.ones_row = self.sb("ones_row", [1, P])
        self.w1all = self.sb("w1all", [P, NE, FF])
        self.w2all = self.sb("w2all", [P, NE, FB, D])
        self.experts_in = self.sem("experts_in")
        self.slots_in = nc.dram_tensor("slots_in", (SLOT_TILES * P, D), F32).ap()
        self.slots_out = nc.dram_tensor("slots_out", (SLOT_TILES * P, D), F32).ap()
        self.slots_zeroed = self.sem("slots_zeroed")
        self.consts_in = self.sem("consts_in")
        self.scattered = self.sem("scattered")
        self.gathered = [self.sem(f"gathered{i}") for i in range(NT)]
        self.consts_set = self.sem("consts_set")
        self.apart = self.sem("apart")
        self.identb_set = self.sem("identb_set")

    def sb(self, name, shape, dt=F32, ctx=None):
        return (ctx or self.ctx).enter_context(self.nc.sbuf_tensor(name, shape, dt))

    def sem(self, name, ctx=None):
        return (ctx or self.ctx).enter_context(self.nc.semaphore(name))

    def tiles(self, k):
        return self.bank[:, k, :].rearrange("p (t n) -> p t n", n=P)


class Stage:

    def __init__(self, core, tag):
        self.core, self.tag, self.ctx = core, tag, ExitStack()
        self.leading, self.sems = [], []

    def sb(self, name, shape, dt=F32):
        return self.core.sb(f"{self.tag}_{name}", shape, dt, self.ctx)

    def sem(self, name):
        s = self.core.sem(f"{self.tag}_{name}", self.ctx)
        self.sems.append(s)
        return s

    def lead(self, name):
        s = self.sem(name)
        self.leading.append(s)
        return s

    def set_leads(self, g):
        for s in self.leading:
            g.sem_inc(s, LEAD)
        for s in self.core.retired:
            g.sem_clear(s)
        self.core.retired = self.sems


class Norm:

    def __init__(self, st, name):
        self.stats = st.sb(name + "_stats", [P, TT, 6])
        self.mv = st.sb(name + "_mv", [P, TT, 2])
        self.ve = st.sb(name + "_ve", [P, TT])
        self.rs = st.sb(name + "_rs", [P, TT])
        self.stats_done = st.sem(name + "_stats_done")
        self.mean_var_ready = st.sem(name + "_mean_var_ready")
        self.var_eps_ready = st.sem(name + "_var_eps_ready")
        self.rstd_ready = st.sem(name + "_rstd_ready")
        self.normed = st.sem(name + "_normed")


def apart(eng, core):
    eng.sem_inc(core.apart, 1)


def norm_vector(v, core, ln, i, src, dst, before=None, also=None):
    apart(v, core)
    for t in range(TT):
        v.bn_stats(ln.stats[:, t, :], src(t)).then_inc(ln.stats_done, 1)
    v.wait_ge(ln.stats_done, TT * i + TT)
    apart(v, core)
    for t in range(TT):
        v.bn_aggr(ln.mv[:, t, :], ln.stats[:, t, :]).then_inc(ln.mean_var_ready, 1)
    v.wait_ge(ln.mean_var_ready, TT * i + TT)
    for reader in (before, also):
        if reader:
            v.wait_ge(*reader)
    v.wait_ge(ln.rstd_ready, i + 1)
    for t in range(TT):
        v.tensor_scalar(dst(t), src(t), ln.mv[:, t, 0:1], ln.rs[:, t:t + 1],
                        ALU.subtract, ALU.mult).then_inc(ln.normed, 1)


def norm_pool(g, core, ln, i):
    g.wait_ge(ln.mean_var_ready, TT * i + TT)
    apart(g, core)
    g.tensor_scalar(ln.ve[:], ln.mv[:, :, 1], EPS, None, ALU.add).then_inc(ln.var_eps_ready, 1)
    g.wait_ge(ln.var_eps_ready, i + 1)
    g.tensor_tensor(ln.rs[:], ln.ve[:], core.half[:], ALU.pow).then_inc(ln.rstd_ready, 1)


def row(x, i):
    return x[:, bass.ds(i, 1), :].rearrange("p a n -> p (a n)")


def mamba(core):
    nc, io, bank, X = core.nc, core.io, core.bank, core.X
    st = Stage(core, "m")
    win = st.sb("win", [P, 2 * D])
    convw = st.sb("convw", [P, NCONV])
    vec = st.sb("vec", [P, 7])
    LN1G, LN1B, CONVB, DTB, DSKIP, LN2G, LN2B = range(7)
    wx = st.sb("wx", [P, RANK + 96])
    wdt = st.sb("wdt", [RANK, P])
    a_neg = st.sb("a_neg", [P, NS])
    wout = st.sb("wout", [P, D])
    w1 = st.sb("w1", [P, FF])
    b1 = st.sb("b1", [P, FB])
    w2 = st.sb("w2", [P, FB, D])
    b2row = st.sb("b2row", [1, D])
    taps = st.sb("taps", [P, NCONV, P])
    dskip = st.sb("dskip", [P, P])
    pick_s = st.sb("pick_s", [96, 32])
    pick = st.sb("pick", [96, 32, P], BF16)

    X1 = st.sb("X1", [P, NT, D])
    un = st.sb("un", [P, TT, D])
    uT = st.sb("uT", [P, T])
    xpad = st.sb("xpad", [P, NCONV - 1 + T])
    XC = st.sb("XC", [P, NB, T])
    SZ = st.sb("SZ", [P, NB, T])
    DELTA = st.sb("DELTA", [P, NB, T])
    DX = st.sb("DX", [P, NB, T])
    BC = st.sb("BC", [96, NB, T], BF16)
    dt_sb = st.sb("dt_sb", [RANK, T])
    rest = st.sb("rest", [96, T])
    mid = st.sb("mid", [96, T], BF16)
    work = st.sb("work", [P, 8, T])
    EXPV, RELU = work[:, 0:NB, :], work[:, NB:2 * NB, :]
    decay, h, c_sb, hc = (work[:, 2 * i:2 * i + 2, :] for i in range(4))
    hT = work[:, 0:FB, :]
    yz = st.sb("yz", [P, T])
    absv = yz
    xa = st.sb("xa", [P, TT, D])

    x_in, w_in, vec_in, alog_in, pick_in = map(st.sem, ("x_in", "w_in", "vec_in", "alog_in", "pick_in"))
    zeros, zeros_set = st.sb("zeros", [P, D]), st.sem("zeros_set")
    edge_set = st.sem("edge_set")
    a_exp, a_ready = st.sem("a_exp"), st.sem("a_ready")
    taps_ready, pick_ready = st.sem("taps_ready"), st.sem("pick_ready")
    ln_x, ln_1, ln_2 = Norm(st, "ln_x"), Norm(st, "ln_1"), Norm(st, "ln_2")
    un_turned, uT_ready, xin_ready, z_ready = map(st.lead, ("un_turned", "uT_ready", "xin_ready", "z_ready"))
    xpad_ready, sz_ready, conv_ready, xc_ready = map(st.lead, ("xpad_ready", "sz_ready", "conv_ready", "xc_ready"))
    dt_ready, dt_copied, bc_ready, bc_split = map(st.lead, ("dt_ready", "dt_copied", "bc_ready", "bc_split"))
    split_step = st.sem("split_step")
    dpre_ready, abs_ready, exp_ready, relu_ready = map(st.lead, ("dpre_ready", "abs_ready", "exp_ready", "relu_ready"))
    onep_ready, lnv_ready, delta_step, dx_ready = map(st.sem, ("onep_ready", "lnv_ready", "delta_step", "dx_ready"))
    b_ready, c_ready, decay_ready, dbx_ready = map(st.lead, ("b_ready", "c_ready", "decay_ready", "dbx_ready"))
    h_ready, c_copied, hc_ready, hc_summed = map(st.lead, ("h_ready", "c_copied", "hc_ready", "hc_summed"))
    y_ready = st.sem("y_ready")
    yz_ready, proj_ready, xa_ready = map(st.lead, ("yz_ready", "proj_ready", "xa_ready"))
    xa_turned, xaT_ready, h1_ready, h1_relu = map(st.lead, ("xa_turned", "xaT_ready", "h1_ready", "h1_relu"))
    ffn_ready, xf_ready, x_done = map(st.lead, ("ffn_ready", "xf_ready", "x_done"))

    with st.ctx, nc.Block() as block:
        W_LOADS = 12

        @block.sync
        def _(sp):
            sp.dma_start(X[:], io["x"].rearrange("b (t p) d -> p (b t) d", p=P)).then_inc(x_in, 16)
            sp.dma_start(core.ident[:], io["ident"]).then_inc(core.consts_in, 16)
            sp.dma_start(pick_s[:], io["pick"]).then_inc(pick_in, 16)
            sp.dma_start(a_neg[:], io["a_log"]).then_inc(alog_in, 16)
            sp.dma_start(win[:], io["in_proj_t"]).then_inc(w_in, 16)
            sp.dma_start(convw[:], io["conv_w"]).then_inc(vec_in, 16)
            sp.dma_start(vec[:], io["vec_a"]).then_inc(vec_in, 16)
            sp.dma_start(wx[:, 0:RANK], io["x_proj_t"][:, 0:RANK]).then_inc(w_in, 16)
            for r in range(3):
                sp.dma_start(wx[:, RANK + 32 * r:RANK + 32 * r + 32],
                             io["x_proj_t"][:, RANK:RANK + 32]).then_inc(w_in, 16)
            sp.dma_start(wdt[:], io["dt_proj_t"]).then_inc(w_in, 16)
            sp.dma_start(wout[:], io["out_proj_t"]).then_inc(w_in, 16)
            sp.dma_start(w1[:], io["a_w1_t"]).then_inc(w_in, 16)
            sp.dma_start(b1[:], io["a_b1_t"]).then_inc(w_in, 16)
            sp.dma_start(w2[:], io["a_w2_t"].rearrange("(f p) n -> p f n", p=P)).then_inc(w_in, 16)
            sp.dma_start(b2row[:], io["a_b2"]).then_inc(w_in, 16)
            sp.dma_start(core.identb[:], io["identb"]).then_inc(w_in, 16)
            for e in range(0, NE, LOAD_EXPERTS):
                sp.dma_start(core.w1all[:, e:e + LOAD_EXPERTS, :],
                             io["e_w1"][e:e + LOAD_EXPERTS].rearrange("e d f -> d e f")).then_inc(core.experts_in, 16)
                sp.dma_start(core.w2all[:, e:e + LOAD_EXPERTS, :, :].rearrange("p e k n -> p (e k) n"),
                             io["e_w2"][e:e + LOAD_EXPERTS].rearrange("e (k p) n -> p (e k) n", p=P))\
                    .then_inc(core.experts_in, 16)
            sp.wait_ge(zeros_set, 1)
            sp.dma_start(core.slots_in.rearrange("(j p) d -> p j d", p=P),
                         zeros[:].unsqueeze(1).to_broadcast([P, SLOT_TILES, D])).then_inc(core.slots_zeroed, 16)

        @block.gpsimd
        def _(g):
            st.set_leads(g)
            g.memset(core.half[:], -0.5).then_inc(core.consts_set, 1)
            g.memset(core.ones_row[:], 1.0).then_inc(core.consts_set, 1)
            g.memset(xpad[:, 0:NCONV - 1], 0.0).then_inc(edge_set, 1)
            g.memset(zeros[:], 0.0).then_inc(zeros_set, 1)
            g.wait_ge(core.consts_set, 2)
            with g.Fori(0, NB) as b:
                norm_pool(g, core, ln_x, b)
                norm_pool(g, core, ln_1, b)

            with g.Fori(0, NS) as n:
                for b in range(NB):
                    k = n * NB + b
                    g.wait_ge(h_ready, LEAD + k + 1)
                    g.wait_ge(c_copied, LEAD + k + 1)
                    g.wait_ge(hc_summed, LEAD + k - 1)
                    g.tensor_tensor(hc[:, b % 2, :], h[:, b % 2, :], c_sb[:, b % 2, :],
                                    ALU.mult).then_inc(hc_ready, 1)
            with g.Fori(0, NB) as b:
                norm_pool(g, core, ln_2, b)

        @block.scalar
        def _(act):
            act.wait_ge(vec_in, 32)
            act.wait_ge(w_in, 16 * W_LOADS)
            act.wait_ge(edge_set, 1)
            with act.Fori(0, NB) as b:
                act.wait_ge(un_turned, LEAD + TT * b + TT)
                act.activation(uT[:], bank[:, 0, :], ACT.Identity, bias=vec[:, LN1B:LN1B + 1],
                               scale=vec[:, LN1G:LN1G + 1]).then_inc(uT_ready, 1)
                act.wait_ge(xin_ready, LEAD + b + 1)
                act.activation(xpad[:, NCONV - 1:], bank[:, 1, :], ACT.Identity).then_inc(xpad_ready, 1)
                act.wait_ge(z_ready, LEAD + b + 1)
                apart(act, core)
                act.activation(row(SZ, b), bank[:, 2, :], ACT.Silu).then_inc(sz_ready, 1)
                act.wait_ge(conv_ready, LEAD + b + 1)
                apart(act, core)
                act.activation(row(XC, b), bank[:, 3, :], ACT.Silu,
                               bias=vec[:, CONVB:CONVB + 1]).then_inc(xc_ready, 1)
            act.preload_act_table(ACT.Exp)
            act.wait_ge(alog_in, 16)
            act.activation(a_neg[:], a_neg[:], ACT.Exp).then_inc(a_exp, 1)
            with act.Fori(0, NB) as b:
                act.wait_ge(exp_ready, LEAD + b)
                act.wait_ge(dpre_ready, LEAD + b + 1)
                act.activation(absv[:], bank[:, 6, :], ACT.Abs, bias=vec[:, DTB:DTB + 1]).then_inc(abs_ready, 1)
                act.wait_ge(abs_ready, LEAD + b + 1)
                apart(act, core)
                act.activation(row(EXPV, b), absv[:], ACT.Exp, scale=-1.0).then_inc(exp_ready, 1)
            act.preload_act_table(ACT.Ln)
            act.wait_ge(onep_ready, 1)
            act.activation(DELTA[:], DX[:], ACT.Ln).then_inc(lnv_ready, 1)
            act.preload_act_table(ACT.Exp)
            act.wait_ge(a_ready, 1)
            act.wait_ge(dx_ready, 1)
            with act.Fori(0, NS) as n:
                for b in range(NB):
                    k = n * NB + b
                    act.wait_ge(h_ready, LEAD + k - 1)
                    apart(act, core)
                    act.activation(decay[:, b % 2, :], DELTA[:, b, :], ACT.Exp,
                                   scale=a_neg[:, bass.ds(n, 1)]).then_inc(decay_ready, 1)
                    act.wait_ge(c_ready, LEAD + k + 1)
                    act.wait_ge(hc_ready, LEAD + k - 1)
                    act.activation(c_sb[:, b % 2, :], bank[:, 6 + b % 2, :], ACT.Identity).then_inc(c_copied, 1)
            with act.Fori(0, NB) as b:
                act.wait_ge(xa_turned, LEAD + TT * b + TT)
                act.activation(uT[:], bank[:, 5, :], ACT.Identity, bias=vec[:, LN2B:LN2B + 1],
                               scale=vec[:, LN2G:LN2G + 1]).then_inc(xaT_ready, 1)
                act.wait_ge(ffn_ready, LEAD + b)
                for f in range(FB):
                    act.wait_ge(h1_ready, LEAD + FB * b + f + 1)
                    act.activation(hT[:, f, :], bank[:, 6 + f % 2, :], ACT.Relu,
                                   bias=b1[:, f:f + 1]).then_inc(h1_relu, 1)

        @block.vector
        def _(v):
            v.wait_ge(core.consts_in, 16)
            v.wait_ge(vec_in, 32)
            for j in range(NCONV):
                v.tensor_scalar(taps[:, j, :], core.ident[:], convw[:, j:j + 1], None, ALU.mult).then_inc(taps_ready, 1)
            v.tensor_scalar(dskip[:], core.ident[:], vec[:, DSKIP:DSKIP + 1], None, ALU.mult).then_inc(taps_ready, 1)
            v.wait_ge(x_in, 16)
            v.wait_ge(core.consts_set, 2)
            with v.Fori(0, NB) as b:
                norm_vector(v, core, ln_x, b, lambda t: row(X, b * TT + t), lambda t: row(X1, b * TT + t))
                v.wait_ge(ln_x.normed, TT * b + TT)
                norm_vector(v, core, ln_1, b, lambda t: row(X1, b * TT + t), lambda t: un[:, t, :],
                            before=(un_turned, LEAD + TT * b))
            v.wait_ge(pick_in, 16)
            v.tensor_copy(pick[:], pick_s[:].unsqueeze(2).to_broadcast([96, 32, P])).then_inc(pick_ready, 1)
            v.wait_ge(a_exp, 1)
            v.tensor_scalar(a_neg[:], a_neg[:], -1.0, None, ALU.mult).then_inc(a_ready, 1)
            SPLIT = 3
            with v.Fori(0, NB) as b:
                v.wait_ge(dt_ready, LEAD + b + 1)
                v.tensor_copy(dt_sb[:], bank[0:RANK, 4, :]).then_inc(dt_copied, 1)
                v.wait_ge(bc_ready, LEAD + b + 1)
                v.tensor_copy(row(BC, b), bank[0:96, 5, :]).then_inc(split_step, 1)
                v.wait_ge(split_step, b * SPLIT + 1)
                v.tensor_tensor(rest[:], bank[0:96, 5, :], row(BC, b), ALU.subtract).then_inc(split_step, 1)
                v.wait_ge(split_step, b * SPLIT + 2)
                v.tensor_copy(mid[:], rest[:]).then_inc(split_step, 1)
                v.wait_ge(split_step, b * SPLIT + 3)
                v.tensor_copy(BC[32:64, bass.ds(b, 1), :], mid[32:64, :].unsqueeze(1))
                v.tensor_tensor(BC[64:96, bass.ds(b, 1), :], rest[64:96, :].unsqueeze(1),
                                mid[64:96, :].unsqueeze(1), ALU.subtract).then_inc(bc_split, 1)
                v.wait_ge(dpre_ready, LEAD + b + 1)
                v.wait_ge(abs_ready, LEAD + b + 1)
                apart(v, core)
                v.tensor_scalar(row(RELU, b), bank[:, 6, :], vec[:, DTB:DTB + 1], 0.0,
                                ALU.add, ALU.max).then_inc(relu_ready, 1)
            v.wait_ge(exp_ready, LEAD + NB)
            v.tensor_scalar(DX[:], EXPV, 1.0, None, ALU.add).then_inc(onep_ready, 1)
            v.wait_ge(onep_ready, 1)
            v.scalar_tensor_tensor(out=EXPV, in0=DX[:], scalar=1.0, in1=EXPV,
                                   op0=ALU.subtract, op1=ALU.subtract).then_inc(delta_step, 1)
            v.wait_ge(delta_step, 1)
            v.wait_ge(relu_ready, LEAD + NB)
            v.tensor_tensor(RELU, RELU, EXPV, ALU.subtract).then_inc(delta_step, 1)
            v.wait_ge(delta_step, 2)
            v.wait_ge(lnv_ready, 1)
            v.tensor_tensor(DELTA[:], DELTA[:], RELU, ALU.add).then_inc(delta_step, 1)
            v.wait_ge(delta_step, 3)
            v.wait_ge(xc_ready, LEAD + NB)
            v.tensor_tensor(DX[:], DELTA[:], XC[:], ALU.mult).then_inc(dx_ready, 1)
            v.wait_ge(dx_ready, 1)
            with v.Fori(0, NS) as n:
                for b in range(NB):
                    k = n * NB + b
                    v.wait_ge(b_ready, LEAD + k + 1)
                    v.tensor_tensor(bank[:, 4 + b % 2, :], bank[:, 4 + b % 2, :], DX[:, b, :],
                                    ALU.mult).then_inc(dbx_ready, 1)
                    v.wait_ge(dbx_ready, LEAD + k + 1)
                    v.wait_ge(decay_ready, LEAD + k + 1)
                    v.wait_ge(hc_ready, LEAD + k - 1)
                    v.tensor_tensor_scan(h[:, b % 2, :], decay[:, b % 2, :], bank[:, 4 + b % 2, :],
                                         0.0, ALU.mult, ALU.add).then_inc(h_ready, 1)
            with v.Fori(0, NB) as b:
                v.wait_ge(y_ready, 1)
                v.wait_ge(proj_ready, LEAD + b)
                v.tensor_tensor(yz[:], row(bank, b), row(SZ, b), ALU.mult).then_inc(yz_ready, 1)
                v.wait_ge(proj_ready, LEAD + b + 1)
                v.tensor_tensor(xa[:], core.tiles(4), X1[:, bass.ds(b * TT, TT), :], ALU.add).then_inc(xa_ready, 1)
                v.wait_ge(xa_ready, LEAD + b + 1)
                norm_vector(v, core, ln_2, b, lambda t: xa[:, t, :], lambda t: un[:, t, :],
                            before=(xa_turned, LEAD + TT * b))
                v.wait_ge(ffn_ready, LEAD + b + 1)
                v.tensor_tensor(xa[:], core.tiles(5), xa[:], ALU.add).then_inc(xf_ready, 1)
                v.wait_ge(xf_ready, LEAD + b + 1)
                v.tensor_tensor(X[:, bass.ds(b * TT, TT), :], X[:, bass.ds(b * TT, TT), :], xa[:],
                                ALU.add).then_inc(x_done, 1)
            v.wait_ge(x_done, LEAD + NB)

        @block.tensor
        def _(pe):
            pe.wait_ge(w_in, 16 * W_LOADS)
            pe.wait_ge(core.consts_in, 16)
            with pe.Fori(0, NB) as b:
                pe.wait_ge(uT_ready, LEAD + b)
                for t in range(TT):
                    pe.wait_ge(ln_1.normed, b * TT + t + 1)
                    pe.transpose(core.tiles(0)[:, t, :], un[:, t, :], core.ident[:]).then_inc(un_turned, 1)
                pe.wait_ge(uT_ready, LEAD + b + 1)
                pe.wait_ge(xpad_ready, LEAD + b)
                pe.matmul(bank[:, 1, :], win[:, 0:D], uT[:], start=True, stop=True).then_inc(xin_ready, 1)
                pe.wait_ge(sz_ready, LEAD + b)
                pe.matmul(bank[:, 2, :], win[:, D:2 * D], uT[:], start=True, stop=True).then_inc(z_ready, 1)
                pe.wait_ge(xpad_ready, LEAD + b + 1)
                pe.wait_ge(xc_ready, LEAD + b)
                pe.wait_ge(taps_ready, NCONV + 1)
                for j in range(NCONV):
                    mm = pe.matmul(bank[:, 3, :], taps[:, j, :], xpad[:, j:j + T],
                                   start=(j == 0), stop=(j == NCONV - 1))
                mm.then_inc(conv_ready, 1)
            with pe.Fori(0, NB) as b:
                pe.wait_ge(xc_ready, LEAD + b + 1)
                pe.wait_ge(dt_copied, LEAD + b)
                pe.matmul(bank[0:RANK, 4, :], wx[:, 0:RANK], row(XC, b), start=True, stop=True).then_inc(dt_ready, 1)
                pe.wait_ge(bc_split, LEAD + b)
                pe.matmul(bank[0:96, 5, :], wx[:, RANK:], row(XC, b), start=True, stop=True).then_inc(bc_ready, 1)
                pe.wait_ge(dt_copied, LEAD + b + 1)
                pe.wait_ge(abs_ready, LEAD + b)
                pe.wait_ge(relu_ready, LEAD + b)
                pe.matmul(bank[:, 6, :], wdt[:], dt_sb[:], start=True, stop=True).then_inc(dpre_ready, 1)
            pe.wait_ge(pick_ready, 1)
            pe.wait_ge(bc_split, LEAD + NB)
            pe.wait_ge(relu_ready, LEAD + NB)
            pe.wait_ge(abs_ready, LEAD + NB)

            for b in range(NB):
                pe.matmul(bank[:, b, :], dskip[:], XC[:, b, :], start=True, stop=False, skip_group_check=True)

            def state(n, first=False, last=False):
                for b in range(NB):
                    k = n * NB + b
                    pe.wait_ge(h_ready, LEAD + k - 1)
                    pe.matmul(bank[:, 4 + b % 2, :], pick[:, bass.ds(n, 1), :].rearrange("p a n -> p (a n)"),
                              BC[:, b, :], start=True, stop=True).then_inc(b_ready, 1)
                    pe.wait_ge(c_copied, LEAD + k - 1)
                    pe.matmul(bank[:, 6 + b % 2, :], pick[:, bass.ds(n + NS, 1), :].rearrange("p a n -> p (a n)"),
                              BC[:, b, :], start=True, stop=True).then_inc(c_ready, 1)
                    if first and b < 2:
                        continue
                    pe.wait_ge(hc_ready, LEAD + k - 1)
                    pe.matmul(bank[:, (b + 2) % NB, :], core.ident[:], hc[:, b % 2, :],
                              start=False, stop=(last and b >= 2), skip_group_check=True).then_inc(hc_summed, 1)

            state(0, first=True)
            with pe.Fori(1, NS - 1) as n:
                state(n)
            state(NS - 1, last=True)
            for b in range(2, NB):
                pe.wait_ge(hc_ready, LEAD + NS * NB - NB + b + 1)
                mm = pe.matmul(bank[:, b, :], core.ident[:], hc[:, b % 2, :],
                               start=False, stop=True, skip_group_check=True)
            mm.then_inc(y_ready, 1)
            with pe.Fori(0, NB) as b:
                pe.wait_ge(yz_ready, LEAD + b + 1)
                pe.wait_ge(xa_ready, LEAD + b)
                for t in range(TT):
                    mm = pe.matmul(core.tiles(4)[:, t, :], yz[:, t * P:t * P + P], wout[:], start=True, stop=True)
                mm.then_inc(proj_ready, 1)
                pe.wait_ge(xf_ready, LEAD + b)
                for t in range(TT):
                    pe.wait_ge(ln_2.normed, b * TT + t + 1)
                    pe.transpose(core.tiles(5)[:, t, :], un[:, t, :], core.ident[:]).then_inc(xa_turned, 1)
                pe.wait_ge(xaT_ready, LEAD + b + 1)
                for f in range(FB):
                    pe.wait_ge(h1_relu, LEAD + FB * b + f - 1)
                    pe.matmul(bank[:, 6 + f % 2, :], w1[:, f * P:f * P + P], uT[:],
                              start=True, stop=True).then_inc(h1_ready, 1)
                pe.wait_ge(h1_relu, LEAD + FB * b + FB)
                for t in range(TT):
                    for f in range(FB):
                        pe.matmul(core.tiles(5)[:, t, :], hT[:, f, t * P:t * P + P], w2[:, f, :],
                                  start=(f == 0), stop=False)
                    mm = pe.matmul(core.tiles(5)[:, t, :], core.ones_row[:], b2row[:], start=False, stop=True)
                mm.then_inc(ffn_ready, 1)


def moe(core, layer):
    io, bank, X = core.io, core.bank, core.X
    st = Stage(core, f"e{layer}")
    scattered, gathered = core.scattered, core.gathered
    gate_w = st.sb("gate_w", [P, NE])
    gate_b = st.sb("gate_b", [P, NE])
    b1all = st.sb("b1all", [P, NE, FB])
    b2all = st.sb("b2all", [P, NE, D])
    iota_e = st.sb("iota_e", [P, NE, NT])
    thresh = st.sb("thresh", [P, NE, NT])
    reset = st.sb("reset", [P, NE * NT])
    iota_j = st.sb("iota_j", [1, SLOT_TILES, NE])
    below = st.sb("below", [P, P], BF16)
    onesb = st.sb("onesb", [P, P], BF16)
    xn = st.sb("xn", [P, TT, D])
    XF = st.sb("XF", [P, NT, D])
    xT = st.sb("xT", [P, T])
    score = st.sb("score", [P, TT, NE])
    best = st.sb("best", [P, TT, 8])
    best_at = st.sb("best_at", [P, TT, 8], U32)
    value = st.sb("value", [P, NT, TOPK])
    expert = st.sb("expert", [P, NT, TOPK])
    chosen = [st.sb(f"chosen{k}", [P, NE, NT]) for k in range(TOPK)]
    member = st.sb("member", [P, NE * NT])
    memberb = st.sb("memberb", [P, NE * NT], BF16)
    upto = st.sb("upto", [P, NE * NT])
    before = st.sb("before", [P, NE * NT], BF16)
    total = st.sb("total", [P, NE], BF16)
    filled = st.sb("filled", [P, NE, NT])
    ntile = st.sb("ntile", [P, NE])
    tile_end = st.sb("tile_end", [P, NE])
    tile_start = st.sb("tile_start", [P, NE])
    place = st.sb("place", [P, NE, NT])
    placed = st.sb("placed", [P, NE, NT])
    slotf = st.sb("slotf", [P, TOPK, NT])
    slot = st.sb("slot", [P, TOPK, NT], I32)
    past = st.sb("past", [1, SLOT_TILES, NE])
    ownerf = st.sb("ownerf", [1, SLOT_TILES])
    owner = st.sb("owner", [1, SLOT_TILES], I32)
    gdiff = st.sb("gdiff", [P, NT])
    gexp = st.sb("gexp", [P, NT])
    gsum = st.sb("gsum", [P, NT])
    gate = st.sb("gate", [P, TOPK, NT])
    xs = st.sb("xs", [P, 4, D])
    xsT = st.sb("xsT", [P, 2, P])
    w1b = st.sb("w1b", [P, 2, FF])
    w2b = st.sb("w2b", [P, 4, FB * D])
    b1b = st.sb("b1b", [P, 4, FB])
    b2b = st.sb("b2b", [P, 4, D])
    hid = st.sb("hid", [P, 2, FB * P])
    ysb = st.sb("ysb", [P, 4, D])
    back = [st.sb(f"back{k}", [P, NT, D]) for k in range(TOPK)]

    gate_in, bias_in, tables_in = map(st.sem, ("gate_in", "bias_in", "tables_in"))
    ln = Norm(st, "ln")
    turned, xT_ready, score_ready, score_biased = map(st.lead, ("turned", "xT_ready", "score_ready", "score_biased"))
    best_ready, best_at_ready, best_kept, xf_kept = map(st.lead, ("best_ready", "best_at_ready", "best_kept", "xf_kept"))
    route_step, rank_ready, slot_ready, owner_ready = map(st.sem, ("route_step", "rank_ready", "slot_ready", "owner_ready"))
    members_ready = st.sem("members_ready")
    gdiff_ready, gexp_ready = st.sem("gdiff_ready"), st.sem("gexp_ready")
    slot_in = [st.sem(f"slot_in{q}") for q in range(4)]
    slot_turned, xsT_ready, w1_ready, b1_ready = map(st.lead, ("slot_turned", "xsT_ready", "w1_ready", "b1_ready"))
    w2_ready, b2_ready, mm1_done, gelu_done = map(st.lead, ("w2_ready", "b2_ready", "mm1_done", "gelu_done"))
    mm2_done, y_ready = map(st.lead, ("mm2_done", "y_ready"))
    y_out = [st.lead(f"y_out{q}") for q in range(4)]
    ones_e, ones_set = st.sb("ones_e", [P, NE]), st.sem("ones_set")
    skip_added, first_added, second_added = map(st.sem, ("skip_added", "first_added", "second_added"))

    STEPS = SLOT_TILES + 3

    def steps(eng, step):
        for j in range(4):
            step(j, j)
        with eng.Fori(1, SLOT_TILES // 4) as i:
            for q in range(4):
                step(i * 4 + q, q, loop=True)
        for j in range(SLOT_TILES, STEPS):
            step(j, j % 4)

    def has(j, lag, loop):
        return loop or 0 <= j - lag < SLOT_TILES

    with st.ctx, core.nc.Block() as block:
        @block.sync
        def _(sp):
            sp.dma_start(gate_w[:], io["gate_w"]).then_inc(gate_in, 16)
            sp.dma_start(gate_b[:], io["gate_b"].partition_broadcast(P)).then_inc(gate_in, 16)
            for dst, name in ((iota_e, "iota_e"), (thresh, "thresh"), (iota_j, "iota_j")):
                n = dst.shape[0]
                sp.dma_start(dst[:].rearrange("p a b -> p (a b)"), io[name].partition_broadcast(n)).then_inc(tables_in, 16)
            sp.dma_start(reset[:], io["reset"].partition_broadcast(P)).then_inc(tables_in, 16)
            sp.dma_start(below[:], io["below"]).then_inc(tables_in, 16)
            sp.dma_start(onesb[:], io["onesb"]).then_inc(tables_in, 16)
            sp.dma_start(b1all[:].rearrange("p e k -> p (e k)"), io["e_b1_t"]).then_inc(bias_in, 16)
            sp.dma_start(b2all[:].rearrange("p e n -> p (e n)"), io["e_b2"].partition_broadcast(P)).then_inc(bias_in, 16)
            sp.wait_ge(scattered, 16 * NT * TOPK * layer)

            def load(j, q):
                sp.dma_start(xs[:, q, :], core.slots_in[bass.ds(j * P, P), :]).then_inc(slot_in[q], 16)

            for j in range(4):
                load(j, j)

            def step(j, q, loop=False):
                if loop or (4 <= j < SLOT_TILES):
                    sp.wait_ge(slot_turned, LEAD + j - 3)
                    load(j, q)
                if has(j, 3, loop):
                    sp.wait_ge(y_ready, LEAD + j - 2)
                    sp.dma_start(core.slots_out[bass.ds((j - 3) * P, P), :], ysb[:, (q + 1) % 4, :])\
                        .then_inc(y_out[(q + 1) % 4], 16)
            steps(sp, step)
            for q in range(4):
                sp.wait_ge(y_out[q], LEAD + 16 * SLOT_TILES // 4)

        @block.gpsimd
        def _(g):
            st.set_leads(g)
            with g.Fori(0, NB) as b:
                norm_pool(g, core, ln, b)
                g.wait_ge(ln.normed, TT * b + TT)
                apart(g, core)
                g.tensor_copy(XF[:, bass.ds(b * TT, TT), :], xn[:]).then_inc(xf_kept, 1)
            g.wait_ge(xf_kept, LEAD + NB)
            g.wait_ge(core.slots_zeroed, 16)
            g.wait_ge(slot_ready, 1)
            for i in range(NT):
                for k in range(TOPK):
                    g.indirect_dma_start(core.slots_in, bass.IndirectOffsetOnAxis(slot[:, k, i:i + 1].bitcast(U32), 0),
                                         XF[:, i, :], None).then_inc(scattered, 16)
            for q in range(4):
                g.wait_ge(y_out[q], LEAD + 16 * SLOT_TILES // 4)
            for i in range(NT):
                for k in range(TOPK):
                    g.indirect_dma_start(back[k][:, i, :], None, core.slots_out,
                                         bass.IndirectOffsetOnAxis(slot[:, k, i:i + 1].bitcast(U32), 0))\
                        .then_inc(gathered[i], 16)

        @block.scalar
        def _(act):
            with act.Fori(0, NB) as b:
                act.wait_ge(turned, LEAD + TT * b + TT)
                act.activation(xT[:], bank[:, 0, :], ACT.Identity).then_inc(xT_ready, 1)
            act.wait_ge(gdiff_ready, 1)
            act.activation(gexp[:], gdiff[:], ACT.Exp).then_inc(gexp_ready, 1)
            act.preload_act_table(ACT.Gelu)

            def step(j, q, loop=False):
                if has(j, 1, loop):
                    m, mq = j - 1, (q + 3) % 4
                    act.wait_ge(b1_ready, LEAD + m + 1)
                    act.wait_ge(mm2_done, LEAD + m - 1)
                    act.wait_ge(mm1_done, LEAD + m + 1)
                    for f in range(FB):
                        ins = act.activation(hid[:, mq % 2, f * P:f * P + P], core.tiles(2 + mq % 2)[:, f, :],
                                             ACT.Gelu, bias=b1b[:, mq, f:f + 1])
                    ins.then_inc(gelu_done, 1)
            steps(act, step)

        @block.vector
        def _(v):
            v.memset(ones_e[:], 1.0).then_inc(ones_set, 1)
            v.wait_ge(ones_set, 1)
            v.wait_ge(gate_in, 32)
            with v.Fori(0, NB) as b:
                norm_vector(v, core, ln, b, lambda t: row(X, b * TT + t), lambda t: xn[:, t, :],
                            before=(turned, LEAD + TT * b), also=(xf_kept, LEAD + b))
                v.wait_ge(score_ready, LEAD + b + 1)
                v.tensor_tensor(score[:], bank[:, 1, 0:TT * NE].rearrange("p (t e) -> p t e", e=NE),
                                gate_b[:].unsqueeze(1).to_broadcast([P, TT, NE]), ALU.add).then_inc(score_biased, 1)
                v.wait_ge(score_biased, LEAD + b + 1)
                apart(v, core)
                for t in range(TT):
                    ins = v.max(best[:, t, :], score[:, t, :])
                ins.then_inc(best_ready, 1)
                v.wait_ge(best_ready, LEAD + b + 1)
                apart(v, core)
                for t in range(TT):
                    ins = v.max_index(best_at[:, t, :], best[:, t, :], score[:, t, :])
                ins.then_inc(best_at_ready, 1)
                v.wait_ge(best_at_ready, LEAD + b + 1)
                apart(v, core)
                v.tensor_copy(value[:, bass.ds(b * TT, TT), :], best[:, :, 0:TOPK])
                v.tensor_copy(expert[:, bass.ds(b * TT, TT), :], best_at[:, :, 0:TOPK]).then_inc(best_kept, 1)
            v.wait_ge(best_kept, LEAD + NB)
            v.wait_ge(tables_in, 16 * 6)
            done = [0]

            def then(ins):
                done[0] += 1
                ins.then_inc(route_step, 1)
                v.wait_ge(route_step, done[0])

            v.tensor_tensor(gdiff[:], value[:, :, 1], value[:, :, 0], ALU.subtract).then_inc(gdiff_ready, 1)
            for k in range(TOPK):
                ins = v.tensor_tensor(chosen[k][:], iota_e[:],
                                      expert[:, :, k].unsqueeze(1).to_broadcast([P, NE, NT]), ALU.is_equal)
            then(ins)
            flat = lambda x: x[:].rearrange("p e t -> p (e t)")
            then(v.tensor_tensor(member[:], flat(chosen[0]), flat(chosen[1]), ALU.add))
            v.tensor_copy(memberb[:], member[:])
            then(v.tensor_tensor_scan(upto[:], reset[:], member[:], 0.0, ALU.mult, ALU.add))
            v.tensor_copy(total[:], upto[:].rearrange("p (e t) -> p e t", t=NT)[:, :, NT - 1])
            v.tensor_tensor(before[:], upto[:], member[:], ALU.subtract).then_inc(members_ready, 1)
            v.wait_ge(rank_ready, 1)
            then(v.tensor_tensor(filled[:], bank[:, 3, 0:NE].unsqueeze(2).to_broadcast([P, NE, NT]), thresh[:],
                                 ALU.is_gt))
            then(v.tensor_reduce(ntile[:], filled[:], AX_X, ALU.add))
            then(v.tensor_tensor_scan(tile_end[:], ones_e[:], ntile[:], 0.0, ALU.mult, ALU.add))
            then(v.tensor_tensor(tile_start[:], tile_end[:], ntile[:], ALU.subtract))
            then(v.scalar_tensor_tensor(out=place[:], in0=tile_start[:].unsqueeze(2).to_broadcast([P, NE, NT]),
                                        scalar=float(P), in1=bank[:, 2, 0:NE * NT].rearrange("p (e t) -> p e t", t=NT),
                                        op0=ALU.mult, op1=ALU.add))
            for k in range(TOPK):
                then(v.tensor_tensor(placed[:], place[:], chosen[k][:], ALU.mult))
                then(v.tensor_reduce(slotf[:, k, :], placed[:].rearrange("p e t -> p t e"), AX_X, ALU.add))
            v.tensor_copy(slot[:], slotf[:]).then_inc(slot_ready, 1)
            then(v.tensor_tensor(past[:], tile_end[0:1, :].unsqueeze(1).to_broadcast([1, SLOT_TILES, NE]), iota_j[:],
                                 ALU.is_le))
            then(v.tensor_reduce(ownerf[:], past[:], AX_X, ALU.add))
            then(v.tensor_scalar(owner[:], ownerf[:], float(NE - 1), None, ALU.min))
            v.wait_ge(gexp_ready, 1)
            then(v.tensor_scalar(gsum[:], gexp[:], 1.0, None, ALU.add))
            then(v.reciprocal(gate[:, 0, :], gsum[:]))
            then(v.tensor_tensor(gate[:, 1, :], gexp[:], gate[:, 0, :], ALU.mult))
            v.wait_ge(xf_kept, LEAD + NB)
            v.tensor_tensor(X[:], X[:], XF[:], ALU.add).then_inc(skip_added, 1)
            v.wait_ge(bias_in, 32)
            v.wait_ge(core.experts_in, 16 * 2 * (NE // LOAD_EXPERTS))

            def step(j, q, loop=False):
                if has(j, 0, loop):
                    e = v.value_load(owner[0:1, bass.ds(j, 1)], min_val=0, max_val=NE - 1)
                    v.wait_ge(mm1_done, LEAD + j - 1)
                    apart(v, core)
                    v.tensor_copy(w1b[:, q % 2, :], row(core.w1all, e)).then_inc(w1_ready, 1)
                    v.wait_ge(gelu_done, LEAD + j - 1)
                    apart(v, core)
                    v.tensor_copy(b1b[:, q, :], row(b1all, e)).then_inc(b1_ready, 1)
                    if loop:
                        v.wait_ge(mm2_done, LEAD + j - 3)
                        v.wait_ge(y_ready, LEAD + j - 3)
                        apart(v, core)
                    v.tensor_copy(w2b[:, q, :], core.w2all[:, bass.ds(e, 1), :, :].rearrange("p a k n -> p (a k n)"))\
                        .then_inc(w2_ready, 1)
                    v.tensor_copy(b2b[:, q, :], row(b2all, e)).then_inc(b2_ready, 1)
                    v.wait_ge(slot_turned, LEAD + j + 1)
                    v.tensor_copy(xsT[:, q % 2, :], core.tiles(q % 2)[:, 0, :]).then_inc(xsT_ready, 1)
                if has(j, 3, loop):
                    m, mq = j - 3, (q + 1) % 4
                    v.wait_ge(b2_ready, LEAD + m + 1)
                    if loop or m >= 4:
                        v.wait_ge(y_out[mq], LEAD + ((m - mq) * 4 if loop else (m // 4) * 16))
                    v.wait_ge(mm2_done, LEAD + m + 1)
                    v.tensor_tensor(ysb[:, mq, :], core.tiles(4 + mq % 2)[:, 0, :], b2b[:, mq, :],
                                    ALU.add).then_inc(y_ready, 1)
            steps(v, step)
            v.wait_ge(skip_added, 1)

            def second(i):
                v.wait_ge(first_added, i + 1)
                v.scalar_tensor_tensor(out=X[:, i, :], in0=back[1][:, i, :], scalar=gate[:, 1, i:i + 1],
                                       in1=X[:, i, :], op0=ALU.mult, op1=ALU.add).then_inc(second_added, 1)

            for i in range(NT):
                v.wait_ge(gathered[i], 16 * TOPK * layer)
                v.scalar_tensor_tensor(out=X[:, i, :], in0=back[0][:, i, :], scalar=gate[:, 0, i:i + 1],
                                       in1=X[:, i, :], op0=ALU.mult, op1=ALU.add).then_inc(first_added, 1)
                if i >= 1:
                    second(i - 1)
            second(NT - 1)
            v.wait_ge(second_added, NT)

        @block.tensor
        def _(pe):
            pe.wait_ge(gate_in, 32)
            with pe.Fori(0, NB) as b:
                pe.wait_ge(xT_ready, LEAD + b)
                for t in range(TT):
                    pe.wait_ge(ln.normed, b * TT + t + 1)
                    pe.transpose(core.tiles(0)[:, t, :], xn[:, t, :], core.ident[:]).then_inc(turned, 1)
                pe.wait_ge(xT_ready, LEAD + b + 1)
                pe.wait_ge(score_biased, LEAD + b)
                for t in range(TT):
                    mm = pe.matmul(bank[:, 1, t * NE:t * NE + NE], xT[:, t * P:t * P + P], gate_w[:],
                                   start=True, stop=True)
                mm.then_inc(score_ready, 1)
            pe.wait_ge(tables_in, 16 * 6)
            pe.wait_ge(members_ready, 1)
            pe.matmul(bank[:, 2, 0:NE * NT], below[:], memberb[:], start=True, stop=False)
            pe.matmul(bank[:, 2, 0:NE * NT], onesb[:], before[:], start=False, stop=True)
            pe.matmul(bank[:, 3, 0:NE], onesb[:], total[:], start=True, stop=True).then_inc(rank_ready, 1)
            pe.wait_ge(slot_ready, 1)

            def step(j, q, loop=False):
                if has(j, 0, loop):
                    pe.wait_ge(slot_in[q], ((j - q) * 4 if loop else (j // 4) * 16) + 16)
                    pe.wait_ge(xsT_ready, LEAD + j - 1)
                    pe.transpose(core.tiles(q % 2)[:, 0, :], xs[:, q, :], core.ident[:]).then_inc(slot_turned, 1)
                if has(j, 1, loop):
                    m, mq = j - 1, (q + 3) % 4
                    pe.wait_ge(w1_ready, LEAD + m + 1)
                    pe.wait_ge(xsT_ready, LEAD + m + 1)
                    pe.wait_ge(gelu_done, LEAD + m - 1)
                    for f in range(FB):
                        mm = pe.matmul(core.tiles(2 + mq % 2)[:, f, :], w1b[:, mq % 2, f * P:f * P + P],
                                       xsT[:, mq % 2, :], start=True, stop=True)
                    mm.then_inc(mm1_done, 1)
                if has(j, 2, loop):
                    m, mq = j - 2, (q + 2) % 4
                    pe.wait_ge(w2_ready, LEAD + m + 1)
                    pe.wait_ge(y_ready, LEAD + m - 1)
                    pe.wait_ge(gelu_done, LEAD + m + 1)
                    for f in range(FB):
                        mm = pe.matmul(core.tiles(4 + mq % 2)[:, 0, :], hid[:, mq % 2, f * P:f * P + P],
                                       w2b[:, mq, f * D:f * D + D], start=(f == 0), stop=(f == FB - 1))
                    mm.then_inc(mm2_done, 1)
            steps(pe, step)


def attention(core):
    nc, io, bank, X = core.nc, core.io, core.bank, core.X
    st = Stage(core, "t")
    UNITS = NB * NH // 4
    ROWS = 6 * HD
    K = ROWS + 2
    Q_PARTS = (0, 0, 1, 0, 2, 1)
    K_PARTS = (0, 1, 0, 2, 0, 1)
    SCALE = 1.0 / float(np.sqrt(HD))
    stacks = nc.dram_tensor("stacks", (2, NB, NH, ROWS, T), BF16).ap()

    vec = st.sb("vec", [P, 6])
    LN1G, LN1B, LN2G, LN2B, BQ, BK = range(6)
    wqkv = st.sb("wqkv", [P, 3 * D])
    bv = st.sb("bv", [P, D])
    rot = st.sb("rot", [P, P])
    cos, sin = st.sb("cos", [P, T]), st.sb("sin", [P, T])
    wo = st.sb("wo", [P, D])
    bo = st.sb("bo", [1, D])
    w1, b1 = st.sb("w1", [P, FF]), st.sb("b1", [P, FB])
    w2, b2row = st.sb("w2", [P, FB, D]), st.sb("b2row", [1, D])
    identb = st.sb("identb", [P, P], BF16)
    hide_k = st.sb("hide_k", [P, P], BF16)
    hide_q = st.sb("hide_q", [P, P], BF16)

    XB = st.sb("XB", [P, NT, D])
    V = st.sb("V", [P, NT, D])
    A = st.sb("A", [P, NT, D])
    un = st.sb("un", [P, TT, D])
    uT = st.sb("uT", [P, T])
    qk = st.sb("qk", [P, 2, T])
    side = st.sb("side", [P, 2, T])
    turnedqk = st.sb("turnedqk", [P, 2, T])
    part = [[st.sb(f"part{x}{i}", [P, T], BF16) for i in range(3)] for x in range(2)]
    QS = [st.sb(f"QS{p}", [P, 2, T], BF16) for p in range(2)]
    KS = [st.sb(f"KS{p}", [P, 2, T], BF16) for p in range(2)]
    va = [st.sb(f"va{p}", [P, TT, 4, 32]) for p in range(2)]
    peak = [st.sb(f"peak{p}", [P, TT, 4]) for p in range(2)]
    low_hi, low_mid = st.sb("low_hi", [4, T], BF16), st.sb("low_mid", [4, T], BF16)
    pa = st.sb("pa", [P, 2, 2 * T])
    pb = st.sb("pb", [P, 2, T])
    oT = st.sb("oT", [P, T])
    rsum = st.sb("rsum", [P, TT, 4])
    at = st.sb("at", [P, TT, D])
    aT = st.sb("aT", [P, T])
    xa = st.sb("xa", [P, TT, D])
    hT = st.sb("hT", [P, FB, T])

    w_in, tables_in = st.sem("w_in"), st.sem("tables_in")
    ones_set, va_set = st.sem("ones_set"), st.sem("va_set")
    ln_x, ln_1, ln_2 = Norm(st, "ln_x"), Norm(st, "ln_1"), Norm(st, "ln_2")
    un_turned, uT_ready, q_ready, k_ready = map(st.lead, ("un_turned", "uT_ready", "q_ready", "k_ready"))
    qk_ready, rot_ready, v_ready, v_kept = map(st.lead, ("qk_ready", "rot_ready", "v_ready", "v_kept"))
    cos_ready, sin_ready, rope_ready = map(st.lead, ("cos_ready", "sin_ready", "rope_ready"))
    split_step = st.sem("split_step")
    part_ready = [st.sem(f"part_ready{x}") for x in range(2)]
    part_out = [st.lead(f"part_out{x}") for x in range(2)]
    unit_in = [st.sem(f"unit_in{p}") for p in range(2)]
    va_ready = st.lead("va_ready")
    peak_scored, peak_read = st.lead("peak_scored"), st.lead("peak_read")
    peak_turned, low_hi_ready, low_ready = map(st.lead, ("peak_turned", "low_hi_ready", "low_ready"))
    low_in = [st.sem(f"low_in{p}") for p in range(2)]
    sa_ready, pa_ready, sb_ready, pb_ready = map(st.lead, ("sa_ready", "pa_ready", "sb_ready", "pb_ready"))
    pa_used, pb_used = map(st.lead, ("pa_used", "pb_used"))
    oT_ready, oT_turned, rsum_ready, a_ready = map(st.lead, ("oT_ready", "oT_turned", "rsum_ready", "a_ready"))
    at_ready, at_turned, aT_ready, proj_ready, xa_ready = map(st.lead, ("at_ready", "at_turned", "aT_ready", "proj_ready", "xa_ready"))
    xa_turned, xaT_ready, h1_ready, h1_gelu = map(st.lead, ("xa_turned", "xaT_ready", "h1_ready", "h1_gelu"))
    ffn_ready, xf_ready, x_done = map(st.lead, ("ffn_ready", "xf_ready", "x_done"))

    PEAKS = [(3, (j,)) for j in range(4)] + [(2, (j,)) for j in range(4)] + [(1, (0, 1)), (1, (2, 3)), (0, (0, 1)), (0, (2, 3))]
    NP = len(PEAKS)

    def sweep(eng, prepare, step):
        prepare(0, 0, 0)
        step(0, 0, 0, True, first=True)
        step(1, 0, 1, True)
        with eng.Fori(1, (UNITS - 2) // 2) as i:
            for p in range(2):
                step(i * 2 + p, i, p, True)
        step(UNITS - 2, UNITS // 2 - 1, 0, True)
        step(UNITS - 1, UNITS // 2 - 1, 1, False)

    with st.ctx, nc.Block() as block:
        @block.sync
        def _(sp):
            for dst, name in ((vec, "vec_b"), (wqkv, "wqkv"), (rot, "rot"), (cos, "cos"), (sin, "sin"), (wo, "wo"),
                              (bo, "bo"), (w1, "b_w1"), (b1, "b_b1_t"), (b2row, "b_b2"), (identb, "identb"),
                              (hide_k, "hide_k"), (hide_q, "hide_q")):
                sp.dma_start(dst[:], io[name]).then_inc(w_in, 16)
            sp.dma_start(bv[:], io["bv"].partition_broadcast(P)).then_inc(w_in, 16)
            sp.dma_start(w2[:], io["b_w2"].rearrange("(f p) n -> p f n", p=P)).then_inc(w_in, 16)
            with sp.Fori(0, NB) as b:
                for x, parts in ((0, Q_PARTS), (1, K_PARTS)):
                    sp.wait_ge(part_ready[x], b + 1)
                    for r, i in enumerate(parts):
                        sp.dma_start(stacks[x, bass.ds(b, 1), :, r * HD:r * HD + HD, :].rearrange("a h d n -> (a h) d n"),
                                     part[x][i][:]).then_inc(part_out[x], 16)
            for x in range(2):
                sp.wait_ge(part_out[x], LEAD + 16 * 6 * NB)
            flat = stacks.rearrange("x b h r n -> x (b h) r n")

            def load(u, p):
                for x, S in ((0, QS), (1, KS)):
                    src = flat[x, bass.ds(u * 4, 4)].rearrange("(a s) r n -> a r s n", a=2)
                    for a in range(2):
                        sp.dma_start(S[p][64 * a:64 * a + ROWS, :, :], src[a]).then_inc(unit_in[p], 16)

            def low(u, p):
                sp.wait_ge(low_ready, LEAD + u + 1)
                for r, src in ((ROWS, low_hi), (ROWS + 1, low_mid)):
                    for a in range(2):
                        sp.dma_start(QS[p][64 * a + r:64 * a + r + 1, :, :],
                                     src[2 * a:2 * a + 2, :]).then_inc(low_in[p], 16)

            sp.wait_ge(ones_set, 4)
            load(0, 0)
            load(1, 1)
            low(0, 0)
            with sp.Fori(0, (UNITS - 2) // 2) as i:
                for p in range(2):
                    u = i * 2 + p
                    low(u + 1, 1 - p)
                    sp.wait_ge(sb_ready, LEAD + 2 * u + 2)
                    load(u + 2, p)
            low(UNITS - 1, 1)

        @block.gpsimd
        def _(g):
            st.set_leads(g)
            for p in range(2):
                g.memset(KS[p][:], 1.0).then_inc(ones_set, 1)
                g.memset(QS[p][:], 0.0).then_inc(ones_set, 1)
                g.memset(va[p][:], 0.0).then_inc(va_set, 1)
            g.wait_ge(va_set, 2)
            for p in range(2):
                g.memset(va[p][:, :, :, HD:HD + 1], 1.0).then_inc(va_set, 1)
            with g.Fori(0, NB) as b:
                norm_pool(g, core, ln_x, b)
                norm_pool(g, core, ln_1, b)
                g.wait_ge(qk_ready, LEAD + 2 * b + 2)
                for x in range(2):
                    g.wait_ge(rope_ready, LEAD + 2 * b + x)
                    g.tensor_tensor(side[:, x, :], qk[:, x, :], cos[:], ALU.mult).then_inc(cos_ready, 1)
            g.wait_ge(va_set, 4)
            g.wait_ge(v_kept, LEAD + NB)

            def values(u, p):
                tile0, col0 = u // 4 * TT, u % 4 * 32
                g.wait_ge(pb_used, LEAD + 2 * u - 2)
                apart(g, core)
                g.tensor_copy(va[p][:, :, :, 0:HD],
                              V[:, bass.ds(tile0, TT), bass.ds(col0, 32)].rearrange("p t (h d) -> p t h d", d=HD))\
                    .then_inc(va_ready, 1)

            with g.Fori(0, UNITS // 2) as i:
                for p in range(2):
                    values(i * 2 + p, p)
            with g.Fori(0, NB) as b:
                g.wait_ge(at_turned, LEAD + TT * b)
                g.wait_ge(a_ready, LEAD + UNITS)
                apart(g, core)
                g.tensor_copy(at[:], A[:, bass.ds(b * TT, TT), :]).then_inc(at_ready, 1)
                norm_pool(g, core, ln_2, b)

        @block.scalar
        def _(act):
            act.wait_ge(w_in, 16 * 15)
            with act.Fori(0, NB) as b:
                act.wait_ge(un_turned, LEAD + TT * b + TT)
                act.activation(uT[:], bank[:, 0, :], ACT.Identity, bias=vec[:, LN1B:LN1B + 1],
                               scale=vec[:, LN1G:LN1G + 1]).then_inc(uT_ready, 1)
                act.wait_ge(q_ready, LEAD + b + 1)
                act.wait_ge(cos_ready, LEAD + 2 * b)
                act.wait_ge(rot_ready, LEAD + 2 * b)
                act.activation(qk[:, 0, :], bank[:, 1, :], ACT.Identity, bias=vec[:, BQ:BQ + 1]).then_inc(qk_ready, 1)
                act.wait_ge(k_ready, LEAD + b + 1)
                act.activation(qk[:, 1, :], bank[:, 2, :], ACT.Identity, bias=vec[:, BK:BK + 1]).then_inc(qk_ready, 1)
            act.preload_act_table(ACT.Exp)

            def low(u, i, p):
                act.wait_ge(peak_turned, LEAD + u + 1)
                act.activation(low_hi[:], bank[0:4, 1, :], ACT.Identity, scale=-1.0).then_inc(low_hi_ready, 1)

            def step(u, i, p, more, first=False):
                for j in range(4):
                    act.wait_ge(sa_ready, LEAD + 4 * u + j + 1)
                    act.wait_ge(pa_used, LEAD + 4 * u + j - 1)
                    act.activation(pa[:, j % 2, :], bank[:, 2 + 2 * (j % 2):4 + 2 * (j % 2), :].rearrange("p a n -> p (a n)"),
                                   ACT.Exp, scale=SCALE).then_inc(pa_ready, 1)
                    if j % 2:
                        act.wait_ge(sb_ready, LEAD + 2 * u + j // 2 + 1)
                        act.wait_ge(pb_used, LEAD + 2 * u + j // 2 - 1)
                        act.activation(pb[:, j // 2, :], bank[:, 6, :], ACT.Exp, scale=SCALE).then_inc(pb_ready, 1)
                if more:
                    act.wait_ge(low_in[p], 64 * (i + 1))
                    low(u + 1, i, p)
            sweep(act, low, step)
            act.preload_act_table(ACT.Gelu)
            with act.Fori(0, NB) as b:
                act.wait_ge(at_turned, LEAD + TT * b + TT)
                act.activation(aT[:], bank[:, 0, :], ACT.Identity).then_inc(aT_ready, 1)
                act.wait_ge(xa_turned, LEAD + TT * b + TT)
                act.activation(uT[:], bank[:, 2, :], ACT.Identity, bias=vec[:, LN2B:LN2B + 1],
                               scale=vec[:, LN2G:LN2G + 1]).then_inc(xaT_ready, 1)
                act.wait_ge(ffn_ready, LEAD + b)
                for f in range(FB):
                    act.wait_ge(h1_ready, LEAD + FB * b + f + 1)
                    act.activation(hT[:, f, :], bank[:, 3 + f % 2, :], ACT.Gelu,
                                   bias=b1[:, f:f + 1]).then_inc(h1_gelu, 1)

        @block.vector
        def _(v):
            with v.Fori(0, NB) as b:
                norm_vector(v, core, ln_x, b, lambda t: row(X, b * TT + t), lambda t: row(XB, b * TT + t))
                v.wait_ge(ln_x.normed, TT * b + TT)
                norm_vector(v, core, ln_1, b, lambda t: row(XB, b * TT + t), lambda t: un[:, t, :],
                            before=(un_turned, LEAD + TT * b))
                v.wait_ge(w_in, 16 * 15)
                v.wait_ge(v_ready, LEAD + b + 1)
                apart(v, core)
                v.tensor_tensor(V[:, bass.ds(b * TT, TT), :], core.tiles(5),
                                bv[:].unsqueeze(1).to_broadcast([P, TT, D]), ALU.add).then_inc(v_kept, 1)
                for x in range(2):
                    v.wait_ge(rot_ready, LEAD + 2 * b + x + 1)
                    v.tensor_tensor(turnedqk[:, x, :], bank[:, 3 + x, :], sin[:], ALU.mult).then_inc(sin_ready, 1)
                    v.wait_ge(sin_ready, LEAD + 2 * b + x + 1)
                    v.wait_ge(cos_ready, LEAD + 2 * b + x + 1)
                    v.tensor_tensor(turnedqk[:, x, :], turnedqk[:, x, :], side[:, x, :], ALU.add).then_inc(rope_ready, 1)
                    v.wait_ge(rope_ready, LEAD + 2 * b + x + 1)
                    v.wait_ge(part_out[x], LEAD + 16 * 6 * b)
                    S = 6 * b + 3 * x
                    v.tensor_copy(part[x][0][:], turnedqk[:, x, :]).then_inc(split_step, 1)
                    v.wait_ge(split_step, S + 1)
                    v.tensor_tensor(turnedqk[:, x, :], turnedqk[:, x, :], part[x][0][:], ALU.subtract).then_inc(split_step, 1)
                    v.wait_ge(split_step, S + 2)
                    v.tensor_copy(part[x][1][:], turnedqk[:, x, :]).then_inc(split_step, 1)
                    v.wait_ge(split_step, S + 3)
                    v.tensor_tensor(part[x][2][:], turnedqk[:, x, :], part[x][1][:], ALU.subtract).then_inc(part_ready[x], 1)

            def prepare(u, i, p):
                for n, (qt, js) in enumerate(PEAKS):
                    v.wait_ge(peak_scored, LEAD + NP * u + n + 1)
                    w = (qt + 1) * P
                    v.tensor_reduce(peak[p][:, qt, js[0]:js[-1] + 1],
                                    bank[:, n % 2, 0:len(js) * w].rearrange("p (j n) -> p j n", n=w),
                                    AX_X, ALU.max).then_inc(peak_read, 1)
                v.wait_ge(low_hi_ready, LEAD + u + 1)
                v.scalar_tensor_tensor(out=low_mid[:], in0=bank[0:4, 1, :], scalar=-1.0,
                                       in1=low_hi[:], op0=ALU.mult, op1=ALU.subtract).then_inc(low_ready, 1)

            def normalise(u):
                v.wait_ge(oT_turned, LEAD + u + 1)
                o = core.tiles(0).rearrange("p t (h c) -> p t h c", c=32)
                v.reciprocal(rsum[:], o[:, :, :, HD]).then_inc(rsum_ready, 1)
                v.wait_ge(rsum_ready, LEAD + u + 1)
                apart(v, core)
                v.tensor_tensor(A[:, bass.ds(u // 4 * TT, TT), bass.ds(u % 4 * 32, 32)]
                                .rearrange("p t (h d) -> p t h d", d=HD), o[:, :, :, 0:HD],
                                rsum[:].unsqueeze(3).to_broadcast([P, TT, 4, HD]), ALU.mult).then_inc(a_ready, 1)

            def step(u, i, p, more, first=False):
                if not first:
                    normalise(u - 1)
                if more:
                    prepare(u + 1, i, 1 - p)
                v.wait_ge(pb_used, LEAD + 2 * u + 2)
                v.tensor_copy(oT[:], bank[:, 7, :]).then_inc(oT_ready, 1)

            sweep(v, prepare, step)
            normalise(UNITS - 1)
            with v.Fori(0, NB) as b:
                v.wait_ge(proj_ready, LEAD + b + 1)
                v.wait_ge(x_done, LEAD + b)
                apart(v, core)
                v.tensor_tensor(xa[:], core.tiles(1), XB[:, bass.ds(b * TT, TT), :], ALU.add).then_inc(xa_ready, 1)
                v.wait_ge(xa_ready, LEAD + b + 1)
                norm_vector(v, core, ln_2, b, lambda t: xa[:, t, :], lambda t: un[:, t, :],
                            before=(xa_turned, LEAD + TT * b))
                v.wait_ge(ffn_ready, LEAD + b + 1)
                v.tensor_tensor(xa[:], core.tiles(5), xa[:], ALU.add).then_inc(xf_ready, 1)
                v.wait_ge(xf_ready, LEAD + b + 1)
                apart(v, core)
                v.tensor_tensor(X[:, bass.ds(b * TT, TT), :], X[:, bass.ds(b * TT, TT), :], xa[:],
                                ALU.add).then_inc(x_done, 1)
            v.wait_ge(x_done, LEAD + NB)

        @block.tensor
        def _(pe):
            pe.wait_ge(w_in, 16 * 15)
            with pe.Fori(0, NB) as b:
                pe.wait_ge(uT_ready, LEAD + b)
                for t in range(TT):
                    pe.wait_ge(ln_1.normed, b * TT + t + 1)
                    pe.transpose(core.tiles(0)[:, t, :], un[:, t, :], core.ident[:]).then_inc(un_turned, 1)
                pe.wait_ge(uT_ready, LEAD + b + 1)
                pe.wait_ge(qk_ready, LEAD + 2 * b)
                pe.matmul(bank[:, 1, :], wqkv[:, 0:D], uT[:], start=True, stop=True).then_inc(q_ready, 1)
                pe.matmul(bank[:, 2, :], wqkv[:, D:2 * D], uT[:], start=True, stop=True).then_inc(k_ready, 1)
                pe.wait_ge(v_kept, LEAD + b)
                for t in range(TT):
                    mm = pe.matmul(core.tiles(5)[:, t, :], uT[:, t * P:t * P + P], wqkv[:, 2 * D:], start=True, stop=True)
                mm.then_inc(v_ready, 1)
                pe.wait_ge(sin_ready, LEAD + 2 * b)
                for x in range(2):
                    pe.wait_ge(qk_ready, LEAD + 2 * b + x + 1)
                    pe.matmul(bank[:, 3 + x, :], rot[:], qk[:, x, :], start=True, stop=True).then_inc(rot_ready, 1)

            pe.wait_ge(uT_ready, LEAD + NB)
            pe.wait_ge(qk_ready, LEAD + 2 * NB)
            pe.wait_ge(sin_ready, LEAD + 2 * NB)
            pe.wait_ge(v_kept, LEAD + NB)

            def peaks(u, p, turns):
                for n in turns:
                    qt, js = PEAKS[n]
                    if n == 0:
                        pe.wait_ge(a_ready, LEAD + u - 1)
                    elif n == 1:
                        pe.wait_ge(low_ready, LEAD + u)
                    else:
                        pe.wait_ge(peak_read, LEAD + NP * u + n - 1)
                    w = (qt + 1) * P
                    for i, j in enumerate(js):
                        r = slice(64 * (j // 2), 64 * (j // 2) + ROWS)
                        o = bank[:, n % 2, i * w:i * w + w]
                        pe.matmul(o, QS[p][r, j % 2, qt * P:qt * P + P], KS[p][r, j % 2, 0:w],
                                  start=True, stop=False, skip_group_check=True)
                        mm = pe.matmul(o[:, qt * P:], identb[:], hide_k[:], start=False, stop=True, skip_group_check=True)
                    mm.then_inc(peak_scored, 1)

            def turn_peaks(u, p):
                pe.wait_ge(peak_read, LEAD + NP * u + NP)
                for t in range(TT):
                    mm = pe.transpose(bank[0:4, 1, t * P:t * P + P], peak[p][:, t, :], core.ident[:])
                mm.then_inc(peak_turned, 1)

            def prepare(u, i, p):
                pe.wait_ge(unit_in[p], 64 * (i + 1))
                peaks(u, p, range(NP))
                turn_peaks(u, p)

            def scores(u, p, j):
                r = slice(64 * (j // 2), 64 * (j // 2) + K)
                first = 2 + 2 * (j % 2)
                pe.wait_ge(pa_ready, LEAD + 4 * u + j - 1)
                for kt, o in ((0, bank[:, first, :]), (1, bank[:, first + 1, 0:3 * P]), (3, bank[:, first + 1, 3 * P:])):
                    pe.matmul(o, KS[p][r, j % 2, kt * P:kt * P + P], QS[p][r, j % 2, kt * P:],
                              start=True, stop=False, skip_group_check=True)
                    mm = pe.matmul(o[:, 0:P], identb[:], hide_q[:], start=False, stop=True, skip_group_check=True)
                mm.then_inc(sa_ready, 1)
                if j % 2 == 0:
                    pe.wait_ge(pb_ready, LEAD + 2 * u + j // 2)
                o = bank[:, 6, 2 * P * (j % 2):2 * P * (j % 2) + 2 * P]
                pe.matmul(o, KS[p][r, j % 2, 2 * P:3 * P], QS[p][r, j % 2, 2 * P:], start=True, stop=False,
                          skip_group_check=True)
                mm = pe.matmul(o[:, 0:P], identb[:], hide_q[:], start=False, stop=True, skip_group_check=True)
                if j % 2:
                    mm.then_inc(sb_ready, 1)

            def outputs(u, p, j):
                pe.wait_ge(pa_ready, LEAD + 4 * u + j + 1)
                for kt, at_col in ((0, 0), (1, T), (3, T + 3 * P)):
                    mm = pe.matmul(bank[32 * j:32 * j + 32, 7, kt * P:], va[p][:, kt, j, :],
                                   pa[:, j % 2, at_col:at_col + T - kt * P], start=(kt == 0), stop=False,
                                   skip_group_check=True)
                mm.then_inc(pa_used, 1)

            def last_outputs(u, p, s):
                pe.wait_ge(pb_ready, LEAD + 2 * u + s + 1)
                for a in range(2):
                    j = 2 * s + a
                    mm = pe.matmul(bank[32 * j:32 * j + 32, 7, 2 * P:], va[p][:, 2, j, :],
                                   pb[:, s, 2 * P * a:2 * P * a + 2 * P], start=False, stop=True, skip_group_check=True)
                mm.then_inc(pb_used, 1)

            def turn_output(u):
                pe.wait_ge(oT_ready, LEAD + u + 1)
                for t in range(TT):
                    mm = pe.transpose(core.tiles(0)[:, t, :], oT[:, t * P:t * P + P], core.ident[:])
                mm.then_inc(oT_turned, 1)

            def step(u, i, p, more, first=False):
                pe.wait_ge(low_in[p], 64 * (i + 1))
                pe.wait_ge(va_ready, LEAD + u + 1)
                scores(u, p, 0)
                scores(u, p, 1)
                if not first:
                    turn_output(u - 1)
                if more:
                    pe.wait_ge(unit_in[1 - p], 64 * (i + 1 + p))
                    peaks(u + 1, 1 - p, range(0, 4))
                pe.wait_ge(oT_ready, LEAD + u)
                outputs(u, p, 0)
                scores(u, p, 2)
                if more:
                    peaks(u + 1, 1 - p, range(4, 8))
                outputs(u, p, 1)
                last_outputs(u, p, 0)
                scores(u, p, 3)
                if more:
                    peaks(u + 1, 1 - p, range(8, NP))
                outputs(u, p, 2)
                if more:
                    turn_peaks(u + 1, 1 - p)
                outputs(u, p, 3)
                last_outputs(u, p, 1)

            sweep(pe, prepare, step)
            turn_output(UNITS - 1)
            with pe.Fori(0, NB) as b:
                pe.wait_ge(at_ready, LEAD + b + 1)
                pe.wait_ge(aT_ready, LEAD + b)
                for t in range(TT):
                    pe.transpose(core.tiles(0)[:, t, :], at[:, t, :], core.ident[:]).then_inc(at_turned, 1)
                pe.wait_ge(aT_ready, LEAD + b + 1)
                pe.wait_ge(xa_ready, LEAD + b)
                for t in range(TT):
                    pe.matmul(core.tiles(1)[:, t, :], aT[:, t * P:t * P + P], wo[:], start=True, stop=False)
                    mm = pe.matmul(core.tiles(1)[:, t, :], core.ones_row[:], bo[:], start=False, stop=True)
                mm.then_inc(proj_ready, 1)
                pe.wait_ge(xaT_ready, LEAD + b)
                for t in range(TT):
                    pe.wait_ge(ln_2.normed, b * TT + t + 1)
                    pe.transpose(core.tiles(2)[:, t, :], un[:, t, :], core.ident[:]).then_inc(xa_turned, 1)
                pe.wait_ge(xaT_ready, LEAD + b + 1)
                for f in range(FB):
                    pe.wait_ge(h1_gelu, LEAD + FB * b + f - 1)
                    pe.matmul(bank[:, 3 + f % 2, :], w1[:, f * P:f * P + P], uT[:],
                              start=True, stop=True).then_inc(h1_ready, 1)
                pe.wait_ge(h1_gelu, LEAD + FB * b + FB)
                pe.wait_ge(xf_ready, LEAD + b)
                for t in range(TT):
                    for f in range(FB):
                        pe.matmul(core.tiles(5)[:, t, :], hT[:, f, t * P:t * P + P], w2[:, f, :],
                                  start=(f == 0), stop=False)
                    mm = pe.matmul(core.tiles(5)[:, t, :], core.ones_row[:], b2row[:], start=False, stop=True)
                mm.then_inc(ffn_ready, 1)


def build(nc, io, out):
    with ExitStack() as ctx:
        core = Core(nc, ctx, io)
        mamba(core)
        moe(core, 1)
        attention(core)
        moe(core, 2)
        stored = core.sem("stored")
        with nc.Block() as block:
            @block.sync
            def _(sp):
                sp.dma_start(out.rearrange("b (t p) d -> p (b t) d", p=P), core.X[:]).then_inc(stored, 16)
                sp.wait_ge(stored, 16)


def constants():
    bf16 = mybir.dt.np(BF16)
    line = lambda x: np.ascontiguousarray(x, dtype=np.float32).reshape(-1)
    grid = np.zeros((NE, NT))
    inverse = (np.float32(1.0) / np.float32(10000.0) ** (np.arange(0, HD, 2, dtype=np.float32) / np.float32(HD))).astype(np.float32)
    angle = np.tile(np.arange(T, dtype=np.float32)[None, :] * np.tile(inverse, 2)[:, None], (NH, 1))
    swap = np.zeros((HD, HD), np.float32)
    for d in range(HD // 2):
        swap[d + HD // 2, d] = -1.0
        swap[d, d + HD // 2] = 1.0
    later = np.triu(np.full((P, P), FAR, np.float32), 1)
    eye = np.eye(P, dtype=np.float32)
    return dict(cos=np.cos(angle), sin=np.sin(angle), rot=np.kron(np.eye(NH, dtype=np.float32), swap),
                hide_k=later.astype(bf16), hide_q=later.T.astype(bf16),
                ident=eye, identb=eye.astype(bf16),
                pick=np.tile(np.eye(32, dtype=np.float32), (3, 1)),
                iota_e=line(grid + np.arange(NE)[:, None]), thresh=line(grid + P * np.arange(NT)),
                reset=line(grid + (np.arange(NT) > 0)),
                iota_j=line(np.zeros((SLOT_TILES, NE)) + np.arange(SLOT_TILES)[:, None]),
                below=np.triu(np.ones((P, P)), 1).astype(bf16),
                onesb=np.ones((P, P), bf16))


def layout(i):
    a = {k: np.asarray(v) for k, v in i.items()}
    A, B, E = "L0_attn_a_", "L0_attn_b_", "L0_ffn_"
    col = lambda x: x.reshape(-1, P).T
    return dict(
        x=a[A + "x"], in_proj_t=a[A + "in_proj_w"].T, conv_w=a[A + "conv_w"],
        vec_a=np.stack([a[A + n] for n in ("ln1_g", "ln1_b", "conv_b", "dt_proj_b", "D_param", "ln2_g", "ln2_b")], 1),
        x_proj_t=a[A + "x_proj_w"].T, dt_proj_t=a[A + "dt_proj_w"].T, a_log=a[A + "A_log"],
        out_proj_t=a[A + "out_proj_w"].T, a_w1_t=a[A + "w1"].T, a_b1_t=col(a[A + "b1"]),
        a_w2_t=a[A + "w2"].T, a_b2=a[A + "b2"][None],
        vec_b=np.stack([a[B + n] for n in ("ln1_g", "ln1_b", "ln2_g", "ln2_b")] +
                       [a[B + "bqkv"][0:D], a[B + "bqkv"][D:2 * D]], 1),
        wqkv=a[B + "Wqkv"], bv=a[B + "bqkv"][2 * D:], wo=a[B + "Wo"], bo=a[B + "bo"][None],
        b_w1=a[B + "W1"], b_b1_t=col(a[B + "b1"]), b_w2=a[B + "W2"], b_b2=a[B + "b2"][None],
        gate_w=a[E + "gate_w"], gate_b=a[E + "gate_b"], e_w1=a[E + "w1"], e_w2=a[E + "w2"],
        e_b1_t=a[E + "b1"].reshape(NE * FB, P).T, e_b2=a[E + "b2"].reshape(-1),
    )


def kernel(**inputs):
    import concourse.bacc as _bacc
    from concourse.bass_utils import run_bass_kernel_spmd as _run

    nc = _bacc.Bacc("TRN2", target_bir_lowering=False, num_devices=1)
    arrays = {k: np.ascontiguousarray(v) for k, v in {**layout(inputs), **constants()}.items()}
    io = {k: nc.dram_tensor(f"in_{k}", v.shape, mybir.dt.from_np(v.dtype), kind="ExternalInput").ap()
          for k, v in arrays.items()}
    out = nc.dram_tensor("out_x", (NB, T, D), F32, kind="ExternalOutput").ap()
    build(nc, io, out)
    r = _run(nc, [{f"in_{k}": v for k, v in arrays.items()}], core_ids=[0])
    return r.results[0]["out_x"]
```

```python
from contextlib import ExitStack

import numpy as np

import concourse.bass as bass
from concourse import mybir

P = 128
D = 128
NB = 4
T = 512
TT = T // P
NT = NB * TT
NS = 16
NCONV = 8
RANK = 8
FF = 512
FB = FF // P
NE = 24
TOPK = 2
SLOT_TILES = (NB * T * TOPK - NE) // P + NE
SLOT_TILES += SLOT_TILES % 2
NH = 16
HD = 8
EPS = 1e-5
LOAD_EXPERTS = 4
LEAD = 4
FAR = -1.0e30

F32 = mybir.dt.float32
BF16 = mybir.dt.bfloat16
I32 = mybir.dt.int32
U32 = mybir.dt.uint32
ACT = mybir.ActivationFunctionType
ALU = mybir.AluOpType
AX_X = mybir.AxisListType.X



class Core:

    def __init__(self, nc, ctx, io):
        self.nc, self.ctx, self.io = nc, ctx, io
        self.retired = []
        self.bank = ctx.enter_context(nc.psum_tensor("bank", [P, 8, T], F32))
        self.X = self.sb("X", [P, NT, D])
        self.ident = self.sb("ident", [P, P])
        self.identb = self.sb("identb", [P, P], BF16)
        self.half = self.sb("half", [P, NT])
        self.ones_row = self.sb("ones_row", [1, P])
        self.w1all = self.sb("w1all", [P, NE, FF])
        self.w2all = self.sb("w2all", [P, NE, FB, D])
        self.experts_in = self.sem("experts_in")
        self.slots_in = nc.dram_tensor("slots_in", (SLOT_TILES * P, D), F32).ap()
        self.slots_out = nc.dram_tensor("slots_out", (SLOT_TILES * P, D), F32).ap()
        self.slots_zeroed = self.sem("slots_zeroed")
        self.consts_in = self.sem("consts_in")
        self.scattered = self.sem("scattered")
        self.gathered = [self.sem(f"gathered{i}") for i in range(NT)]
        self.consts_set = self.sem("consts_set")
        self.apart = self.sem("apart")
        self.identb_set = self.sem("identb_set")

    def sb(self, name, shape, dt=F32, ctx=None):
        return (ctx or self.ctx).enter_context(self.nc.sbuf_tensor(name, shape, dt))

    def sem(self, name, ctx=None):
        return (ctx or self.ctx).enter_context(self.nc.semaphore(name))

    def tiles(self, k):
        return self.bank[:, k, :].rearrange("p (t n) -> p t n", n=P)


class Stage:

    def __init__(self, core, tag):
        self.core, self.tag, self.ctx = core, tag, ExitStack()
        self.leading, self.sems = [], []

    def sb(self, name, shape, dt=F32):
        return self.core.sb(f"{self.tag}_{name}", shape, dt, self.ctx)

    def sem(self, name):
        s = self.core.sem(f"{self.tag}_{name}", self.ctx)
        self.sems.append(s)
        return s

    def lead(self, name):
        s = self.sem(name)
        self.leading.append(s)
        return s

    def set_leads(self, g):
        for s in self.leading:
            g.sem_inc(s, LEAD)
        for s in self.core.retired:
            g.sem_clear(s)
        self.core.retired = self.sems


class Norm:

    def __init__(self, st, name):
        self.stats = st.sb(name + "_stats", [P, NT, 6])
        self.mv = st.sb(name + "_mv", [P, NT, 2])
        self.ve = st.sb(name + "_ve", [P, NT])
        self.rs = st.sb(name + "_rs", [P, NT])
        self.stats_done = st.sem(name + "_stats_done")
        self.mean_var_ready = st.sem(name + "_mean_var_ready")
        self.var_eps_ready = st.sem(name + "_var_eps_ready")
        self.rstd_ready = st.sem(name + "_rstd_ready")
        self.normed = st.sem(name + "_normed")


def apart(eng, core):
    eng.sem_inc(core.apart, 1)


def norm_vector(v, ln, src, dst):
    with v.Fori(0, NB) as b:
        for t in range(TT):
            v.bn_stats(row(ln.stats, b * TT + t), row(src, b * TT + t)).then_inc(ln.stats_done, 1)
    v.wait_ge(ln.stats_done, NT)
    for i in range(NT):
        v.bn_aggr(ln.mv[:, i, :], ln.stats[:, i, :]).then_inc(ln.mean_var_ready, 1)
    v.wait_ge(ln.mean_var_ready, NT)
    v.wait_ge(ln.rstd_ready, 1)
    for i in range(NT):
        v.tensor_scalar(dst[:, i, :], src[:, i, :], ln.mv[:, i, 0:1], ln.rs[:, i:i + 1],
                        ALU.subtract, ALU.mult).then_inc(ln.normed, 1)


def norm_pool(g, core, ln):
    g.wait_ge(ln.mean_var_ready, NT)
    g.tensor_scalar(ln.ve[:], ln.mv[:, :, 1], EPS, None, ALU.add).then_inc(ln.var_eps_ready, 1)
    g.wait_ge(ln.var_eps_ready, 1)
    g.tensor_tensor(ln.rs[:], ln.ve[:], core.half[:], ALU.pow).then_inc(ln.rstd_ready, 1)


def row(x, i):
    return x[:, bass.ds(i, 1), :].rearrange("p a n -> p (a n)")


def mamba(core):
    nc, io, bank, X = core.nc, core.io, core.bank, core.X
    st = Stage(core, "m")
    win = st.sb("win", [P, 2 * D])
    convw = st.sb("convw", [P, NCONV])
    vec = st.sb("vec", [P, 7])
    LN1G, LN1B, CONVB, DTB, DSKIP, LN2G, LN2B = range(7)
    wx = st.sb("wx", [P, RANK + 96])
    wdt = st.sb("wdt", [RANK, P])
    a_neg = st.sb("a_neg", [P, NS])
    wout = st.sb("wout", [P, D])
    w1 = st.sb("w1", [P, FF])
    b1 = st.sb("b1", [P, FB])
    w2 = st.sb("w2", [P, FB, D])
    b2 = st.sb("b2", [P, D])
    taps = st.sb("taps", [P, NCONV, P])
    dskip = st.sb("dskip", [P, P])
    pick_s = st.sb("pick_s", [96, 32])
    pick = st.sb("pick", [96, 32, P], BF16)

    X1 = st.sb("X1", [P, NT, D])
    xpad = st.sb("xpad", [P, NCONV - 1 + T])
    XC = st.sb("XC", [P, NB, T])
    SZ = st.sb("SZ", [P, NB, T])
    DELTA = st.sb("DELTA", [P, NB, T])
    DX = st.sb("DX", [P, NB, T])
    BC = st.sb("BC", [96, NB, T], BF16)
    dt_sb = st.sb("dt_sb", [RANK, T])
    rest = st.sb("rest", [96, T])
    mid = st.sb("mid", [96, T], BF16)
    work = st.sb("work", [P, 8, T])
    token_major = lambda x: x.rearrange("p b (t d) -> p (b t) d", d=D)
    UN, UT = token_major(work[:, 0:NB, :]), work[:, NB:2 * NB, :]
    EXPV, RELU = work[:, 0:NB, :], work[:, NB:2 * NB, :]
    decay, h, c_sb, hc = (work[:, 2 * i:2 * i + 2, :] for i in range(4))
    YZ = work[:, 0:NB, :]
    hT = [work[:, FB * p:FB * p + FB, :] for p in range(2)]
    XA, UN2, UT2 = token_major(DELTA[:]), token_major(DX[:]), XC

    x_in, w_in, vec_in, alog_in, pick_in = map(st.sem, ("x_in", "w_in", "vec_in", "alog_in", "pick_in"))
    zeros, zeros_set = st.sb("zeros", [P, D]), st.sem("zeros_set")
    edge_set = st.sem("edge_set")
    a_exp, a_ready = st.sem("a_exp"), st.sem("a_ready")
    taps_ready, pick_ready = st.sem("taps_ready"), st.sem("pick_ready")
    ln_x, ln_1, ln_2 = Norm(st, "ln_x"), Norm(st, "ln_1"), Norm(st, "ln_2")
    un_turned, uT_ready, xin_ready, z_ready = map(st.sem, ("un_turned", "uT_ready", "xin_ready", "z_ready"))
    xpad_ready, sz_ready, conv_ready, xc_ready = map(st.lead, ("xpad_ready", "sz_ready", "conv_ready", "xc_ready"))
    dt_ready, dt_copied, bc_ready, bc_split = map(st.lead, ("dt_ready", "dt_copied", "bc_ready", "bc_split"))
    split_step = st.sem("split_step")
    dpre_ready, abs_ready, exp_ready, relu_ready = map(st.lead, ("dpre_ready", "abs_ready", "exp_ready", "relu_ready"))
    onep_ready, lnv_ready, delta_step, dx_ready = map(st.sem, ("onep_ready", "lnv_ready", "delta_step", "dx_ready"))
    b_ready, c_ready, decay_ready, dbx_ready = map(st.lead, ("b_ready", "c_ready", "decay_ready", "dbx_ready"))
    h_ready, c_copied, hc_ready, hc_summed = map(st.lead, ("h_ready", "c_copied", "hc_ready", "hc_summed"))
    y_ready = st.sem("y_ready")
    yz_ready, proj_ready, xa_ready, xa_added = map(st.sem, ("yz_ready", "proj_ready", "xa_ready", "xa_added"))
    xa_turned, xaT_ready, h1_ready, h1_relu = map(st.lead, ("xa_turned", "xaT_ready", "h1_ready", "h1_relu"))
    ffn_ready, x_done, b2_added = st.lead("ffn_ready"), st.lead("x_done"), st.sem("b2_added")

    with st.ctx, nc.Block() as block:
        W_LOADS = 12

        @block.sync
        def _(sp):
            sp.dma_start(X[:], io["x"].rearrange("b (t p) d -> p (b t) d", p=P)).then_inc(x_in, 16)
            sp.dma_start(core.ident[:], io["ident"]).then_inc(core.consts_in, 16)
            sp.dma_start(pick_s[:], io["pick"]).then_inc(pick_in, 16)
            sp.dma_start(a_neg[:], io["a_log"]).then_inc(alog_in, 16)
            sp.dma_start(win[:], io["in_proj_t"]).then_inc(w_in, 16)
            sp.dma_start(convw[:], io["conv_w"]).then_inc(vec_in, 16)
            sp.dma_start(vec[:], io["vec_a"]).then_inc(vec_in, 16)
            sp.dma_start(wx[:, 0:RANK], io["x_proj_t"][:, 0:RANK]).then_inc(w_in, 16)
            for r in range(3):
                sp.dma_start(wx[:, RANK + 32 * r:RANK + 32 * r + 32],
                             io["x_proj_t"][:, RANK:RANK + 32]).then_inc(w_in, 16)
            sp.dma_start(wdt[:], io["dt_proj_t"]).then_inc(w_in, 16)
            sp.dma_start(wout[:], io["out_proj_t"]).then_inc(w_in, 16)
            sp.dma_start(w1[:], io["a_w1_t"]).then_inc(w_in, 16)
            sp.dma_start(b1[:], io["a_b1_t"]).then_inc(w_in, 16)
            sp.dma_start(w2[:], io["a_w2_t"].rearrange("(f p) n -> p f n", p=P)).then_inc(w_in, 16)
            sp.dma_start(b2[:], io["a_b2"].partition_broadcast(P)).then_inc(w_in, 16)
            sp.dma_start(core.identb[:], io["identb"]).then_inc(w_in, 16)
            for e in range(0, NE, LOAD_EXPERTS):
                sp.dma_start(core.w1all[:, e:e + LOAD_EXPERTS, :],
                             io["e_w1"][e:e + LOAD_EXPERTS].rearrange("e d f -> d e f")).then_inc(core.experts_in, 16)
                sp.dma_start(core.w2all[:, e:e + LOAD_EXPERTS, :, :].rearrange("p e k n -> p (e k) n"),
                             io["e_w2"][e:e + LOAD_EXPERTS].rearrange("e (k p) n -> p (e k) n", p=P))\
                    .then_inc(core.experts_in, 16)
            sp.wait_ge(zeros_set, 1)
            sp.dma_start(core.slots_in.rearrange("(j p) d -> p j d", p=P),
                         zeros[:].unsqueeze(1).to_broadcast([P, SLOT_TILES, D])).then_inc(core.slots_zeroed, 16)

        @block.gpsimd
        def _(g):
            st.set_leads(g)
            g.memset(core.half[:], -0.5).then_inc(core.consts_set, 1)
            g.memset(core.ones_row[:], 1.0).then_inc(core.consts_set, 1)
            g.memset(xpad[:, 0:NCONV - 1], 0.0).then_inc(edge_set, 1)
            g.memset(zeros[:], 0.0).then_inc(zeros_set, 1)
            g.wait_ge(core.consts_set, 2)
            norm_pool(g, core, ln_x)
            norm_pool(g, core, ln_1)
            g.wait_ge(ln_x.normed, NT)
            g.wait_ge(w_in, 16 * W_LOADS)
            g.tensor_tensor(X[:], X[:], b2[:].unsqueeze(1).to_broadcast([P, NT, D]), ALU.add).then_inc(b2_added, 1)

            with g.Fori(0, NS) as n:
                for b in range(NB):
                    k = n * NB + b
                    g.wait_ge(h_ready, LEAD + k + 1)
                    g.wait_ge(c_copied, LEAD + k + 1)
                    g.wait_ge(hc_summed, LEAD + k - 1)
                    g.tensor_tensor(hc[:, b % 2, :], h[:, b % 2, :], c_sb[:, b % 2, :],
                                    ALU.mult).then_inc(hc_ready, 1)
            norm_pool(g, core, ln_2)
            g.wait_ge(b2_added, 1)
            for b in range(NB):
                g.tensor_tensor(X[:, b * TT:b * TT + TT, :], X[:, b * TT:b * TT + TT, :],
                                XA[:, b * TT:b * TT + TT, :], ALU.add).then_inc(xa_added, 1)

        @block.scalar
        def _(act):
            act.wait_ge(vec_in, 32)
            act.wait_ge(w_in, 16 * W_LOADS)
            act.wait_ge(edge_set, 1)
            for b in range(NB):
                act.wait_ge(un_turned, b + 1)
                act.activation(UT[:, b, :], bank[:, b, :], ACT.Identity, bias=vec[:, LN1B:LN1B + 1],
                               scale=vec[:, LN1G:LN1G + 1]).then_inc(uT_ready, 1)
            for b in range(NB + 1):
                if b < NB:
                    act.wait_ge(xin_ready, b + 1)
                    if b >= 1:
                        act.wait_ge(conv_ready, LEAD + b)
                    act.activation(xpad[:, NCONV - 1:], bank[:, 4, :], ACT.Identity).then_inc(xpad_ready, 1)
                    act.wait_ge(z_ready, b + 1)
                    act.activation(SZ[:, b, :], bank[:, 5, :], ACT.Silu).then_inc(sz_ready, 1)
                if b >= 1:
                    act.wait_ge(dpre_ready, LEAD + b)
                    act.activation(EXPV[:, b - 1, :], bank[:, 6, :], ACT.Abs,
                                   bias=vec[:, DTB:DTB + 1]).then_inc(abs_ready, 1)
                if b < NB:
                    act.wait_ge(conv_ready, LEAD + b + 1)
                    act.activation(XC[:, b, :], bank[:, 0, :], ACT.Silu,
                                   bias=vec[:, CONVB:CONVB + 1]).then_inc(xc_ready, 1)
            act.preload_act_table(ACT.Exp)
            act.wait_ge(alog_in, 16)
            act.activation(a_neg[:], a_neg[:], ACT.Exp).then_inc(a_exp, 1)
            act.wait_ge(abs_ready, LEAD + NB)
            act.activation(EXPV, EXPV, ACT.Exp, scale=-1.0).then_inc(exp_ready, 1)
            act.preload_act_table(ACT.Ln)
            act.wait_ge(onep_ready, 1)
            act.activation(DELTA[:], DX[:], ACT.Ln).then_inc(lnv_ready, 1)
            act.preload_act_table(ACT.Exp)
            act.wait_ge(a_ready, 1)
            act.wait_ge(dx_ready, 1)
            with act.Fori(0, NS) as n:
                for b in range(NB):
                    k = n * NB + b
                    act.wait_ge(h_ready, LEAD + k - 1)
                    apart(act, core)
                    act.activation(decay[:, b % 2, :], DELTA[:, b, :], ACT.Exp,
                                   scale=a_neg[:, bass.ds(n, 1)]).then_inc(decay_ready, 1)
                    act.wait_ge(c_ready, LEAD + k + 1)
                    act.wait_ge(hc_ready, LEAD + k - 1)
                    act.activation(c_sb[:, b % 2, :], bank[:, 6 + b % 2, :], ACT.Identity).then_inc(c_copied, 1)
            for b in range(NB):
                act.wait_ge(xa_turned, LEAD + b + 1)
                act.activation(UT2[:, b, :], bank[:, b, :], ACT.Identity, bias=vec[:, LN2B:LN2B + 1],
                               scale=vec[:, LN2G:LN2G + 1]).then_inc(xaT_ready, 1)
            act.wait_ge(proj_ready, NB)
            with act.Fori(0, NB // 2) as i:
                for p in range(2):
                    b = i * 2 + p
                    act.wait_ge(ffn_ready, LEAD + b - 1)
                    for f in range(FB):
                        act.wait_ge(h1_ready, LEAD + FB * b + f + 1)
                        act.activation(hT[p][:, f, :], bank[:, 4 + f, :], ACT.Relu,
                                       bias=b1[:, f:f + 1]).then_inc(h1_relu, 1)

        @block.vector
        def _(v):
            v.wait_ge(core.consts_in, 16)
            v.wait_ge(vec_in, 32)
            for j in range(NCONV):
                v.tensor_scalar(taps[:, j, :], core.ident[:], convw[:, j:j + 1], None, ALU.mult).then_inc(taps_ready, 1)
            v.tensor_scalar(dskip[:], core.ident[:], vec[:, DSKIP:DSKIP + 1], None, ALU.mult).then_inc(taps_ready, 1)
            v.wait_ge(x_in, 16)
            v.wait_ge(core.consts_set, 2)
            norm_vector(v, ln_x, X, X1)
            v.wait_ge(ln_x.normed, NT)
            norm_vector(v, ln_1, X1, UN)

            def split(b):
                v.wait_ge(dt_ready, LEAD + b + 1)
                v.tensor_copy(dt_sb[:], bank[0:RANK, 2, :]).then_inc(dt_copied, 1)
                v.wait_ge(bc_ready, LEAD + b + 1)
                v.tensor_copy(BC[:, b, :], bank[0:96, 3, :]).then_inc(split_step, 1)
                v.wait_ge(split_step, b * 3 + 1)
                v.tensor_tensor(rest[:], bank[0:96, 3, :], BC[:, b, :], ALU.subtract).then_inc(split_step, 1)
                v.wait_ge(split_step, b * 3 + 2)
                v.tensor_copy(mid[:], rest[:]).then_inc(split_step, 1)
                v.wait_ge(split_step, b * 3 + 3)
                v.tensor_copy(BC[32:64, b, :], mid[32:64, :])
                v.tensor_tensor(BC[64:96, b, :], rest[64:96, :], mid[64:96, :], ALU.subtract).then_inc(bc_split, 1)
                v.wait_ge(dpre_ready, LEAD + b + 1)
                v.wait_ge(abs_ready, LEAD + b + 1)
                v.tensor_scalar(RELU[:, b, :], bank[:, 6, :], vec[:, DTB:DTB + 1], 0.0,
                                ALU.add, ALU.max).then_inc(relu_ready, 1)

            v.wait_ge(pick_in, 16)
            v.tensor_copy(pick[:], pick_s[:].unsqueeze(2).to_broadcast([96, 32, P])).then_inc(pick_ready, 1)
            for b in range(NB):
                split(b)
            v.wait_ge(a_exp, 1)
            v.tensor_scalar(a_neg[:], a_neg[:], -1.0, None, ALU.mult).then_inc(a_ready, 1)
            v.wait_ge(exp_ready, LEAD + 1)
            v.tensor_scalar(DX[:], EXPV, 1.0, None, ALU.add).then_inc(onep_ready, 1)
            v.wait_ge(onep_ready, 1)
            v.scalar_tensor_tensor(out=EXPV, in0=DX[:], scalar=1.0, in1=EXPV,
                                   op0=ALU.subtract, op1=ALU.subtract).then_inc(delta_step, 1)
            v.wait_ge(delta_step, 1)
            v.wait_ge(relu_ready, LEAD + NB)
            v.tensor_tensor(RELU, RELU, EXPV, ALU.subtract).then_inc(delta_step, 1)
            v.wait_ge(delta_step, 2)
            v.wait_ge(lnv_ready, 1)
            v.tensor_tensor(DELTA[:], DELTA[:], RELU, ALU.add).then_inc(delta_step, 1)
            v.wait_ge(delta_step, 3)
            v.wait_ge(xc_ready, LEAD + NB)
            v.tensor_tensor(DX[:], DELTA[:], XC[:], ALU.mult).then_inc(dx_ready, 1)
            v.wait_ge(dx_ready, 1)
            with v.Fori(0, NS) as n:
                for b in range(NB):
                    k = n * NB + b
                    v.wait_ge(b_ready, LEAD + k + 1)
                    v.tensor_tensor(bank[:, 4 + b % 2, :], bank[:, 4 + b % 2, :], DX[:, b, :],
                                    ALU.mult).then_inc(dbx_ready, 1)
                    v.wait_ge(dbx_ready, LEAD + k + 1)
                    v.wait_ge(decay_ready, LEAD + k + 1)
                    v.wait_ge(hc_ready, LEAD + k - 1)
                    v.tensor_tensor_scan(h[:, b % 2, :], decay[:, b % 2, :], bank[:, 4 + b % 2, :],
                                         0.0, ALU.mult, ALU.add).then_inc(h_ready, 1)
            v.wait_ge(y_ready, 1)
            for b in range(NB):
                v.tensor_tensor(YZ[:, b, :], bank[:, b, :], SZ[:, b, :], ALU.mult).then_inc(yz_ready, 1)
            for b in range(NB):
                v.wait_ge(proj_ready, b + 1)
                v.tensor_tensor(XA[:, b * TT:b * TT + TT, :], core.tiles(4 + b), X1[:, b * TT:b * TT + TT, :],
                                ALU.add).then_inc(xa_ready, 1)
            v.wait_ge(xa_ready, NB)
            norm_vector(v, ln_2, XA, UN2)
            v.wait_ge(xa_added, NB)
            with v.Fori(0, NB // 2) as i:
                for p in range(2):
                    b = i * 2 + p
                    v.wait_ge(ffn_ready, LEAD + b + 1)
                    v.tensor_tensor(X[:, bass.ds(b * TT, TT), :], X[:, bass.ds(b * TT, TT), :], core.tiles(p),
                                    ALU.add).then_inc(x_done, 1)
            v.wait_ge(x_done, LEAD + NB)

        @block.tensor
        def _(pe):
            pe.wait_ge(w_in, 16 * W_LOADS)
            pe.wait_ge(core.consts_in, 16)
            for b in range(NB):
                pe.wait_ge(ln_1.normed, b * TT + TT)
                for t in range(TT):
                    tr = pe.transpose(core.tiles(b)[:, t, :], UN[:, b * TT + t, :], core.ident[:])
                tr.then_inc(un_turned, 1)

            def project(b):
                pe.wait_ge(uT_ready, b + 1)
                pe.wait_ge(xpad_ready, LEAD + b)
                pe.matmul(bank[:, 4, :], win[:, 0:D], UT[:, b, :], start=True, stop=True).then_inc(xin_ready, 1)
                pe.wait_ge(sz_ready, LEAD + b)
                pe.matmul(bank[:, 5, :], win[:, D:2 * D], UT[:, b, :], start=True, stop=True).then_inc(z_ready, 1)

            def convolve(b):
                pe.wait_ge(xpad_ready, LEAD + b + 1)
                pe.wait_ge(xc_ready, LEAD + b)
                for j in range(NCONV):
                    mm = pe.matmul(bank[:, 0, :], taps[:, j, :], xpad[:, j:j + T],
                                   start=(j == 0), stop=(j == NCONV - 1))
                mm.then_inc(conv_ready, 1)

            def select(b):
                pe.wait_ge(xc_ready, LEAD + b + 1)
                pe.wait_ge(dt_copied, LEAD + b)
                pe.matmul(bank[0:RANK, 2, :], wx[:, 0:RANK], XC[:, b, :], start=True, stop=True).then_inc(dt_ready, 1)
                pe.wait_ge(bc_split, LEAD + b)
                pe.matmul(bank[0:96, 3, :], wx[:, RANK:], XC[:, b, :], start=True, stop=True).then_inc(bc_ready, 1)

            def time_step(b):
                pe.wait_ge(dt_copied, LEAD + b + 1)
                pe.wait_ge(abs_ready, LEAD + b)
                pe.wait_ge(relu_ready, LEAD + b)
                pe.matmul(bank[:, 6, :], wdt[:], dt_sb[:], start=True, stop=True).then_inc(dpre_ready, 1)

            pe.wait_ge(uT_ready, NB)
            pe.wait_ge(taps_ready, NCONV + 1)
            project(0)
            convolve(0)
            for b in range(1, NB):
                project(b)
                select(b - 1)
                time_step(b - 1)
                convolve(b)
            select(NB - 1)
            time_step(NB - 1)
            pe.wait_ge(pick_ready, 1)
            pe.wait_ge(bc_split, LEAD + NB)
            pe.wait_ge(relu_ready, LEAD + NB)
            pe.wait_ge(abs_ready, LEAD + NB)

            for b in range(NB):
                pe.matmul(bank[:, b, :], dskip[:], XC[:, b, :], start=True, stop=False, skip_group_check=True)

            def state(n, first=False, last=False):
                for b in range(NB):
                    k = n * NB + b
                    pe.wait_ge(h_ready, LEAD + k - 1)
                    pe.matmul(bank[:, 4 + b % 2, :], pick[:, bass.ds(n, 1), :].rearrange("p a n -> p (a n)"),
                              BC[:, b, :], start=True, stop=True).then_inc(b_ready, 1)
                    pe.wait_ge(c_copied, LEAD + k - 1)
                    pe.matmul(bank[:, 6 + b % 2, :], pick[:, bass.ds(n + NS, 1), :].rearrange("p a n -> p (a n)"),
                              BC[:, b, :], start=True, stop=True).then_inc(c_ready, 1)
                    if first and b < 2:
                        continue
                    pe.wait_ge(hc_ready, LEAD + k - 1)
                    pe.matmul(bank[:, (b + 2) % NB, :], core.ident[:], hc[:, b % 2, :],
                              start=False, stop=(last and b >= 2), skip_group_check=True).then_inc(hc_summed, 1)

            state(0, first=True)
            with pe.Fori(1, NS - 1) as n:
                state(n)
            state(NS - 1, last=True)
            for b in range(2, NB):
                pe.wait_ge(hc_ready, LEAD + NS * NB - NB + b + 1)
                mm = pe.matmul(bank[:, b, :], core.ident[:], hc[:, b % 2, :],
                               start=False, stop=True, skip_group_check=True)
            mm.then_inc(y_ready, 1)
            for b in range(NB):
                pe.wait_ge(yz_ready, b + 1)
                for t in range(TT):
                    mm = pe.matmul(core.tiles(4 + b)[:, t, :], YZ[:, b, t * P:t * P + P], wout[:], start=True, stop=True)
                mm.then_inc(proj_ready, 1)
            for b in range(NB):
                pe.wait_ge(ln_2.normed, b * TT + TT)
                for t in range(TT):
                    tr = pe.transpose(core.tiles(b)[:, t, :], UN2[:, b * TT + t, :], core.ident[:])
                tr.then_inc(xa_turned, 1)
            pe.wait_ge(xaT_ready, LEAD + NB)

            def hidden(b):
                for f in range(FB):
                    pe.wait_ge(h1_relu, LEAD + FB * b + f - FB + 1)
                    pe.matmul(bank[:, 4 + f, :], w1[:, f * P:f * P + P], row(UT2, b),
                              start=True, stop=True).then_inc(h1_ready, 1)

            def feed_forward(b, p):
                pe.wait_ge(h1_relu, LEAD + FB * b + FB)
                pe.wait_ge(x_done, LEAD + b - 1)
                for t in range(TT):
                    for f in range(FB):
                        mm = pe.matmul(core.tiles(p)[:, t, :], hT[p][:, f, t * P:t * P + P], w2[:, f, :],
                                       start=(f == 0), stop=(f == FB - 1))
                mm.then_inc(ffn_ready, 1)

            hidden(0)
            hidden(1)
            feed_forward(0, 0)
            with pe.Fori(1, NB // 2) as i:
                for p in range(2):
                    hidden(i * 2 + p)
                    feed_forward(i * 2 + p - 1, 1 - p)
            feed_forward(NB - 1, 1)


def moe(core, layer):
    io, bank, X = core.io, core.bank, core.X
    st = Stage(core, f"e{layer}")
    scattered, gathered = core.scattered, core.gathered
    gate_w = st.sb("gate_w", [P, NE])
    gate_b = st.sb("gate_b", [P, NE])
    b1all = st.sb("b1all", [P, NE, FB])
    b2all = st.sb("b2all", [P, NE, D])
    iota_e = st.sb("iota_e", [P, NE, NT])
    thresh = st.sb("thresh", [P, NE, NT])
    reset = st.sb("reset", [P, NE * NT])
    iota_j = st.sb("iota_j", [1, SLOT_TILES, NE])
    below = st.sb("below", [P, P], BF16)
    onesb = st.sb("onesb", [P, P], BF16)
    XF = st.sb("XF", [P, NT, D])
    score = st.sb("score", [P, NT, NE])
    best = st.sb("best", [P, NT, 8])
    best_at = st.sb("best_at", [P, NT, 8], U32)
    value = st.sb("value", [P, NT, TOPK])
    expert = st.sb("expert", [P, NT, TOPK])
    chosen = [st.sb(f"chosen{k}", [P, NE, NT]) for k in range(TOPK)]
    member = st.sb("member", [P, NE * NT])
    memberb = st.sb("memberb", [P, NE * NT], BF16)
    upto = st.sb("upto", [P, NE * NT])
    before = st.sb("before", [P, NE * NT], BF16)
    total = st.sb("total", [P, NE], BF16)
    filled = st.sb("filled", [P, NE, NT])
    ntile = st.sb("ntile", [P, NE])
    tile_end = st.sb("tile_end", [P, NE])
    tile_start = st.sb("tile_start", [P, NE])
    place = st.sb("place", [P, NE, NT])
    placed = st.sb("placed", [P, NE, NT])
    slotf = st.sb("slotf", [P, TOPK, NT])
    slot = st.sb("slot", [P, TOPK, NT], I32)
    past = st.sb("past", [1, SLOT_TILES, NE])
    ownerf = st.sb("ownerf", [1, SLOT_TILES])
    owner = st.sb("owner", [1, SLOT_TILES], I32)
    gdiff = st.sb("gdiff", [P, NT])
    gexp = st.sb("gexp", [P, NT])
    gsum = st.sb("gsum", [P, NT])
    gate = st.sb("gate", [P, TOPK, NT])
    xs = st.sb("xs", [P, 4, D])
    xsT = st.sb("xsT", [P, 2, P])
    w1b = st.sb("w1b", [P, 4, FF])
    b1b = st.sb("b1b", [P, 4, FB])
    b2b = st.sb("b2b", [P, 4, D])
    hid = st.sb("hid", [P, 2, FB * P])
    ysb = st.sb("ysb", [P, 4, D])
    back = [st.sb(f"back{k}", [P, NT, D]) for k in range(TOPK)]
    xT = back[0][:].rearrange("p (b t) d -> p b (t d)", t=TT)

    gate_in, bias_in, tables_in = map(st.sem, ("gate_in", "bias_in", "tables_in"))
    ln = Norm(st, "ln")
    turned, xT_ready, score_ready, score_biased = map(st.sem, ("turned", "xT_ready", "score_ready", "score_biased"))
    best_ready, best_at_ready, best_kept = map(st.sem, ("best_ready", "best_at_ready", "best_kept"))
    route_step, rank_ready, slot_ready, owner_ready = map(st.sem, ("route_step", "rank_ready", "slot_ready", "owner_ready"))
    members_ready = st.sem("members_ready")
    gdiff_ready, gexp_ready = st.sem("gdiff_ready"), st.sem("gexp_ready")
    slot_in = [st.sem(f"slot_in{q}") for q in range(4)]
    slot_turned, xsT_ready, w1_ready, b1_ready = map(st.lead, ("slot_turned", "xsT_ready", "w1_ready", "b1_ready"))
    b2_ready, mm1_done, gelu_done = map(st.lead, ("b2_ready", "mm1_done", "gelu_done"))
    mm2_done, y_ready = map(st.lead, ("mm2_done", "y_ready"))
    y_out = [st.lead(f"y_out{q}") for q in range(4)]
    ones_e, ones_set = st.sb("ones_e", [P, NE]), st.sem("ones_set")
    skip_added, first_added, second_added = map(st.sem, ("skip_added", "first_added", "second_added"))

    STEPS = SLOT_TILES + 3

    def steps(eng, step):
        for j in range(4):
            step(j, j)
        with eng.Fori(1, SLOT_TILES // 4 - 1) as i:
            for q in range(4):
                step(i * 4 + q, q, loop=True)
        for j in range(SLOT_TILES - 4, STEPS):
            step(j, j % 4)

    def has(j, lag, loop):
        return loop or 0 <= j - lag < SLOT_TILES

    with st.ctx, core.nc.Block() as block:
        @block.sync
        def _(sp):
            sp.dma_start(gate_w[:], io["gate_w"]).then_inc(gate_in, 16)
            sp.dma_start(gate_b[:], io["gate_b"].partition_broadcast(P)).then_inc(gate_in, 16)
            for dst, name in ((iota_e, "iota_e"), (thresh, "thresh"), (iota_j, "iota_j")):
                n = dst.shape[0]
                sp.dma_start(dst[:].rearrange("p a b -> p (a b)"), io[name].partition_broadcast(n)).then_inc(tables_in, 16)
            sp.dma_start(reset[:], io["reset"].partition_broadcast(P)).then_inc(tables_in, 16)
            sp.dma_start(below[:], io["below"]).then_inc(tables_in, 16)
            sp.dma_start(onesb[:], io["onesb"]).then_inc(tables_in, 16)
            sp.dma_start(b1all[:].rearrange("p e k -> p (e k)"), io["e_b1_t"]).then_inc(bias_in, 16)
            sp.dma_start(b2all[:].rearrange("p e n -> p (e n)"), io["e_b2"].partition_broadcast(P)).then_inc(bias_in, 16)
            sp.wait_ge(scattered, 16 * NT * TOPK * layer)

            def load(j, q):
                sp.dma_start(xs[:, q, :], core.slots_in[bass.ds(j * P, P), :]).then_inc(slot_in[q], 16)

            for j in range(4):
                load(j, j)

            def step(j, q, loop=False):
                if loop or (4 <= j + 2 < SLOT_TILES):
                    sp.wait_ge(slot_turned, LEAD + j - 1)
                    load(j + 2, (q + 2) % 4)
                if has(j, 3, loop):
                    sp.wait_ge(y_ready, LEAD + j - 2)
                    sp.dma_start(core.slots_out[bass.ds((j - 3) * P, P), :], ysb[:, (q + 1) % 4, :])\
                        .then_inc(y_out[(q + 1) % 4], 16)
            steps(sp, step)
            for q in range(4):
                sp.wait_ge(y_out[q], LEAD + 16 * SLOT_TILES // 4)

        @block.gpsimd
        def _(g):
            st.set_leads(g)
            norm_pool(g, core, ln)
            g.wait_ge(ln.normed, NT)
            g.wait_ge(core.slots_zeroed, 16)
            g.wait_ge(slot_ready, 1)
            for i in range(NT):
                for k in range(TOPK):
                    g.indirect_dma_start(core.slots_in, bass.IndirectOffsetOnAxis(slot[:, k, i:i + 1].bitcast(U32), 0),
                                         XF[:, i, :], None).then_inc(scattered, 16)
            for q in range(4):
                g.wait_ge(y_out[q], LEAD + 16 * SLOT_TILES // 4)
            for i in range(NT):
                for k in range(TOPK):
                    g.indirect_dma_start(back[k][:, i, :], None, core.slots_out,
                                         bass.IndirectOffsetOnAxis(slot[:, k, i:i + 1].bitcast(U32), 0))\
                        .then_inc(gathered[i], 16)

        @block.scalar
        def _(act):
            for b in range(NB):
                act.wait_ge(turned, b + 1)
                act.activation(xT[:, b, :], bank[:, b, :], ACT.Identity).then_inc(xT_ready, 1)
            act.wait_ge(gdiff_ready, 1)
            act.activation(gexp[:], gdiff[:], ACT.Exp).then_inc(gexp_ready, 1)
            act.preload_act_table(ACT.Gelu)

            def step(j, q, loop=False):
                if has(j, 1, loop):
                    m, mq = j - 1, (q + 3) % 4
                    act.wait_ge(b1_ready, LEAD + m + 1)
                    act.wait_ge(mm2_done, LEAD + m - 1)
                    act.wait_ge(mm1_done, LEAD + m + 1)
                    for f in range(FB):
                        ins = act.activation(hid[:, mq % 2, f * P:f * P + P], core.tiles(2 + mq % 2)[:, f, :],
                                             ACT.Gelu, bias=b1b[:, mq, f:f + 1])
                    ins.then_inc(gelu_done, 1)
            steps(act, step)

        @block.vector
        def _(v):
            v.memset(ones_e[:], 1.0).then_inc(ones_set, 1)
            v.wait_ge(ones_set, 1)
            v.wait_ge(gate_in, 32)
            norm_vector(v, ln, X, XF)
            v.wait_ge(score_ready, 1)
            v.tensor_tensor(score[:], bank[:, 4, 0:NT * NE].rearrange("p (t e) -> p t e", e=NE),
                            gate_b[:].unsqueeze(1).to_broadcast([P, NT, NE]), ALU.add).then_inc(score_biased, 1)
            v.wait_ge(score_biased, 1)
            for i in range(NT):
                v.max(best[:, i, :], score[:, i, :]).then_inc(best_ready, 1)
            v.wait_ge(best_ready, NT)
            for i in range(NT):
                v.max_index(best_at[:, i, :], best[:, i, :], score[:, i, :]).then_inc(best_at_ready, 1)
            v.wait_ge(best_at_ready, NT)
            v.tensor_copy(value[:], best[:, :, 0:TOPK]).then_inc(best_kept, 1)
            v.tensor_copy(expert[:], best_at[:, :, 0:TOPK]).then_inc(best_kept, 1)
            v.wait_ge(best_kept, 2)
            v.wait_ge(tables_in, 16 * 6)
            done = [0]

            def then(ins):
                done[0] += 1
                ins.then_inc(route_step, 1)
                v.wait_ge(route_step, done[0])

            v.tensor_tensor(gdiff[:], value[:, :, 1], value[:, :, 0], ALU.subtract).then_inc(gdiff_ready, 1)
            for k in range(TOPK):
                ins = v.tensor_tensor(chosen[k][:], iota_e[:],
                                      expert[:, :, k].unsqueeze(1).to_broadcast([P, NE, NT]), ALU.is_equal)
            then(ins)
            flat = lambda x: x[:].rearrange("p e t -> p (e t)")
            then(v.tensor_tensor(member[:], flat(chosen[0]), flat(chosen[1]), ALU.add))
            v.tensor_copy(memberb[:], member[:])
            then(v.tensor_tensor_scan(upto[:], reset[:], member[:], 0.0, ALU.mult, ALU.add))
            v.tensor_copy(total[:], upto[:].rearrange("p (e t) -> p e t", t=NT)[:, :, NT - 1])
            v.tensor_tensor(before[:], upto[:], member[:], ALU.subtract).then_inc(members_ready, 1)
            v.wait_ge(rank_ready, 1)
            then(v.tensor_tensor(filled[:], bank[:, 3, 0:NE].unsqueeze(2).to_broadcast([P, NE, NT]), thresh[:],
                                 ALU.is_gt))
            then(v.tensor_reduce(ntile[:], filled[:], AX_X, ALU.add))
            then(v.tensor_tensor_scan(tile_end[:], ones_e[:], ntile[:], 0.0, ALU.mult, ALU.add))
            then(v.tensor_tensor(tile_start[:], tile_end[:], ntile[:], ALU.subtract))
            then(v.scalar_tensor_tensor(out=place[:], in0=tile_start[:].unsqueeze(2).to_broadcast([P, NE, NT]),
                                        scalar=float(P), in1=bank[:, 2, 0:NE * NT].rearrange("p (e t) -> p e t", t=NT),
                                        op0=ALU.mult, op1=ALU.add))
            for k in range(TOPK):
                then(v.tensor_tensor(placed[:], place[:], chosen[k][:], ALU.mult))
                then(v.tensor_reduce(slotf[:, k, :], placed[:].rearrange("p e t -> p t e"), AX_X, ALU.add))
            v.tensor_copy(slot[:], slotf[:]).then_inc(slot_ready, 1)
            then(v.tensor_tensor(past[:], tile_end[0:1, :].unsqueeze(1).to_broadcast([1, SLOT_TILES, NE]), iota_j[:],
                                 ALU.is_le))
            then(v.tensor_reduce(ownerf[:], past[:], AX_X, ALU.add))
            v.tensor_scalar(owner[:], ownerf[:], float(NE - 1), None, ALU.min).then_inc(owner_ready, 1)
            v.wait_ge(owner_ready, 1)
            v.wait_ge(gexp_ready, 1)
            then(v.tensor_scalar(gsum[:], gexp[:], 1.0, None, ALU.add))
            then(v.reciprocal(gate[:, 0, :], gsum[:]))
            then(v.tensor_tensor(gate[:, 1, :], gexp[:], gate[:, 0, :], ALU.mult))
            v.tensor_tensor(X[:], X[:], XF[:], ALU.add).then_inc(skip_added, 1)
            v.wait_ge(bias_in, 32)
            v.wait_ge(core.experts_in, 16 * 2 * (NE // LOAD_EXPERTS))

            def step(j, q, loop=False):
                if has(j, 0, loop):
                    e = v.value_load(owner[0:1, bass.ds(j, 1)], min_val=0, max_val=NE - 1)
                    v.wait_ge(mm1_done, LEAD + j - 3)
                    v.wait_ge(gelu_done, LEAD + j - 3)
                    if loop or j >= 4:
                        v.wait_ge(y_ready, LEAD + j - 3)
                    apart(v, core)
                    v.tensor_copy(w1b[:, q, :], row(core.w1all, e)).then_inc(w1_ready, 1)
                    v.tensor_copy(b1b[:, q, :], row(b1all, e)).then_inc(b1_ready, 1)
                    v.tensor_copy(b2b[:, q, :], row(b2all, e)).then_inc(b2_ready, 1)
                    v.wait_ge(slot_turned, LEAD + j + 1)
                    v.tensor_copy(xsT[:, q % 2, :], core.tiles(q % 2)[:, 0, :]).then_inc(xsT_ready, 1)
                if has(j, 3, loop):
                    m, mq = j - 3, (q + 1) % 4
                    v.wait_ge(b2_ready, LEAD + m + 1)
                    if loop or m >= 4:
                        v.wait_ge(y_out[mq], LEAD + ((m - mq) * 4 if loop else (m // 4) * 16))
                    v.wait_ge(mm2_done, LEAD + m + 1)
                    v.tensor_tensor(ysb[:, mq, :], core.tiles(4 + mq % 2)[:, 0, :], b2b[:, mq, :],
                                    ALU.add).then_inc(y_ready, 1)
            steps(v, step)
            v.wait_ge(skip_added, 1)

            def second(i):
                v.wait_ge(first_added, i + 1)
                v.scalar_tensor_tensor(out=X[:, i, :], in0=back[1][:, i, :], scalar=gate[:, 1, i:i + 1],
                                       in1=X[:, i, :], op0=ALU.mult, op1=ALU.add).then_inc(second_added, 1)

            for i in range(NT):
                v.wait_ge(gathered[i], 16 * TOPK * layer)
                v.scalar_tensor_tensor(out=X[:, i, :], in0=back[0][:, i, :], scalar=gate[:, 0, i:i + 1],
                                       in1=X[:, i, :], op0=ALU.mult, op1=ALU.add).then_inc(first_added, 1)
                if i >= 1:
                    second(i - 1)
            second(NT - 1)
            v.wait_ge(second_added, NT)

        @block.tensor
        def _(pe):
            pe.wait_ge(gate_in, 32)
            for b in range(NB):
                pe.wait_ge(ln.normed, b * TT + TT)
                for t in range(TT):
                    tr = pe.transpose(core.tiles(b)[:, t, :], XF[:, b * TT + t, :], core.ident[:])
                tr.then_inc(turned, 1)
            for b in range(NB):
                pe.wait_ge(xT_ready, b + 1)
                for t in range(TT):
                    i = b * TT + t
                    mm = pe.matmul(bank[:, 4, i * NE:i * NE + NE], xT[:, b, t * P:t * P + P], gate_w[:],
                                   start=True, stop=True)
            mm.then_inc(score_ready, 1)
            pe.wait_ge(tables_in, 16 * 6)
            pe.wait_ge(members_ready, 1)
            pe.matmul(bank[:, 2, 0:NE * NT], below[:], memberb[:], start=True, stop=False)
            pe.matmul(bank[:, 2, 0:NE * NT], onesb[:], before[:], start=False, stop=True)
            pe.matmul(bank[:, 3, 0:NE], onesb[:], total[:], start=True, stop=True).then_inc(rank_ready, 1)
            pe.wait_ge(owner_ready, 1)
            pe.wait_ge(core.experts_in, 16 * 2 * (NE // LOAD_EXPERTS))
            pe.wait_ge(slot_ready, 1)

            def step(j, q, loop=False):
                if has(j, 0, loop):
                    pe.wait_ge(slot_in[q], ((j - q) * 4 if loop else (j // 4) * 16) + 16)
                    pe.wait_ge(xsT_ready, LEAD + j - 1)
                    pe.transpose(core.tiles(q % 2)[:, 0, :], xs[:, q, :], core.ident[:]).then_inc(slot_turned, 1)
                if has(j, 1, loop):
                    m, mq = j - 1, (q + 3) % 4
                    pe.wait_ge(w1_ready, LEAD + m + 1)
                    pe.wait_ge(xsT_ready, LEAD + m + 1)
                    pe.wait_ge(gelu_done, LEAD + m - 1)
                    for f in range(FB):
                        mm = pe.matmul(core.tiles(2 + mq % 2)[:, f, :], w1b[:, mq, f * P:f * P + P],
                                       xsT[:, mq % 2, :], start=True, stop=True)
                    mm.then_inc(mm1_done, 1)
                if has(j, 2, loop):
                    m, mq = j - 2, (q + 2) % 4
                    e = pe.value_load(owner[0:1, bass.ds(m, 1)], min_val=0, max_val=NE - 1)
                    pe.wait_ge(y_ready, LEAD + m - 1)
                    pe.wait_ge(gelu_done, LEAD + m + 1)
                    for f in range(FB):
                        mm = pe.matmul(core.tiles(4 + mq % 2)[:, 0, :], hid[:, mq % 2, f * P:f * P + P],
                                       core.w2all[:, bass.ds(e, 1), f, :].rearrange("p a n -> p (a n)"), start=(f == 0), stop=(f == FB - 1))
                    mm.then_inc(mm2_done, 1)
            steps(pe, step)


def attention(core):
    nc, io, bank, X = core.nc, core.io, core.bank, core.X
    st = Stage(core, "t")
    UNITS = NB * NH // 4
    ROWS = 6 * HD
    MID = 32
    Q_PARTS = (0, 0, 1, 0, 2, 1)
    K_PARTS = (0, 1, 0, 2, 0, 1)
    SCALE = 1.0 / float(np.sqrt(HD))
    ROT = (7, 0)
    stacks = nc.dram_tensor("stacks", (2, NB, NH, ROWS, T), BF16).ap()

    vec = st.sb("vec", [P, 6])
    LN1G, LN1B, LN2G, LN2B, BQ, BK = range(6)
    wqkv = st.sb("wqkv", [P, 3 * D])
    bv = st.sb("bv", [P, D])
    rot = st.sb("rot", [P, P])
    cos, sin = st.sb("cos", [P, T]), st.sb("sin", [P, T])
    wo = st.sb("wo", [P, D])
    bo, b2 = st.sb("bo", [P, D]), st.sb("b2", [P, D])
    w1, b1 = st.sb("w1", [P, FF]), st.sb("b1", [P, FB])
    w2 = st.sb("w2", [P, FB, D])
    identb = st.sb("identb", [P, P], BF16)
    hide_k = st.sb("hide_k", [P, P], BF16)
    hide_q = st.sb("hide_q", [P, P], BF16)

    XB = st.sb("XB", [P, NT, D])
    V = st.sb("V", [P, NT, D])
    A = st.sb("A", [P, NT, D])
    uT = [st.sb(f"uT{p}", [P, T]) for p in range(2)]
    qk = st.sb("qk", [P, 2, T])
    ropes = st.sb("ropes", [P, 4, T])
    side, turnedqk = ropes[:, 0:2, :], ropes[:, 2:4, :]
    part = [[st.sb(f"part{x}{i}", [P, T], BF16) for i in range(3)] for x in range(2)]
    QS = [st.sb(f"QS{p}", [P, 2, T], BF16) for p in range(2)]
    KS = [st.sb(f"KS{p}", [P, 2, T], BF16) for p in range(2)]
    va = [st.sb(f"va{p}", [P, TT, 4, 32]) for p in range(2)]
    peak = [st.sb(f"peak{p}", [P, TT, MID + 4]) for p in range(2)]
    low = [st.sb(f"low{p}", [P, T], BF16) for p in range(2)]
    spread = st.sb("spread", [P, 4, P], BF16)
    probs = st.sb("probs", [P, 6, T])
    pa = probs[:, 0:4, :].rearrange("p (s a) n -> p s (a n)", a=2)
    pb = probs[:, 4:6, :]
    token_major = lambda x: x.rearrange("p b (t d) -> p (b t) d", d=D)
    UN = token_major(probs[:, 0:NB, :])
    oT = st.sb("oT", [P, T])
    rsum = st.sb("rsum", [P, TT, 4])
    aT = uT
    XA = V
    hT = [st.sb("hT0", [P, FB, T]), ropes]

    w_in, tables_in = st.sem("w_in"), st.sem("tables_in")
    low_set, va_set = st.sem("low_set"), st.sem("va_set")
    ln_x, ln_1, ln_2 = Norm(st, "ln_x"), Norm(st, "ln_1"), Norm(st, "ln_2")
    un_turned, uT_ready, q_ready, k_ready = map(st.lead, ("un_turned", "uT_ready", "q_ready", "k_ready"))
    qk_ready, rot_ready, v_ready, v_kept = map(st.lead, ("qk_ready", "rot_ready", "v_ready", "v_kept"))
    cos_ready, sin_ready, rope_ready = map(st.lead, ("cos_ready", "sin_ready", "rope_ready"))
    part_ready = [st.sem(f"part_ready{x}") for x in range(2)]
    part_out = [st.lead(f"part_out{x}") for x in range(2)]
    unit_in = [st.sem(f"unit_in{p}") for p in range(2)]
    va_ready = st.lead("va_ready")
    peak_scored, peak_read = st.lead("peak_scored"), st.lead("peak_read")
    peak_whole, peak_turned = st.lead("peak_whole"), st.lead("peak_turned")
    low_hi_ready, low_ready = st.lead("low_hi_ready"), st.lead("low_ready")
    sa_ready, pa_ready, sb_ready, pb_ready = map(st.lead, ("sa_ready", "pa_ready", "sb_ready", "pb_ready"))
    pa_used, pb_used = map(st.lead, ("pa_used", "pb_used"))
    oT_ready, oT_turned, rsum_ready, a_ready = map(st.lead, ("oT_ready", "oT_turned", "rsum_ready", "a_ready"))
    at_turned, aT_ready, proj_ready, xa_ready, xa_added = map(st.sem, ("at_turned", "aT_ready", "proj_ready", "xa_ready", "xa_added"))
    xa_turned, xaT_ready, h1_ready, h1_gelu = map(st.lead, ("xa_turned", "xaT_ready", "h1_ready", "h1_gelu"))
    ffn_ready, x_done, bias_added = st.lead("ffn_ready"), st.lead("x_done"), st.sem("bias_added")
    part_copied, rest_ready = st.sem("part_copied"), st.sem("rest_ready")

    PEAKS = [(3, (j,)) for j in range(4)] + [(2, (j,)) for j in range(4)] + [(1, (0, 1)), (1, (2, 3)), (0, (0, 1)), (0, (2, 3))]
    NP = len(PEAKS)

    def sweep(eng, prepare, step):
        prepare(0, 0, 0)
        step(0, 0, 0, True, first=True)
        step(1, 0, 1, True)
        with eng.Fori(1, (UNITS - 2) // 2) as i:
            for p in range(2):
                step(i * 2 + p, i, p, True)
        step(UNITS - 2, UNITS // 2 - 1, 0, True)
        step(UNITS - 1, UNITS // 2 - 1, 1, False)

    W_LOADS = 16
    UT = A[:].rearrange("p (b t) d -> p b (t d)", t=TT)

    with st.ctx, nc.Block() as block:
        @block.sync
        def _(sp):
            for dst, name in ((vec, "vec_b"), (wqkv, "wqkv"), (rot, "rot"), (cos, "cos"), (sin, "sin"), (wo, "wo"),
                              (w1, "b_w1"), (b1, "b_b1_t"), (identb, "identb"),
                              (hide_k, "hide_k"), (hide_q, "hide_q"), (spread, "spread")):
                sp.dma_start(dst[:], io[name]).then_inc(w_in, 16)
            for dst, name in ((bv, "bv"), (bo, "bo"), (b2, "b_b2")):
                sp.dma_start(dst[:], io[name].partition_broadcast(P)).then_inc(w_in, 16)
            sp.dma_start(w2[:], io["b_w2"].rearrange("(f p) n -> p f n", p=P)).then_inc(w_in, 16)
            with sp.Fori(0, NB) as b:
                for x, parts in ((0, Q_PARTS), (1, K_PARTS)):
                    sp.wait_ge(part_ready[x], b + 1)
                    for r, i in enumerate(parts):
                        sp.dma_start(stacks[x, bass.ds(b, 1), :, r * HD:r * HD + HD, :].rearrange("a h d n -> (a h) d n"),
                                     part[x][i][:]).then_inc(part_out[x], 16)
            for x in range(2):
                sp.wait_ge(part_out[x], LEAD + 16 * 6 * NB)
            flat = stacks.rearrange("x b h r n -> x (b h) r n")

            def load(u, p):
                for x, S in ((0, QS), (1, KS)):
                    src = flat[x, bass.ds(u * 4, 4)].rearrange("(a s) r n -> a r s n", a=2)
                    for a in range(2):
                        sp.dma_start(S[p][64 * a:64 * a + ROWS, :, :], src[a]).then_inc(unit_in[p], 16)

            load(0, 0)
            load(1, 1)
            with sp.Fori(0, (UNITS - 2) // 2) as i:
                for p in range(2):
                    u = i * 2 + p
                    sp.wait_ge(sb_ready, LEAD + 2 * u + 2)
                    load(u + 2, p)

        @block.gpsimd
        def _(g):
            st.set_leads(g)
            for p in range(2):
                g.memset(peak[p][:], 0.0).then_inc(low_set, 1)
                g.memset(low[p][:], 0.0).then_inc(low_set, 1)
                g.memset(va[p][:], 0.0).then_inc(va_set, 1)
            g.wait_ge(va_set, 2)
            for p in range(2):
                g.memset(va[p][:, :, :, HD:HD + 1], 1.0).then_inc(va_set, 1)
            norm_pool(g, core, ln_x)
            norm_pool(g, core, ln_1)
            for b in range(NB):
                g.wait_ge(qk_ready, LEAD + 2 * b + 2)
                for x in range(2):
                    g.wait_ge(rope_ready, LEAD + 2 * b + x - 1)
                    g.tensor_tensor(side[:, x, :], qk[:, x, :], cos[:], ALU.mult).then_inc(cos_ready, 1)
            g.wait_ge(ln_1.normed, NT)
            for B, bias in ((XB, bo), (X, b2)):
                g.tensor_tensor(B[:], B[:], bias[:].unsqueeze(1).to_broadcast([P, NT, D]), ALU.add).then_inc(bias_added, 1)
            g.wait_ge(va_set, 4)
            g.wait_ge(v_kept, LEAD + NB)

            def values(u, p):
                tile0, col0 = u // 4 * TT, u % 4 * 32
                g.wait_ge(pb_used, LEAD + 2 * u - 2)
                apart(g, core)
                g.tensor_copy(va[p][:, :, :, 0:HD],
                              V[:, bass.ds(tile0, TT), bass.ds(col0, 32)].rearrange("p t (h d) -> p t h d", d=HD))\
                    .then_inc(va_ready, 1)

            with g.Fori(0, UNITS // 2) as i:
                for p in range(2):
                    values(i * 2 + p, p)
            norm_pool(g, core, ln_2)
            g.wait_ge(bias_added, 2)
            for b in range(NB):
                g.tensor_tensor(X[:, b * TT:b * TT + TT, :], X[:, b * TT:b * TT + TT, :],
                                XA[:, b * TT:b * TT + TT, :], ALU.add).then_inc(xa_added, 1)

        @block.scalar
        def _(act):
            act.wait_ge(w_in, 16 * W_LOADS)
            for b in range(NB + 1):
                if b < NB:
                    act.wait_ge(un_turned, LEAD + b + 1)
                    act.wait_ge(v_ready, LEAD + b - 1)
                    act.activation(uT[b % 2][:], bank[:, b, :], ACT.Identity, bias=vec[:, LN1B:LN1B + 1],
                                   scale=vec[:, LN1G:LN1G + 1]).then_inc(uT_ready, 1)
                for x in range(2):
                    if b < NB:
                        act.wait_ge((q_ready, k_ready)[x], LEAD + b + 1)
                        act.wait_ge(cos_ready, LEAD + 2 * b + x - 1)
                        act.wait_ge(rot_ready, LEAD + 2 * b + x - 1)
                        act.activation(qk[:, x, :], bank[:, 4 + x, :], ACT.Identity,
                                       bias=vec[:, BQ + x:BQ + x + 1]).then_inc(qk_ready, 1)
                if b >= 1:
                    for x in range(2):
                        k = 2 * (b - 1) + x
                        act.wait_ge(rope_ready, LEAD + k + 1)
                        act.wait_ge(part_out[x], LEAD + 16 * 6 * (b - 1))
                        act.activation(part[x][0][:], turnedqk[:, x, :], ACT.Identity).then_inc(part_copied, 1)
                        act.wait_ge(rest_ready, k + 1)
                        act.activation(part[x][1][:], turnedqk[:, x, :], ACT.Identity).then_inc(part_copied, 1)
            act.preload_act_table(ACT.Exp)

            act.wait_ge(low_set, 4)

            def prepare(u, i, p):
                act.wait_ge(peak_turned, LEAD + u + 1)
                act.activation(low[p][0:MID + 4, :], bank[0:MID + 4, 1, :], ACT.Identity, scale=-1.0)\
                    .then_inc(low_hi_ready, 1)

            def step(u, i, p, more, first=False):
                for j in range(4):
                    if j == 3 and more:
                        prepare(u + 1, i, 1 - p)
                    act.wait_ge(sa_ready, LEAD + 4 * u + j + 1)
                    act.wait_ge(pa_used, LEAD + 4 * u + j - 1)
                    act.activation(pa[:, j % 2, :], bank[:, 2 + 2 * (j % 2):4 + 2 * (j % 2), :].rearrange("p a n -> p (a n)"),
                                   ACT.Exp, scale=SCALE).then_inc(pa_ready, 1)
                    if j % 2:
                        act.wait_ge(sb_ready, LEAD + 2 * u + j // 2 + 1)
                        act.wait_ge(pb_used, LEAD + 2 * u + j // 2 - 1)
                        act.activation(pb[:, j // 2, :], bank[:, 6, :], ACT.Exp, scale=SCALE).then_inc(pb_ready, 1)
            sweep(act, prepare, step)
            act.preload_act_table(ACT.Gelu)
            for b in range(NB):
                act.wait_ge(at_turned, b + 1)
                if b >= 2:
                    act.wait_ge(proj_ready, b - 1)
                act.activation(aT[b % 2][:], bank[:, b, :], ACT.Identity).then_inc(aT_ready, 1)
            act.wait_ge(proj_ready, NB)
            for b in range(NB):
                act.wait_ge(xa_turned, LEAD + b + 1)
                act.wait_ge(a_ready, LEAD + UNITS)
                act.activation(UT[:, b, :], bank[:, b, :], ACT.Identity, bias=vec[:, LN2B:LN2B + 1],
                               scale=vec[:, LN2G:LN2G + 1]).then_inc(xaT_ready, 1)
            with act.Fori(0, NB // 2) as i:
                for p in range(2):
                    b = i * 2 + p
                    act.wait_ge(ffn_ready, LEAD + b - 1)
                    for f in range(FB):
                        act.wait_ge(h1_ready, LEAD + FB * b + f + 1)
                        act.activation(hT[p][:, f, :], bank[:, 4 + f, :], ACT.Gelu,
                                       bias=b1[:, f:f + 1]).then_inc(h1_gelu, 1)

        @block.vector
        def _(v):
            norm_vector(v, ln_x, X, XB)
            v.wait_ge(ln_x.normed, NT)
            norm_vector(v, ln_1, XB, UN)
            v.wait_ge(w_in, 16 * W_LOADS)
            for b in range(NB):
                v.wait_ge(v_ready, LEAD + b + 1)
                v.tensor_tensor(V[:, b * TT:b * TT + TT, :], core.tiles(6),
                                bv[:].unsqueeze(1).to_broadcast([P, TT, D]), ALU.add).then_inc(v_kept, 1)
                for x in range(2):
                    k = 2 * b + x
                    v.wait_ge(rot_ready, LEAD + k + 1)
                    if b >= 1:
                        v.wait_ge(part_ready[x], b)
                    v.tensor_tensor(turnedqk[:, x, :], core.bank[:, ROT[x], :], sin[:], ALU.mult).then_inc(sin_ready, 1)
                for x in range(2):
                    k = 2 * b + x
                    v.wait_ge(sin_ready, LEAD + k + 1)
                    v.wait_ge(cos_ready, LEAD + k + 1)
                    v.tensor_tensor(turnedqk[:, x, :], turnedqk[:, x, :], side[:, x, :], ALU.add).then_inc(rope_ready, 1)
                for x in range(2):
                    k = 2 * b + x
                    v.wait_ge(part_copied, 2 * k + 1)
                    v.tensor_tensor(turnedqk[:, x, :], turnedqk[:, x, :], part[x][0][:], ALU.subtract).then_inc(rest_ready, 1)
                    v.wait_ge(part_copied, 2 * k + 2)
                    v.wait_ge(part_out[x], LEAD + 16 * 6 * b)
                    v.tensor_tensor(part[x][2][:], turnedqk[:, x, :], part[x][1][:], ALU.subtract).then_inc(part_ready[x], 1)

            v.wait_ge(low_set, 4)

            def prepare(u, i, p):
                for n, (qt, js) in enumerate(PEAKS):
                    v.wait_ge(peak_scored, LEAD + NP * u + n + 1)
                    w = (qt + 1) * P
                    v.tensor_reduce(peak[p][:, qt, js[0]:js[-1] + 1],
                                    bank[:, n % 2, 0:len(js) * w].rearrange("p (j n) -> p j n", n=w),
                                    AX_X, ALU.max).then_inc(peak_read, 1)
                v.wait_ge(peak_read, LEAD + NP * u + NP)
                apart(v, core)
                v.tensor_copy(peak[p][:, :, MID:MID + 4], peak[p][:, :, 0:4]).then_inc(peak_whole, 1)
                v.wait_ge(low_hi_ready, LEAD + u + 1)
                second = slice(MID, MID + 4)
                v.scalar_tensor_tensor(out=low[p][second, :], in0=bank[second, 1, :], scalar=-1.0,
                                       in1=low[p][second, :], op0=ALU.mult, op1=ALU.subtract).then_inc(low_ready, 1)

            def normalise(u):
                v.wait_ge(oT_turned, LEAD + u + 1)
                o = core.tiles(0).rearrange("p t (h c) -> p t h c", c=32)
                v.reciprocal(rsum[:], o[:, :, :, HD]).then_inc(rsum_ready, 1)
                v.wait_ge(rsum_ready, LEAD + u + 1)
                apart(v, core)
                v.tensor_tensor(A[:, bass.ds(u // 4 * TT, TT), bass.ds(u % 4 * 32, 32)]
                                .rearrange("p t (h d) -> p t h d", d=HD), o[:, :, :, 0:HD],
                                rsum[:].unsqueeze(3).to_broadcast([P, TT, 4, HD]), ALU.mult).then_inc(a_ready, 1)

            def step(u, i, p, more, first=False):
                if more:
                    prepare(u + 1, i, 1 - p)
                if not first:
                    normalise(u - 1)
                v.wait_ge(pb_used, LEAD + 2 * u + 2)
                v.tensor_copy(oT[:], bank[:, 7, :]).then_inc(oT_ready, 1)

            sweep(v, prepare, step)
            normalise(UNITS - 1)
            v.wait_ge(bias_added, 2)
            for b in range(NB):
                v.wait_ge(proj_ready, b + 1)
                v.tensor_tensor(XA[:, b * TT:b * TT + TT, :], core.tiles(4 + b), XB[:, b * TT:b * TT + TT, :],
                                ALU.add).then_inc(xa_ready, 1)
            v.wait_ge(xa_ready, NB)
            norm_vector(v, ln_2, XA, UN)
            v.wait_ge(xa_added, NB)
            with v.Fori(0, NB // 2) as i:
                for p in range(2):
                    b = i * 2 + p
                    v.wait_ge(ffn_ready, LEAD + b + 1)
                    v.tensor_tensor(X[:, bass.ds(b * TT, TT), :], X[:, bass.ds(b * TT, TT), :], core.tiles(p),
                                    ALU.add).then_inc(x_done, 1)
            v.wait_ge(x_done, LEAD + NB)

        @block.tensor
        def _(pe):
            pe.wait_ge(w_in, 16 * W_LOADS)
            pe.wait_ge(low_set, 4)
            for b in range(NB):
                pe.wait_ge(ln_1.normed, b * TT + TT)
                for t in range(TT):
                    tr = pe.transpose(core.tiles(b)[:, t, :], UN[:, b * TT + t, :], core.ident[:])
                tr.then_inc(un_turned, 1)
            for b in range(NB):
                pe.wait_ge(uT_ready, LEAD + b + 1)
                pe.wait_ge(qk_ready, LEAD + 2 * b)
                pe.matmul(bank[:, 4, :], wqkv[:, 0:D], uT[b % 2][:], start=True, stop=True).then_inc(q_ready, 1)
                pe.matmul(bank[:, 5, :], wqkv[:, D:2 * D], uT[b % 2][:], start=True, stop=True).then_inc(k_ready, 1)
                pe.wait_ge(v_kept, LEAD + b)
                for t in range(TT):
                    mm = pe.matmul(core.tiles(6)[:, t, :], uT[b % 2][:, t * P:t * P + P], wqkv[:, 2 * D:],
                                   start=True, stop=True)
                mm.then_inc(v_ready, 1)
                for x in range(2):
                    pe.wait_ge(sin_ready, LEAD + 2 * b + x - 1)
                    pe.wait_ge(qk_ready, LEAD + 2 * b + x + 1)
                    pe.matmul(bank[:, ROT[x], :], rot[:], qk[:, x, :], start=True, stop=True).then_inc(rot_ready, 1)

            pe.wait_ge(uT_ready, LEAD + NB)
            pe.wait_ge(qk_ready, LEAD + 2 * NB)
            pe.wait_ge(sin_ready, LEAD + 2 * NB)
            pe.wait_ge(v_kept, LEAD + NB)

            def peaks(u, p, turns):
                for n in turns:
                    qt, js = PEAKS[n]
                    if n == 0:
                        pe.wait_ge(a_ready, LEAD + u - 2)
                    elif n == 1:
                        pe.wait_ge(low_ready, LEAD + u)
                    else:
                        pe.wait_ge(peak_read, LEAD + NP * u + n - 1)
                    w = (qt + 1) * P
                    for i, j in enumerate(js):
                        r = slice(64 * (j // 2), 64 * (j // 2) + ROWS)
                        o = bank[:, n % 2, i * w:i * w + w]
                        pe.matmul(o, QS[p][r, j % 2, qt * P:qt * P + P], KS[p][r, j % 2, 0:w],
                                  start=True, stop=False, skip_group_check=True)
                        mm = pe.matmul(o[:, qt * P:], identb[:], hide_k[:], start=False, stop=True, skip_group_check=True)
                    mm.then_inc(peak_scored, 1)

            def turn_peaks(u, p):
                pe.wait_ge(peak_whole, LEAD + u + 1)
                apart(pe, core)
                for t in range(TT):
                    mm = pe.transpose(bank[0:MID + 4, 1, t * P:t * P + P], peak[p][:, t, :], core.ident[:])
                mm.then_inc(peak_turned, 1)

            def prepare(u, i, p):
                pe.wait_ge(unit_in[p], 64 * (i + 1))
                peaks(u, p, range(NP))
                turn_peaks(u, p)

            def scores(u, p, j):
                r = slice(64 * (j // 2), 64 * (j // 2) + ROWS)
                first = 2 + 2 * (j % 2)
                pe.wait_ge(pa_ready, LEAD + 4 * u + j - 1)
                for kt, o in ((0, bank[:, first, :]), (1, bank[:, first + 1, 0:3 * P]), (3, bank[:, first + 1, 3 * P:])):
                    pe.matmul(o, KS[p][r, j % 2, kt * P:kt * P + P], QS[p][r, j % 2, kt * P:],
                              start=True, stop=False, skip_group_check=True)
                    pe.matmul(o, spread[:, j, :], low[p][:, kt * P:], start=False, stop=False, skip_group_check=True)
                    mm = pe.matmul(o[:, 0:P], identb[:], hide_q[:], start=False, stop=True, skip_group_check=True)
                mm.then_inc(sa_ready, 1)
                if j % 2 == 0:
                    pe.wait_ge(pb_ready, LEAD + 2 * u + j // 2)
                o = bank[:, 6, 2 * P * (j % 2):2 * P * (j % 2) + 2 * P]
                pe.matmul(o, KS[p][r, j % 2, 2 * P:3 * P], QS[p][r, j % 2, 2 * P:], start=True, stop=False,
                          skip_group_check=True)
                pe.matmul(o, spread[:, j, :], low[p][:, 2 * P:], start=False, stop=False, skip_group_check=True)
                mm = pe.matmul(o[:, 0:P], identb[:], hide_q[:], start=False, stop=True, skip_group_check=True)
                if j % 2:
                    mm.then_inc(sb_ready, 1)

            def outputs(u, p, j, tiles):
                if 0 in tiles:
                    pe.wait_ge(pa_ready, LEAD + 4 * u + j + 1)
                for kt in tiles:
                    at_col = (0, T, None, T + 3 * P)[kt]
                    mm = pe.matmul(bank[32 * j:32 * j + 32, 7, kt * P:], va[p][:, kt, j, :],
                                   pa[:, j % 2, at_col:at_col + T - kt * P], start=(kt == 0), stop=False,
                                   skip_group_check=True)
                if 3 in tiles:
                    mm.then_inc(pa_used, 1)

            def last_outputs(u, p, s):
                pe.wait_ge(pb_ready, LEAD + 2 * u + s + 1)
                for a in range(2):
                    j = 2 * s + a
                    mm = pe.matmul(bank[32 * j:32 * j + 32, 7, 2 * P:], va[p][:, 2, j, :],
                                   pb[:, s, 2 * P * a:2 * P * a + 2 * P], start=False, stop=True, skip_group_check=True)
                mm.then_inc(pb_used, 1)

            def turn_output(u):
                pe.wait_ge(oT_ready, LEAD + u + 1)
                for t in range(TT):
                    mm = pe.transpose(core.tiles(0)[:, t, :], oT[:, t * P:t * P + P], core.ident[:])
                mm.then_inc(oT_turned, 1)

            def step(u, i, p, more, first=False):
                pe.wait_ge(low_ready, LEAD + u + 1)
                pe.wait_ge(va_ready, LEAD + u + 1)
                if more:
                    pe.wait_ge(unit_in[1 - p], 64 * (i + 1 + p))

                def peak_turns(k):
                    if more:
                        peaks(u + 1, 1 - p, range(2 * k, 2 * k + 2))

                peak_turns(0)
                scores(u, p, 0)
                peak_turns(1)
                scores(u, p, 1)
                peak_turns(2)
                pe.wait_ge(oT_ready, LEAD + u)
                outputs(u, p, 0, (0,))
                peak_turns(3)
                outputs(u, p, 0, (1, 3))
                peak_turns(4)
                scores(u, p, 2)
                outputs(u, p, 1, (0,))
                peak_turns(5)
                outputs(u, p, 1, (1, 3))
                scores(u, p, 3)
                last_outputs(u, p, 0)
                if more:
                    turn_peaks(u + 1, 1 - p)
                if not first:
                    turn_output(u - 1)
                outputs(u, p, 2, (0, 1, 3))
                outputs(u, p, 3, (0, 1, 3))
                last_outputs(u, p, 1)

            sweep(pe, prepare, step)
            turn_output(UNITS - 1)
            pe.wait_ge(a_ready, LEAD + UNITS)
            for b in range(NB):
                for t in range(TT):
                    tr = pe.transpose(core.tiles(b)[:, t, :], A[:, b * TT + t, :], core.ident[:])
                tr.then_inc(at_turned, 1)
            for b in range(NB):
                pe.wait_ge(aT_ready, b + 1)
                for t in range(TT):
                    mm = pe.matmul(core.tiles(4 + b)[:, t, :], aT[b % 2][:, t * P:t * P + P], wo[:], start=True, stop=True)
                mm.then_inc(proj_ready, 1)
            for b in range(NB):
                pe.wait_ge(ln_2.normed, b * TT + TT)
                for t in range(TT):
                    tr = pe.transpose(core.tiles(b)[:, t, :], UN[:, b * TT + t, :], core.ident[:])
                tr.then_inc(xa_turned, 1)
            pe.wait_ge(xaT_ready, LEAD + NB)

            def hidden(b):
                for f in range(FB):
                    pe.wait_ge(h1_gelu, LEAD + FB * b + f - FB + 1)
                    pe.matmul(bank[:, 4 + f, :], w1[:, f * P:f * P + P], row(UT, b),
                              start=True, stop=True).then_inc(h1_ready, 1)

            def feed_forward(b, p):
                pe.wait_ge(h1_gelu, LEAD + FB * b + FB)
                pe.wait_ge(x_done, LEAD + b - 1)
                for t in range(TT):
                    for f in range(FB):
                        mm = pe.matmul(core.tiles(p)[:, t, :], hT[p][:, f, t * P:t * P + P], w2[:, f, :],
                                       start=(f == 0), stop=(f == FB - 1))
                mm.then_inc(ffn_ready, 1)

            hidden(0)
            hidden(1)
            feed_forward(0, 0)
            with pe.Fori(1, NB // 2) as i:
                for p in range(2):
                    hidden(i * 2 + p)
                    feed_forward(i * 2 + p - 1, 1 - p)
            feed_forward(NB - 1, 1)


def build(nc, io, out):
    with ExitStack() as ctx:
        core = Core(nc, ctx, io)
        mamba(core)
        moe(core, 1)
        attention(core)
        moe(core, 2)
        stored = core.sem("stored")
        with nc.Block() as block:
            @block.sync
            def _(sp):
                sp.dma_start(out.rearrange("b (t p) d -> p (b t) d", p=P), core.X[:]).then_inc(stored, 16)
                sp.wait_ge(stored, 16)


def constants():
    bf16 = mybir.dt.np(BF16)
    line = lambda x: np.ascontiguousarray(x, dtype=np.float32).reshape(-1)
    grid = np.zeros((NE, NT))
    inverse = (np.float32(1.0) / np.float32(10000.0) ** (np.arange(0, HD, 2, dtype=np.float32) / np.float32(HD))).astype(np.float32)
    angle = np.tile(np.arange(T, dtype=np.float32)[None, :] * np.tile(inverse, 2)[:, None], (NH, 1))
    swap = np.zeros((HD, HD), np.float32)
    for d in range(HD // 2):
        swap[d + HD // 2, d] = -1.0
        swap[d, d + HD // 2] = 1.0
    later = np.triu(np.full((P, P), FAR, np.float32), 1)
    eye = np.eye(P, dtype=np.float32)
    spread = np.zeros((P, 4, P), np.float32)
    for j in range(4):
        spread[[j, 32 + j], j, :] = 1.0
    return dict(cos=np.cos(angle), sin=np.sin(angle), rot=np.kron(np.eye(NH, dtype=np.float32), swap),
                hide_k=later.astype(bf16), hide_q=later.T.astype(bf16),
                spread=spread.astype(bf16), ident=eye, identb=eye.astype(bf16),
                pick=np.tile(np.eye(32, dtype=np.float32), (3, 1)),
                iota_e=line(grid + np.arange(NE)[:, None]), thresh=line(grid + P * np.arange(NT)),
                reset=line(grid + (np.arange(NT) > 0)),
                iota_j=line(np.zeros((SLOT_TILES, NE)) + np.arange(SLOT_TILES)[:, None]),
                below=np.triu(np.ones((P, P)), 1).astype(bf16),
                onesb=np.ones((P, P), bf16))


def layout(i):
    a = {k: np.asarray(v) for k, v in i.items()}
    A, B, E = "L0_attn_a_", "L0_attn_b_", "L0_ffn_"
    col = lambda x: x.reshape(-1, P).T
    return dict(
        x=a[A + "x"], in_proj_t=a[A + "in_proj_w"].T, conv_w=a[A + "conv_w"],
        vec_a=np.stack([a[A + n] for n in ("ln1_g", "ln1_b", "conv_b", "dt_proj_b", "D_param", "ln2_g", "ln2_b")], 1),
        x_proj_t=a[A + "x_proj_w"].T, dt_proj_t=a[A + "dt_proj_w"].T, a_log=a[A + "A_log"],
        out_proj_t=a[A + "out_proj_w"].T, a_w1_t=a[A + "w1"].T, a_b1_t=col(a[A + "b1"]),
        a_w2_t=a[A + "w2"].T, a_b2=a[A + "b2"],
        vec_b=np.stack([a[B + n] for n in ("ln1_g", "ln1_b", "ln2_g", "ln2_b")] +
                       [a[B + "bqkv"][0:D], a[B + "bqkv"][D:2 * D]], 1),
        wqkv=a[B + "Wqkv"], bv=a[B + "bqkv"][2 * D:], wo=a[B + "Wo"], bo=a[B + "bo"],
        b_w1=a[B + "W1"], b_b1_t=col(a[B + "b1"]), b_w2=a[B + "W2"], b_b2=a[B + "b2"],
        gate_w=a[E + "gate_w"], gate_b=a[E + "gate_b"], e_w1=a[E + "w1"], e_w2=a[E + "w2"],
        e_b1_t=a[E + "b1"].reshape(NE * FB, P).T, e_b2=a[E + "b2"].reshape(-1),
    )


def kernel(**inputs):
    import concourse.bacc as _bacc
    from concourse.bass_utils import run_bass_kernel_spmd as _run

    nc = _bacc.Bacc("TRN2", target_bir_lowering=False, num_devices=1)
    arrays = {k: np.ascontiguousarray(v) for k, v in {**layout(inputs), **constants()}.items()}
    io = {k: nc.dram_tensor(f"in_{k}", v.shape, mybir.dt.from_np(v.dtype), kind="ExternalInput").ap()
          for k, v in arrays.items()}
    out = nc.dram_tensor("out_x", (NB, T, D), F32, kind="ExternalOutput").ap()
    build(nc, io, out)
    r = _run(nc, [{f"in_{k}": v for k, v in arrays.items()}], core_ids=[0])
    return r.results[0]["out_x"]
```

```python
from contextlib import ExitStack

import numpy as np

import concourse.bass as bass
from concourse import mybir

P = 128
D = 128
NB = 4
T = 512
TT = T // P
NT = NB * TT
NS = 16
NCONV = 8
RANK = 8
FF = 512
FB = FF // P
NE = 24
TOPK = 2
SLOT_TILES = (NB * T * TOPK - NE) // P + NE
SLOT_TILES += SLOT_TILES % 2
NH = 16
HD = 8
EPS = 1e-5
LOAD_EXPERTS = 4
LEAD = 4
FAR = -1.0e30

F32 = mybir.dt.float32
BF16 = mybir.dt.bfloat16
I32 = mybir.dt.int32
U32 = mybir.dt.uint32
ACT = mybir.ActivationFunctionType
ALU = mybir.AluOpType
AX_X = mybir.AxisListType.X



class Core:

    def __init__(self, nc, ctx, io, out):
        self.nc, self.ctx, self.io, self.out = nc, ctx, io, out
        self.retired = []
        self.bank = ctx.enter_context(nc.psum_tensor("bank", [P, 8, T], F32))
        self.X = self.sb("X", [P, NT, D])
        self.XN = self.sb("XN", [P, NT, D])
        self.UN = self.sb("UN", [P, NT, D])
        self.ident = self.sb("ident", [P, P])
        self.half = self.sb("half", [P, NT])
        self.ones_row = self.sb("ones_row", [1, P])
        self.w1all = self.sb("w1all", [P, NE, FF])
        self.w2all = self.sb("w2all", [P, NE, FB, D])
        self.experts_in = self.sem("experts_in")
        self.rows = nc.dram_tensor("rows", (NT * P, D), F32).ap()
        self.results = nc.dram_tensor("results", ((TOPK * NT + SLOT_TILES) * P, D), F32).ap()
        self.consts_in = self.sem("consts_in")
        self.slot_in = [self.sem(f"slot_in{q}") for q in range(4)]
        self.y_out = [self.sem(f"y_out{q}") for q in range(4)]
        self.consts_set = self.sem("consts_set")
        self.apart = self.sem("apart")

    def sb(self, name, shape, dt=F32, ctx=None):
        return (ctx or self.ctx).enter_context(self.nc.sbuf_tensor(name, shape, dt))

    def sem(self, name, ctx=None):
        return (ctx or self.ctx).enter_context(self.nc.semaphore(name))

    def tiles(self, k):
        return self.bank[:, k, :].rearrange("p (t n) -> p t n", n=P)


class Stage:

    def __init__(self, core, tag):
        self.core, self.tag, self.ctx = core, tag, ExitStack()
        self.leading, self.sems = [], []

    def sb(self, name, shape, dt=F32):
        return self.core.sb(f"{self.tag}_{name}", shape, dt, self.ctx)

    def sem(self, name):
        s = self.core.sem(f"{self.tag}_{name}", self.ctx)
        self.sems.append(s)
        return s

    def lead(self, name):
        s = self.sem(name)
        self.leading.append(s)
        return s

    def set_leads(self, g):
        for s in self.leading:
            g.sem_inc(s, LEAD)
        numbers = sorted(s.num for s in self.core.retired)
        while numbers:
            n = 1
            while n < len(numbers) and numbers[n] == numbers[0] + n:
                n += 1
            g.sem_clear(range(numbers[0], numbers[0] + n))
            numbers = numbers[n:]
        self.core.retired = self.sems


class Norm:

    def __init__(self, st, name):
        self.stats = st.sb(name + "_stats", [P, NT, 6])
        self.mv = st.sb(name + "_mv", [P, NT, 2])
        self.ve = st.sb(name + "_ve", [P, NT])
        self.rs = st.sb(name + "_rs", [P, NT])
        self.negmean = st.sb(name + "_negmean", [P, NT])
        self.shift = st.sb(name + "_shift", [P, NT])
        self.stats_done = st.sem(name + "_stats_done")
        self.mean_var_ready = st.sem(name + "_mean_var_ready")
        self.var_eps_ready = st.sem(name + "_var_eps_ready")
        self.rstd_ready = st.sem(name + "_rstd_ready")
        self.shift_ready = st.sem(name + "_shift_ready")
        self.normed = st.sem(name + "_normed")


def apart(eng, core):
    eng.sem_inc(core.apart, 1)


def norm_stats(v, ln, src, b):
    tiles = range(b * TT, b * TT + TT)
    for i in tiles:
        v.bn_stats(ln.stats[:, i, :], src[:, i, :]).then_inc(ln.stats_done, 1)
    v.wait_ge(ln.stats_done, b * TT + TT)
    for i in tiles:
        v.bn_aggr(ln.mv[:, i, :], ln.stats[:, i, :]).then_inc(ln.mean_var_ready, 1)


def norm_apply(v, ln, src, dst, b):
    v.wait_ge(ln.mean_var_ready, b * TT + TT)
    v.wait_ge(ln.rstd_ready, b + 1)
    for i in range(b * TT, b * TT + TT):
        v.tensor_scalar(dst[:, i, :], src[:, i, :], ln.mv[:, i, 0:1], ln.rs[:, i:i + 1],
                        ALU.subtract, ALU.mult).then_inc(ln.normed, 1)


def norm_scalar(act, ln, src, dst, b):
    act.wait_ge(ln.shift_ready, b + 1)
    for i in range(b * TT, b * TT + TT):
        act.activation(dst[:, i, :], src[:, i, :], ACT.Identity, bias=ln.shift[:, i:i + 1],
                       scale=ln.rs[:, i:i + 1]).then_inc(ln.normed, 1)


def norm_pool(g, core, ln, b):
    c = slice(b * TT, b * TT + TT)
    g.wait_ge(ln.mean_var_ready, b * TT + TT)
    g.tensor_scalar(ln.ve[:, c], ln.mv[:, c, 1], EPS, None, ALU.add).then_inc(ln.var_eps_ready, 1)
    g.tensor_scalar(ln.negmean[:, c], ln.mv[:, c, 0], -1.0, None, ALU.mult).then_inc(ln.var_eps_ready, 1)
    g.wait_ge(ln.var_eps_ready, 2 * b + 2)
    g.tensor_tensor(ln.rs[:, c], ln.ve[:, c], core.half[:, c], ALU.pow).then_inc(ln.rstd_ready, 1)
    g.wait_ge(ln.rstd_ready, b + 1)
    g.tensor_tensor(ln.shift[:, c], ln.negmean[:, c], ln.rs[:, c], ALU.mult).then_inc(ln.shift_ready, 1)


def row(x, i):
    return x[:, bass.ds(i, 1), :].rearrange("p a n -> p (a n)")


def mamba(core):
    nc, io, bank, X = core.nc, core.io, core.bank, core.X
    st = Stage(core, "m")
    win = st.sb("win", [P, 2 * D])
    convw = st.sb("convw", [P, NCONV])
    vec = st.sb("vec", [P, 7])
    LN1G, LN1B, CONVB, DTB, DSKIP, LN2G, LN2B = range(7)
    wx = st.sb("wx", [P, RANK + 96])
    wdt = st.sb("wdt", [RANK, P])
    a_neg = st.sb("a_neg", [P, NS])
    wout = st.sb("wout", [P, D])
    w1 = st.sb("w1", [P, FF])
    b1 = st.sb("b1", [P, FB])
    w2 = st.sb("w2", [P, FB, D])
    b2 = st.sb("b2", [P, D])
    taps = st.sb("taps", [P, NCONV, P])
    dskip = st.sb("dskip", [P, P])
    pick_s = st.sb("pick_s", [96, 32])
    pick = st.sb("pick", [96, 32, P], BF16)

    X1 = core.XN
    xpad = st.sb("xpad", [P, NCONV - 1 + T])
    XC = st.sb("XC", [P, NB, T])
    SZ = st.sb("SZ", [P, NB, T])
    DELTA = st.sb("DELTA", [P, NB, T])
    DX = st.sb("DX", [P, NB, T])
    BC = st.sb("BC", [96, NB, T], BF16)
    dt_sb = st.sb("dt_sb", [RANK, T])
    rest = st.sb("rest", [96, T])
    mid = st.sb("mid", [96, T], BF16)
    work = st.sb("work", [P, 8, T])
    token_major = lambda x: x.rearrange("p b (t d) -> p (b t) d", d=D)
    UN, UT = token_major(work[:, 0:NB, :]), work[:, NB:2 * NB, :]
    EXPV, RELU = work[:, 0:NB, :], work[:, NB:2 * NB, :]
    hc = core.UN[:].rearrange("p (b t) d -> p b (t d)", t=TT)
    decay, h, c_sb, dbx = (work[:, 2 * i:2 * i + 2, :] for i in range(4))
    YZ = work[:, 0:NB, :]
    hT = [work[:, FB * p:FB * p + FB, :] for p in range(2)]
    XA, UN2, UT2 = token_major(DELTA[:]), token_major(DX[:]), XC

    w_in, vec_in, alog_in, pick_in = map(st.sem, ("w_in", "vec_in", "alog_in", "pick_in"))
    x_in = [st.sem(f"x_in{b}") for b in range(NB)]
    edge_set = st.sem("edge_set")
    a_exp, a_ready = st.sem("a_exp"), st.sem("a_ready")
    taps_ready, pick_ready = st.sem("taps_ready"), st.sem("pick_ready")
    ln_x, ln_1, ln_2, ln_next = (Norm(st, n) for n in ("ln_x", "ln_1", "ln_2", "ln_next"))
    un_turned, uT_ready, xin_ready, z_ready = map(st.sem, ("un_turned", "uT_ready", "xin_ready", "z_ready"))
    xpad_ready, sz_ready, conv_ready, xc_ready = map(st.lead, ("xpad_ready", "sz_ready", "conv_ready", "xc_ready"))
    dt_ready, dt_copied, bc_ready, bc_split = map(st.lead, ("dt_ready", "dt_copied", "bc_ready", "bc_split"))
    split_step = st.sem("split_step")
    dpre_ready, abs_ready, exp_ready, relu_ready = map(st.lead, ("dpre_ready", "abs_ready", "exp_ready", "relu_ready"))
    onep_ready, lnv_ready, delta_step, dx_ready = map(st.sem, ("onep_ready", "lnv_ready", "delta_step", "dx_ready"))
    b_ready, c_ready, decay_ready, dbx_ready = map(st.lead, ("b_ready", "c_ready", "decay_ready", "dbx_ready"))
    h_ready, c_copied, hc_ready, hc_summed = map(st.lead, ("h_ready", "c_copied", "hc_ready", "hc_summed"))
    y_ready = st.sem("y_ready")
    yz_ready, proj_ready, xa_ready, xa_added = map(st.sem, ("yz_ready", "proj_ready", "xa_ready", "xa_added"))
    xa_turned, xaT_ready, h1_ready, h1_relu = map(st.lead, ("xa_turned", "xaT_ready", "h1_ready", "h1_relu"))
    ffn_ready, x_done, b2_added = st.lead("ffn_ready"), st.lead("x_done"), st.sem("b2_added")

    with st.ctx, nc.Block() as block:
        W_LOADS = 11

        @block.sync
        def _(sp):
            for b in range(NB):
                sp.dma_start(X[:, b * TT:b * TT + TT, :], io["x"][b].rearrange("(t p) d -> p t d", p=P)).then_inc(x_in[b], 16)
            sp.dma_start(core.ident[:], io["ident"]).then_inc(core.consts_in, 16)
            sp.dma_start(pick_s[:], io["pick"]).then_inc(pick_in, 16)
            sp.dma_start(a_neg[:], io["a_log"]).then_inc(alog_in, 16)
            sp.dma_start(win[:], io["in_proj_t"]).then_inc(w_in, 16)
            sp.dma_start(convw[:], io["conv_w"]).then_inc(vec_in, 16)
            sp.dma_start(vec[:], io["vec_a"]).then_inc(vec_in, 16)
            sp.dma_start(wx[:, 0:RANK], io["x_proj_t"][:, 0:RANK]).then_inc(w_in, 16)
            for r in range(3):
                sp.dma_start(wx[:, RANK + 32 * r:RANK + 32 * r + 32],
                             io["x_proj_t"][:, RANK:RANK + 32]).then_inc(w_in, 16)
            sp.dma_start(wdt[:], io["dt_proj_t"]).then_inc(w_in, 16)
            sp.dma_start(wout[:], io["out_proj_t"]).then_inc(w_in, 16)
            sp.dma_start(w1[:], io["a_w1_t"]).then_inc(w_in, 16)
            sp.dma_start(b1[:], io["a_b1_t"]).then_inc(w_in, 16)
            sp.dma_start(w2[:], io["a_w2_t"].rearrange("(f p) n -> p f n", p=P)).then_inc(w_in, 16)
            sp.dma_start(b2[:], io["a_b2"].partition_broadcast(P)).then_inc(w_in, 16)
            for e in range(0, NE, LOAD_EXPERTS):
                sp.dma_start(core.w1all[:, e:e + LOAD_EXPERTS, :],
                             io["e_w1"][e:e + LOAD_EXPERTS].rearrange("e d f -> d e f")).then_inc(core.experts_in, 16)
                sp.dma_start(core.w2all[:, e:e + LOAD_EXPERTS, :, :].rearrange("p e k n -> p (e k) n"),
                             io["e_w2"][e:e + LOAD_EXPERTS].rearrange("e (k p) n -> p (e k) n", p=P))\
                    .then_inc(core.experts_in, 16)

        @block.gpsimd
        def _(g):
            st.set_leads(g)
            g.memset(core.half[:], -0.5).then_inc(core.consts_set, 1)
            g.memset(core.ones_row[:], 1.0).then_inc(core.consts_set, 1)
            g.memset(xpad[:, 0:NCONV - 1], 0.0).then_inc(edge_set, 1)
            g.wait_ge(core.consts_set, 2)
            for ln in (ln_x, ln_1):
                for b in range(NB):
                    norm_pool(g, core, ln, b)
            g.wait_ge(ln_x.normed, NT)
            g.wait_ge(w_in, 16 * W_LOADS)
            g.tensor_tensor(X[:], X[:], b2[:].unsqueeze(1).to_broadcast([P, NT, D]), ALU.add).then_inc(b2_added, 1)

            with g.Fori(0, NS) as n:
                for b in range(NB):
                    k = n * NB + b
                    g.wait_ge(h_ready, LEAD + k + 1)
                    g.wait_ge(c_copied, LEAD + k + 1)
                    g.wait_ge(hc_summed, LEAD + k - 3)
                    g.tensor_tensor(hc[:, b, :], h[:, b % 2, :], c_sb[:, b % 2, :],
                                    ALU.mult).then_inc(hc_ready, 1)
            for b in range(NB):
                norm_pool(g, core, ln_2, b)
            g.wait_ge(b2_added, 1)
            for b in range(NB):
                g.tensor_tensor(X[:, b * TT:b * TT + TT, :], X[:, b * TT:b * TT + TT, :],
                                XA[:, b * TT:b * TT + TT, :], ALU.add).then_inc(xa_added, 1)
            for b in range(NB):
                norm_pool(g, core, ln_next, b)

        @block.scalar
        def _(act):
            for b in range(NB):
                norm_scalar(act, ln_x, X, X1, b)
            act.wait_ge(vec_in, 32)
            act.wait_ge(w_in, 16 * W_LOADS)
            act.wait_ge(edge_set, 1)
            def turned(b):
                act.wait_ge(un_turned, b + 1)
                act.activation(UT[:, b, :], bank[:, b, :], ACT.Identity, bias=vec[:, LN1B:LN1B + 1],
                               scale=vec[:, LN1G:LN1G + 1]).then_inc(uT_ready, 1)

            def projected(b):
                act.wait_ge(xin_ready, b + 1)
                if b >= 1:
                    act.wait_ge(conv_ready, LEAD + b)
                act.activation(xpad[:, NCONV - 1:], bank[:, 4, :], ACT.Identity).then_inc(xpad_ready, 1)
                act.wait_ge(z_ready, b + 1)
                act.activation(SZ[:, b, :], bank[:, 5, :], ACT.Silu).then_inc(sz_ready, 1)

            def convolved(b):
                act.wait_ge(conv_ready, LEAD + b + 1)
                act.activation(XC[:, b, :], bank[:, 0, :], ACT.Silu,
                               bias=vec[:, CONVB:CONVB + 1]).then_inc(xc_ready, 1)

            def time_step(b):
                act.wait_ge(dpre_ready, LEAD + b + 1)
                act.activation(EXPV[:, b, :], bank[:, 6, :], ACT.Abs, bias=vec[:, DTB:DTB + 1]).then_inc(abs_ready, 1)

            turned(0)
            projected(0)
            turned(1)
            turned(2)
            convolved(0)
            turned(3)
            for b in range(1, NB):
                projected(b)
                time_step(b - 1)
                convolved(b)
            time_step(NB - 1)
            act.preload_act_table(ACT.Exp)
            act.wait_ge(alog_in, 16)
            act.activation(a_neg[:], a_neg[:], ACT.Exp).then_inc(a_exp, 1)
            act.wait_ge(abs_ready, LEAD + NB)
            act.activation(EXPV, EXPV, ACT.Exp, scale=-1.0).then_inc(exp_ready, 1)
            act.preload_act_table(ACT.Ln)
            act.wait_ge(onep_ready, 1)
            act.activation(DELTA[:], DX[:], ACT.Ln).then_inc(lnv_ready, 1)
            act.preload_act_table(ACT.Exp)
            act.wait_ge(a_ready, 1)
            act.wait_ge(dx_ready, 1)
            with act.Fori(0, NS) as n:
                for b in range(NB):
                    k = n * NB + b
                    act.wait_ge(h_ready, LEAD + k - 1)
                    apart(act, core)
                    act.activation(decay[:, b % 2, :], DELTA[:, b, :], ACT.Exp,
                                   scale=a_neg[:, bass.ds(n, 1)]).then_inc(decay_ready, 1)
                    act.wait_ge(c_ready, LEAD + k + 1)
                    act.wait_ge(hc_ready, LEAD + k - 1)
                    act.activation(c_sb[:, b % 2, :], bank[:, 6 + b % 2, :], ACT.Identity).then_inc(c_copied, 1)
            for b in range(NB):
                norm_scalar(act, ln_2, XA, UN2, b)
            for b in range(NB):
                act.wait_ge(xa_turned, LEAD + b + 1)
                act.activation(UT2[:, b, :], bank[:, b, :], ACT.Identity, bias=vec[:, LN2B:LN2B + 1],
                               scale=vec[:, LN2G:LN2G + 1]).then_inc(xaT_ready, 1)
            act.wait_ge(proj_ready, NB)
            with act.Fori(0, NB // 2) as i:
                for p in range(2):
                    b = i * 2 + p
                    act.wait_ge(ffn_ready, LEAD + b - 1)
                    for f in range(FB):
                        act.wait_ge(h1_ready, LEAD + FB * b + f + 1)
                        act.activation(hT[p][:, f, :], bank[:, 4 + f, :], ACT.Relu,
                                       bias=b1[:, f:f + 1]).then_inc(h1_relu, 1)

        @block.vector
        def _(v):
            for b in range(NB):
                v.wait_ge(x_in[b], 16)
                norm_stats(v, ln_x, X, b)
            v.wait_ge(core.consts_in, 16)
            v.wait_ge(vec_in, 32)
            for j in range(NCONV):
                v.tensor_scalar(taps[:, j, :], core.ident[:], convw[:, j:j + 1], None, ALU.mult).then_inc(taps_ready, 1)
            v.tensor_scalar(dskip[:], core.ident[:], vec[:, DSKIP:DSKIP + 1], None, ALU.mult).then_inc(taps_ready, 1)
            for b in range(NB):
                v.wait_ge(ln_x.normed, b * TT + TT)
                norm_stats(v, ln_1, X1, b)
                if b >= 1:
                    norm_apply(v, ln_1, X1, UN, b - 1)
            norm_apply(v, ln_1, X1, UN, NB - 1)

            def split(b):
                v.wait_ge(dt_ready, LEAD + b + 1)
                v.tensor_copy(dt_sb[:], bank[0:RANK, 2, :]).then_inc(dt_copied, 1)
                v.wait_ge(bc_ready, LEAD + b + 1)
                v.tensor_copy(BC[:, b, :], bank[0:96, 3, :]).then_inc(split_step, 1)
                v.wait_ge(split_step, b * 3 + 1)
                v.tensor_tensor(rest[:], bank[0:96, 3, :], BC[:, b, :], ALU.subtract).then_inc(split_step, 1)
                v.wait_ge(split_step, b * 3 + 2)
                v.tensor_copy(mid[:], rest[:]).then_inc(split_step, 1)
                v.wait_ge(split_step, b * 3 + 3)
                v.tensor_copy(BC[32:64, b, :], mid[32:64, :])
                v.tensor_tensor(BC[64:96, b, :], rest[64:96, :], mid[64:96, :], ALU.subtract).then_inc(bc_split, 1)
                v.wait_ge(dpre_ready, LEAD + b + 1)
                v.wait_ge(abs_ready, LEAD + b + 1)
                v.tensor_scalar(RELU[:, b, :], bank[:, 6, :], vec[:, DTB:DTB + 1], 0.0,
                                ALU.add, ALU.max).then_inc(relu_ready, 1)

            v.wait_ge(pick_in, 16)
            v.tensor_copy(pick[:], pick_s[:].unsqueeze(2).to_broadcast([96, 32, P])).then_inc(pick_ready, 1)
            for b in range(NB):
                split(b)
            v.wait_ge(a_exp, 1)
            v.tensor_scalar(a_neg[:], a_neg[:], -1.0, None, ALU.mult).then_inc(a_ready, 1)
            v.wait_ge(exp_ready, LEAD + 1)
            v.tensor_scalar(DX[:], EXPV, 1.0, None, ALU.add).then_inc(onep_ready, 1)
            v.wait_ge(onep_ready, 1)
            v.scalar_tensor_tensor(out=EXPV, in0=DX[:], scalar=1.0, in1=EXPV,
                                   op0=ALU.subtract, op1=ALU.subtract).then_inc(delta_step, 1)
            v.wait_ge(delta_step, 1)
            v.wait_ge(relu_ready, LEAD + NB)
            v.tensor_tensor(RELU, RELU, EXPV, ALU.subtract).then_inc(delta_step, 1)
            v.wait_ge(delta_step, 2)
            v.wait_ge(lnv_ready, 1)
            v.tensor_tensor(DELTA[:], DELTA[:], RELU, ALU.add).then_inc(delta_step, 1)
            v.wait_ge(delta_step, 3)
            v.wait_ge(xc_ready, LEAD + NB)
            v.tensor_tensor(DX[:], DELTA[:], XC[:], ALU.mult).then_inc(dx_ready, 1)
            v.wait_ge(dx_ready, 1)

            def drive(k, b):
                v.wait_ge(b_ready, LEAD + k + 1)
                v.wait_ge(h_ready, LEAD + k - 1)
                v.tensor_tensor(dbx[:, b % 2, :], bank[:, 4 + b % 2, :], DX[:, b, :], ALU.mult).then_inc(dbx_ready, 1)

            def scan(k, b):
                v.wait_ge(dbx_ready, LEAD + k + 1)
                v.wait_ge(decay_ready, LEAD + k + 1)
                v.wait_ge(hc_ready, LEAD + k - 1)
                v.tensor_tensor_scan(h[:, b % 2, :], decay[:, b % 2, :], dbx[:, b % 2, :],
                                     0.0, ALU.mult, ALU.add).then_inc(h_ready, 1)

            drive(0, 0)
            with v.Fori(0, NS - 1) as n:
                for b in range(NB):
                    drive(n * NB + b + 1, (b + 1) % NB)
                    scan(n * NB + b, b)
            for b in range(NB):
                if b < NB - 1:
                    drive((NS - 1) * NB + b + 1, b + 1)
                scan((NS - 1) * NB + b, b)
            v.wait_ge(y_ready, 1)
            for b in range(NB):
                v.tensor_tensor(YZ[:, b, :], bank[:, b, :], SZ[:, b, :], ALU.mult).then_inc(yz_ready, 1)
            for b in range(NB):
                v.wait_ge(proj_ready, b + 1)
                v.tensor_tensor(XA[:, b * TT:b * TT + TT, :], core.tiles(4 + b), X1[:, b * TT:b * TT + TT, :],
                                ALU.add).then_inc(xa_ready, 1)
                v.wait_ge(xa_ready, b + 1)
                norm_stats(v, ln_2, XA, b)
            v.wait_ge(xa_added, NB)
            for b in range(NB):
                v.wait_ge(ffn_ready, LEAD + b + 1)
                v.tensor_tensor(X[:, b * TT:b * TT + TT, :], X[:, b * TT:b * TT + TT, :], core.tiles(b % 2),
                                ALU.add).then_inc(x_done, 1)
                if b >= 1:
                    norm_apply(v, ln_next, X, core.XN, b - 1)
                v.wait_ge(x_done, LEAD + b + 1)
                norm_stats(v, ln_next, X, b)
            norm_apply(v, ln_next, X, core.XN, NB - 1)
            v.wait_ge(ln_next.normed, NT)

        @block.tensor
        def _(pe):
            pe.wait_ge(w_in, 16 * W_LOADS)
            pe.wait_ge(core.consts_in, 16)
            def turn(b):
                pe.wait_ge(ln_1.normed, b * TT + TT)
                for t in range(TT):
                    tr = pe.transpose(core.tiles(b)[:, t, :], UN[:, b * TT + t, :], core.ident[:])
                tr.then_inc(un_turned, 1)

            def project(b):
                pe.wait_ge(uT_ready, b + 1)
                pe.wait_ge(xpad_ready, LEAD + b)
                pe.matmul(bank[:, 4, :], win[:, 0:D], UT[:, b, :], start=True, stop=True).then_inc(xin_ready, 1)
                pe.wait_ge(sz_ready, LEAD + b)
                pe.matmul(bank[:, 5, :], win[:, D:2 * D], UT[:, b, :], start=True, stop=True).then_inc(z_ready, 1)

            def convolve(b):
                pe.wait_ge(xpad_ready, LEAD + b + 1)
                pe.wait_ge(xc_ready, LEAD + b)
                for j in range(NCONV):
                    mm = pe.matmul(bank[:, 0, :], taps[:, j, :], xpad[:, j:j + T],
                                   start=(j == 0), stop=(j == NCONV - 1))
                mm.then_inc(conv_ready, 1)

            def select(b):
                pe.wait_ge(xc_ready, LEAD + b + 1)
                pe.wait_ge(dt_copied, LEAD + b)
                pe.matmul(bank[0:RANK, 2, :], wx[:, 0:RANK], XC[:, b, :], start=True, stop=True).then_inc(dt_ready, 1)
                pe.wait_ge(bc_split, LEAD + b)
                pe.matmul(bank[0:96, 3, :], wx[:, RANK:], XC[:, b, :], start=True, stop=True).then_inc(bc_ready, 1)

            def time_step(b):
                pe.wait_ge(dt_copied, LEAD + b + 1)
                pe.wait_ge(abs_ready, LEAD + b)
                pe.wait_ge(relu_ready, LEAD + b)
                pe.matmul(bank[:, 6, :], wdt[:], dt_sb[:], start=True, stop=True).then_inc(dpre_ready, 1)

            turn(0)
            project(0)
            turn(1)
            turn(2)
            pe.wait_ge(taps_ready, NCONV + 1)
            convolve(0)
            turn(3)
            pe.wait_ge(uT_ready, NB)
            for b in range(1, NB):
                project(b)
                select(b - 1)
                time_step(b - 1)
                convolve(b)
            select(NB - 1)
            time_step(NB - 1)
            pe.wait_ge(pick_ready, 1)
            pe.wait_ge(bc_split, LEAD + NB)
            pe.wait_ge(relu_ready, LEAD + NB)
            pe.wait_ge(abs_ready, LEAD + NB)

            for b in range(NB):
                pe.matmul(bank[:, b, :], dskip[:], XC[:, b, :], start=True, stop=False, skip_group_check=True)

            def spread_b(n, b):
                pe.wait_ge(dbx_ready, LEAD + n * NB + b - 1)
                pe.matmul(bank[:, 4 + b % 2, :], pick[:, bass.ds(n, 1), :].rearrange("p a n -> p (a n)"),
                          BC[:, b, :], start=True, stop=True).then_inc(b_ready, 1)

            def state(n, first=False, last=False):
                for b in range(NB):
                    k = n * NB + b
                    pe.wait_ge(c_copied, LEAD + k - 1)
                    pe.matmul(bank[:, 6 + b % 2, :], pick[:, bass.ds(n + NS, 1), :].rearrange("p a n -> p (a n)"),
                              BC[:, b, :], start=True, stop=True).then_inc(c_ready, 1)
                    if b < NB - 1:
                        spread_b(n, b + 1)
                    elif not last:
                        spread_b(n + 1, 0)
                    if first and b < 3:
                        continue
                    c = (b + 1) % NB
                    pe.wait_ge(hc_ready, LEAD + k - 2)
                    pe.matmul(bank[:, c, :], core.ident[:], hc[:, c, :],
                              start=False, stop=(last and b == 3), skip_group_check=True).then_inc(hc_summed, 1)

            spread_b(0, 0)
            state(0, first=True)
            with pe.Fori(1, NS - 1) as n:
                state(n)
            state(NS - 1, last=True)
            for b in range(1, NB):
                pe.wait_ge(hc_ready, LEAD + NS * NB - NB + b + 1)
                mm = pe.matmul(bank[:, b, :], core.ident[:], hc[:, b, :],
                               start=False, stop=True, skip_group_check=True)
            mm.then_inc(y_ready, 1)
            for b in range(NB):
                pe.wait_ge(yz_ready, b + 1)
                for t in range(TT):
                    mm = pe.matmul(core.tiles(4 + b)[:, t, :], YZ[:, b, t * P:t * P + P], wout[:], start=True, stop=True)
                mm.then_inc(proj_ready, 1)
            for b in range(NB):
                pe.wait_ge(ln_2.normed, b * TT + TT)
                for t in range(TT):
                    tr = pe.transpose(core.tiles(b)[:, t, :], UN2[:, b * TT + t, :], core.ident[:])
                tr.then_inc(xa_turned, 1)
            pe.wait_ge(xaT_ready, LEAD + NB)

            def hidden(b):
                for f in range(FB):
                    pe.wait_ge(h1_relu, LEAD + FB * b + f - FB + 1)
                    pe.matmul(bank[:, 4 + f, :], w1[:, f * P:f * P + P], row(UT2, b),
                              start=True, stop=True).then_inc(h1_ready, 1)

            def feed_forward(b, p):
                pe.wait_ge(h1_relu, LEAD + FB * b + FB)
                pe.wait_ge(x_done, LEAD + b - 1)
                for t in range(TT):
                    for f in range(FB):
                        mm = pe.matmul(core.tiles(p)[:, t, :], hT[p][:, f, t * P:t * P + P], w2[:, f, :],
                                       start=(f == 0), stop=(f == FB - 1))
                mm.then_inc(ffn_ready, 1)

            hidden(0)
            hidden(1)
            feed_forward(0, 0)
            with pe.Fori(1, NB // 2) as i:
                for p in range(2):
                    hidden(i * 2 + p)
                    feed_forward(i * 2 + p - 1, 1 - p)
            feed_forward(NB - 1, 1)


def moe(core, layer):
    io, bank, X = core.io, core.bank, core.X
    st = Stage(core, f"e{layer}")
    slot_in, y_out = core.slot_in, core.y_out
    counted = 16 * SLOT_TILES // 4 * (layer - 1)
    gate_w = st.sb("gate_w", [P, NE])
    gate_b = st.sb("gate_b", [P, NE])
    b1all = st.sb("b1all", [P, NE, FB])
    b2all = st.sb("b2all", [P, NE, D])
    iota_e = st.sb("iota_e", [P, NE, NT])
    thresh = st.sb("thresh", [P, NE, NT])
    reset = st.sb("reset", [P, NE * NT])
    iota_j = st.sb("iota_j", [1, SLOT_TILES, NE])
    below = st.sb("below", [P, P], BF16)
    onesb = st.sb("onesb", [P, P], BF16)
    XF = core.XN
    score = st.sb("score", [P, NT, NE])
    best = st.sb("best", [P, NT, 8])
    best_at = st.sb("best_at", [P, NT, 8], U32)
    value = st.sb("value", [P, NT, TOPK])
    expert = st.sb("expert", [P, NT, TOPK])
    chosen = [st.sb(f"chosen{k}", [P, NE, NT]) for k in range(TOPK)]
    member = st.sb("member", [P, NE * NT])
    memberb = st.sb("memberb", [P, NE * NT], BF16)
    upto = st.sb("upto", [P, NE * NT])
    before = st.sb("before", [P, NE * NT], BF16)
    total = st.sb("total", [P, NE], BF16)
    filled = st.sb("filled", [P, NE, NT])
    ntile = st.sb("ntile", [P, NE])
    tile_end = st.sb("tile_end", [P, NE])
    tile_start = st.sb("tile_start", [P, NE])
    place = st.sb("place", [P, NE, NT])
    placed = filled
    slotf = st.sb("slotf", [P, TOPK, NT])
    quotient, rounded, slot_tile, slot_row = (st.sb(n, [P, TOPK, NT]) for n in ("quotient", "rounded", "slot_tile", "slot_row"))
    iota_p = st.sb("iota_p", [P, P], BF16)
    iota_s = st.sb("iota_s", [P, SLOT_TILES], BF16)
    number = st.sb("number", [P, TOPK * NT], BF16)
    partition = st.sb("partition", [P, 1])
    spare = st.sb("spare", [P, SLOT_TILES])
    on_tile = st.sb("on_tile", [P, TOPK * NT, SLOT_TILES], BF16)
    row_at, empty_at, wrap, token_at = (st.sb(n, [P, SLOT_TILES]) for n in ("row_at", "empty_at", "wrap", "token_at"))
    to_row, from_token = st.sb("to_row", [P, SLOT_TILES], U32), st.sb("from_token", [P, SLOT_TILES], U32)
    past = st.sb("past", [1, SLOT_TILES, NE])
    ownerf = st.sb("ownerf", [1, SLOT_TILES])
    owner = st.sb("owner", [1, SLOT_TILES], I32)
    gdiff = st.sb("gdiff", [P, NT])
    gexp = st.sb("gexp", [P, NT])
    gsum = st.sb("gsum", [P, NT])
    gate = st.sb("gate", [P, TOPK, NT])
    xs = st.sb("xs", [P, 4, D])
    xsT = st.sb("xsT", [P, 2, P])
    w1b = st.sb("w1b", [P, 4, FF])
    b1b = st.sb("b1b", [P, 4, FB])
    b2b = st.sb("b2b", [P, 4, D])
    hid = st.sb("hid", [P, 2, FB * P])
    ysb = st.sb("ysb", [P, 4, D])
    back = [st.sb(f"back{k}", [P, NT, D]) for k in range(TOPK)]
    xT = back[0][:].rearrange("p (b t) d -> p b (t d)", t=TT)
    halves = lambda x: x[:].rearrange("p t d -> p (t d)").bitcast(BF16)
    on_row = [halves(back[1])[:, k * NT * P:(k + 1) * NT * P].rearrange("p (t r) -> p t r", r=P) for k in range(TOPK)]
    whose = halves(back[0])[:, 0:TOPK * NT * 2 * SLOT_TILES].rearrange("p (i a j) -> p i a j", a=2, j=SLOT_TILES)

    gate_in, bias_in, tables_in = map(st.sem, ("gate_in", "bias_in", "tables_in"))
    ln_next, ln_1 = Norm(st, "ln_next"), Norm(st, "ln_1")
    turned, xT_ready, score_ready, score_biased = map(st.sem, ("turned", "xT_ready", "score_ready", "score_biased"))
    best_ready, best_at_ready, best_kept = map(st.sem, ("best_ready", "best_at_ready", "best_kept"))
    route_step, rank_ready, owner_ready = map(st.sem, ("route_step", "rank_ready", "owner_ready"))
    members_ready = st.sem("members_ready")
    gdiff_ready, gexp_ready = st.sem("gdiff_ready"), st.sem("gexp_ready")
    on_tile_ready = st.sem("on_tile_ready")
    split_done, on_row_ready, whose_ready = st.sem("split_done"), st.sem("on_row_ready"), st.sem("whose_ready")
    inverted, tables_ready, rows_out = st.sem("inverted"), st.sem("tables_ready"), st.sem("rows_out")
    from_next, to_next = st.sb("from_next", [P, 4, 1], U32), st.sb("to_next", [P, 4, 1], U32)
    from_ready, to_ready = st.lead("from_ready"), st.lead("to_ready")
    stored = st.sem("stored")
    back_in = [st.sem(f"back_in{b}") for b in range(NB)]
    slot_turned, xsT_ready, w1_ready, b1_ready = map(st.lead, ("slot_turned", "xsT_ready", "w1_ready", "b1_ready"))
    b2_ready, mm1_done, gelu_done = map(st.lead, ("b2_ready", "mm1_done", "gelu_done"))
    mm2_done, y_ready = map(st.lead, ("mm2_done", "y_ready"))
    ones_e, ones_set = st.sb("ones_e", [P, NE]), st.sem("ones_set")
    skip_added, first_added, second_added = map(st.sem, ("skip_added", "first_added", "second_added"))

    TABLES = 11
    WHOLE = 1.5 * 2 ** 23
    STEPS = SLOT_TILES + 3

    def steps(eng, step):
        for j in range(4):
            step(j, j)
        with eng.Fori(1, SLOT_TILES // 4 - 1) as i:
            for q in range(4):
                step(i * 4 + q, q, loop=True)
        for j in range(SLOT_TILES - 4, STEPS):
            step(j, j % 4)

    def has(j, lag, loop):
        return loop or 0 <= j - lag < SLOT_TILES

    with st.ctx, core.nc.Block() as block:
        @block.sync
        def _(sp):
            sp.dma_start(gate_w[:], io["gate_w"]).then_inc(gate_in, 16)
            sp.dma_start(gate_b[:], io["gate_b"].partition_broadcast(P)).then_inc(gate_in, 16)
            for dst, name in ((iota_e, "iota_e"), (thresh, "thresh"), (iota_j, "iota_j")):
                n = dst.shape[0]
                sp.dma_start(dst[:].rearrange("p a b -> p (a b)"), io[name].partition_broadcast(n)).then_inc(tables_in, 16)
            sp.dma_start(reset[:], io["reset"].partition_broadcast(P)).then_inc(tables_in, 16)
            sp.dma_start(below[:], io["below"]).then_inc(tables_in, 16)
            sp.dma_start(onesb[:], io["onesb"]).then_inc(tables_in, 16)
            sp.dma_start(b1all[:].rearrange("p e k -> p (e k)"), io["e_b1_t"]).then_inc(bias_in, 16)
            sp.dma_start(b2all[:].rearrange("p e n -> p (e n)"), io["e_b2"].partition_broadcast(P)).then_inc(bias_in, 16)
            for dst, name in ((spare, "spare"), (partition, "partition")):
                sp.dma_start(dst[:], io[name]).then_inc(tables_in, 16)
            for dst, name in ((iota_p, "iota_p"), (iota_s, "iota_s"), (number, "number")):
                sp.dma_start(dst[:], io[name].partition_broadcast(P)).then_inc(tables_in, 16)
            rows = core.rows.rearrange("(t p) d -> p t d", p=P)
            for b in range(NB):
                sp.dma_start(rows[:, b * TT:b * TT + TT, :], XF[:, b * TT:b * TT + TT, :]).then_inc(rows_out, 16)
            for q in range(4):
                sp.wait_ge(y_out[q], counted + 16 * SLOT_TILES // 4)
            results = core.results.rearrange("(t p) d -> p t d", p=P)
            for b in range(NB):
                for k in range(TOPK):
                    sp.dma_start(back[k][:, b * TT:b * TT + TT, :],
                                 results[:, k * NT + b * TT:k * NT + b * TT + TT, :]).then_inc(back_in[b], 16)
            if layer == 2:
                for b in range(NB):
                    sp.wait_ge(second_added, b * TT + TT)
                    sp.dma_start(core.out[b].rearrange("(t p) d -> p t d", p=P), X[:, b * TT:b * TT + TT, :])\
                        .then_inc(stored, 16)
                sp.wait_ge(stored, 16 * NB)

        @block.gpsimd
        def _(g):
            st.set_leads(g)
            g.wait_ge(tables_in, 16 * TABLES)
            g.wait_ge(on_tile_ready, 1)
            g.tensor_tensor(whose[:, :, 0, :], on_tile[:], number[:].unsqueeze(2).to_broadcast([P, TOPK * NT, SLOT_TILES]),
                            ALU.mult).then_inc(whose_ready, 1)
            g.wait_ge(rows_out, 16 * NB)
            g.wait_ge(tables_ready, 2)

            def load(q, tokens):
                g.indirect_dma_start(xs[:, q, :], None, core.rows, bass.IndirectOffsetOnAxis(tokens, 0))\
                    .then_inc(slot_in[q], 16)

            for j in range(3):
                load(j, from_token[:, j:j + 1])

            def step(j, q, loop=False):
                if loop or (j + 3 < SLOT_TILES):
                    if loop or j >= 1:
                        g.wait_ge(slot_turned, LEAD + j)
                    g.wait_ge(from_ready, LEAD + j + 1)
                    apart(g, core)
                    load((q + 3) % 4, from_next[:, (q + 3) % 4, :])
                if has(j, 3, loop):
                    m, mq = j - 3, (q + 1) % 4
                    g.wait_ge(to_ready, LEAD + m + 1)
                    g.wait_ge(y_ready, LEAD + m + 1)
                    apart(g, core)
                    g.indirect_dma_start(core.results, bass.IndirectOffsetOnAxis(to_next[:, mq, :], 0),
                                         ysb[:, mq, :], None).then_inc(y_out[mq], 16)
            steps(g, step)
            if layer == 1:
                for b in range(NB):
                    norm_pool(g, core, ln_next, b)
                    if b >= 1:
                        norm_pool(g, core, ln_1, b - 1)
                norm_pool(g, core, ln_1, NB - 1)

        @block.scalar
        def _(act):
            for b in range(NB):
                act.wait_ge(turned, b + 1)
                act.activation(xT[:, b, :], bank[:, b, :], ACT.Identity).then_inc(xT_ready, 1)
            act.wait_ge(gdiff_ready, 1)
            act.activation(gexp[:], gdiff[:], ACT.Exp).then_inc(gexp_ready, 1)
            act.preload_act_table(ACT.Gelu)

            def step(j, q, loop=False):
                if has(j, 1, loop):
                    m, mq = j - 1, (q + 3) % 4
                    act.wait_ge(b1_ready, LEAD + m + 1)
                    act.wait_ge(mm2_done, LEAD + m - 1)
                    act.wait_ge(mm1_done, LEAD + m + 1)
                    for f in range(FB):
                        ins = act.activation(hid[:, mq % 2, f * P:f * P + P], core.tiles(2 + mq % 2)[:, f, :],
                                             ACT.Gelu, bias=b1b[:, mq, f:f + 1])
                    ins.then_inc(gelu_done, 1)
            steps(act, step)
            if layer == 1:
                for b in range(NB):
                    norm_scalar(act, ln_next, X, core.XN, b)
                    if b >= 1:
                        norm_scalar(act, ln_1, core.XN, core.UN, b - 1)
                norm_scalar(act, ln_1, core.XN, core.UN, NB - 1)

        @block.vector
        def _(v):
            v.memset(ones_e[:], 1.0).then_inc(ones_set, 1)
            v.wait_ge(ones_set, 1)
            v.wait_ge(gate_in, 32)
            for b in range(NB):
                tiles = range(b * TT, b * TT + TT)
                v.wait_ge(score_ready, b + 1)
                v.tensor_tensor(score[:, b * TT:b * TT + TT, :], bank[:, 4 + b, 0:TT * NE].rearrange("p (t e) -> p t e", e=NE),
                                gate_b[:].unsqueeze(1).to_broadcast([P, TT, NE]), ALU.add).then_inc(score_biased, 1)
                v.wait_ge(score_biased, b + 1)
                for i in tiles:
                    v.max(best[:, i, :], score[:, i, :]).then_inc(best_ready, 1)
                v.wait_ge(best_ready, b * TT + TT)
                for i in tiles:
                    v.max_index(best_at[:, i, :], best[:, i, :], score[:, i, :]).then_inc(best_at_ready, 1)
            v.wait_ge(best_at_ready, NT)
            v.tensor_copy(value[:], best[:, :, 0:TOPK]).then_inc(best_kept, 1)
            v.tensor_copy(expert[:], best_at[:, :, 0:TOPK]).then_inc(best_kept, 1)
            v.wait_ge(best_kept, 2)
            v.wait_ge(tables_in, 16 * TABLES)
            done = [0]

            def then(ins):
                done[0] += 1
                ins.then_inc(route_step, 1)
                v.wait_ge(route_step, done[0])

            v.tensor_tensor(gdiff[:], value[:, :, 1], value[:, :, 0], ALU.subtract).then_inc(gdiff_ready, 1)
            for k in range(TOPK):
                ins = v.tensor_tensor(chosen[k][:], iota_e[:],
                                      expert[:, :, k].unsqueeze(1).to_broadcast([P, NE, NT]), ALU.is_equal)
            then(ins)
            flat = lambda x: x[:].rearrange("p e t -> p (e t)")
            then(v.tensor_tensor(member[:], flat(chosen[0]), flat(chosen[1]), ALU.add))
            v.tensor_copy(memberb[:], member[:])
            then(v.tensor_tensor_scan(upto[:], reset[:], member[:], 0.0, ALU.mult, ALU.add))
            v.tensor_copy(total[:], upto[:].rearrange("p (e t) -> p e t", t=NT)[:, :, NT - 1])
            v.tensor_tensor(before[:], upto[:], member[:], ALU.subtract).then_inc(members_ready, 1)
            v.wait_ge(rank_ready, 1)
            then(v.tensor_tensor(filled[:], bank[:, 3, 0:NE].unsqueeze(2).to_broadcast([P, NE, NT]), thresh[:],
                                 ALU.is_gt))
            then(v.tensor_reduce(ntile[:], filled[:], AX_X, ALU.add))
            then(v.tensor_tensor_scan(tile_end[:], ones_e[:], ntile[:], 0.0, ALU.mult, ALU.add))
            then(v.tensor_tensor(tile_start[:], tile_end[:], ntile[:], ALU.subtract))
            then(v.scalar_tensor_tensor(out=place[:], in0=tile_start[:].unsqueeze(2).to_broadcast([P, NE, NT]),
                                        scalar=float(P), in1=bank[:, 2, 0:NE * NT].rearrange("p (e t) -> p e t", t=NT),
                                        op0=ALU.mult, op1=ALU.add))
            for k in range(TOPK):
                then(v.tensor_tensor(placed[:], place[:], chosen[k][:], ALU.mult))
                then(v.tensor_reduce(slotf[:, k, :], placed[:].rearrange("p e t -> p t e"), AX_X, ALU.add))
            then(v.tensor_scalar(quotient[:], slotf[:], 1.0 / P, -(P - 1) / 2 / P, ALU.mult, ALU.add))
            then(v.tensor_scalar(rounded[:], quotient[:], WHOLE, None, ALU.add))
            then(v.tensor_scalar(slot_tile[:], rounded[:], -WHOLE, None, ALU.add))
            v.scalar_tensor_tensor(out=slot_row[:], in0=slot_tile[:], scalar=-float(P), in1=slotf[:],
                                   op0=ALU.mult, op1=ALU.add).then_inc(split_done, 1)
            flat_kt = lambda x: x[:].rearrange("p k t -> p (k t)")
            v.tensor_tensor(on_tile[:], iota_s[:].unsqueeze(1).to_broadcast([P, TOPK * NT, SLOT_TILES]),
                            flat_kt(slot_tile).unsqueeze(2).to_broadcast([P, TOPK * NT, SLOT_TILES]), ALU.is_equal)\
                .then_inc(on_tile_ready, 1)
            v.wait_ge(split_done, 1)
            for k in range(TOPK):
                v.tensor_tensor(on_row[k], iota_p[:].unsqueeze(1).to_broadcast([P, NT, P]),
                                slot_row[:, k, :].unsqueeze(2).to_broadcast([P, NT, P]), ALU.is_equal)\
                    .then_inc(on_row_ready, 1)
            v.wait_ge(on_tile_ready, 1)
            v.tensor_scalar(whose[:, :, 1, :], on_tile[:], partition[:], None, ALU.mult).then_inc(whose_ready, 1)
            v.wait_ge(inverted, 1)
            num, part = bank[:, 2, 0:SLOT_TILES], bank[:, 2, SLOT_TILES:2 * SLOT_TILES]
            v.scalar_tensor_tensor(out=empty_at[:], in0=num, scalar=0.0, in1=spare[:], op0=ALU.is_equal, op1=ALU.mult)\
                .then_inc(route_step, 1)
            v.tensor_scalar(wrap[:], num, float(NT), -float(NT * P), ALU.is_gt, ALU.mult).then_inc(route_step, 1)
            v.tensor_scalar(token_at[:], num, float(P), -float(P), ALU.mult, ALU.add).then_inc(route_step, 1)
            done[0] += 3
            v.wait_ge(route_step, done[0])
            then(v.tensor_tensor(row_at[:], token_at[:], part, ALU.add))
            v.tensor_tensor(to_row[:], row_at[:], empty_at[:], ALU.add).then_inc(tables_ready, 1)
            then(v.tensor_tensor(token_at[:], row_at[:], wrap[:], ALU.add))
            v.tensor_scalar(from_token[:], token_at[:], 0.0, None, ALU.max).then_inc(tables_ready, 1)
            then(v.tensor_tensor(past[:], tile_end[0:1, :].unsqueeze(1).to_broadcast([1, SLOT_TILES, NE]), iota_j[:],
                                 ALU.is_le))
            then(v.tensor_reduce(ownerf[:], past[:], AX_X, ALU.add))
            v.tensor_scalar(owner[:], ownerf[:], float(NE - 1), None, ALU.min).then_inc(owner_ready, 1)
            v.wait_ge(owner_ready, 1)
            v.wait_ge(bias_in, 32)
            v.wait_ge(core.experts_in, 16 * 2 * (NE // LOAD_EXPERTS))

            def step(j, q, loop=False):
                if loop or j + 3 < SLOT_TILES:
                    v.tensor_copy(from_next[:, (q + 3) % 4, :], from_token[:, bass.ds(j + 3, 1)]).then_inc(from_ready, 1)
                if has(j, 0, loop):
                    e = v.value_load(owner[0:1, bass.ds(j, 1)], min_val=0, max_val=NE - 1)
                    v.wait_ge(mm1_done, LEAD + j - 3)
                    v.wait_ge(gelu_done, LEAD + j - 3)
                    if loop or j >= 4:
                        v.wait_ge(y_ready, LEAD + j - 3)
                    apart(v, core)
                    v.tensor_copy(w1b[:, q, :], row(core.w1all, e)).then_inc(w1_ready, 1)
                    v.tensor_copy(b1b[:, q, :], row(b1all, e)).then_inc(b1_ready, 1)
                    v.tensor_copy(b2b[:, q, :], row(b2all, e)).then_inc(b2_ready, 1)
                    v.wait_ge(slot_turned, LEAD + j + 1)
                    v.tensor_copy(xsT[:, q % 2, :], core.tiles(q % 2)[:, 0, :]).then_inc(xsT_ready, 1)
                if has(j, 3, loop):
                    m, mq = j - 3, (q + 1) % 4
                    v.wait_ge(b2_ready, LEAD + m + 1)
                    if loop or m >= 4:
                        v.wait_ge(y_out[mq], counted + ((m - mq) * 4 if loop else (m // 4) * 16))
                    apart(v, core)
                    v.tensor_copy(to_next[:, mq, :], to_row[:, bass.ds(m, 1)]).then_inc(to_ready, 1)
                    v.wait_ge(mm2_done, LEAD + m + 1)
                    v.tensor_tensor(ysb[:, mq, :], core.tiles(4 + mq % 2)[:, 0, :], b2b[:, mq, :],
                                    ALU.add).then_inc(y_ready, 1)
            steps(v, step)
            v.wait_ge(gexp_ready, 1)
            then(v.tensor_scalar(gsum[:], gexp[:], 1.0, None, ALU.add))
            then(v.reciprocal(gate[:, 0, :], gsum[:]))
            then(v.tensor_tensor(gate[:, 1, :], gexp[:], gate[:, 0, :], ALU.mult))
            v.tensor_tensor(X[:], X[:], XF[:], ALU.add).then_inc(skip_added, 1)
            v.wait_ge(skip_added, 1)

            def add(k, i, done):
                v.scalar_tensor_tensor(out=X[:, i, :], in0=back[k][:, i, :], scalar=gate[:, k, i:i + 1],
                                       in1=X[:, i, :], op0=ALU.mult, op1=ALU.add).then_inc(done, 1)

            for b in range(NB):
                v.wait_ge(back_in[b], 16 * TOPK)
                for i in range(b * TT, b * TT + TT):
                    add(0, i, first_added)
                v.wait_ge(first_added, b * TT + TT)
                for i in range(b * TT, b * TT + TT):
                    add(1, i, second_added)
                if layer == 1:
                    v.wait_ge(second_added, b * TT + TT)
                    norm_stats(v, ln_next, X, b)
                    if b >= 1:
                        v.wait_ge(ln_next.normed, b * TT)
                        norm_stats(v, ln_1, core.XN, b - 1)
            if layer == 1:
                v.wait_ge(ln_next.normed, NT)
                norm_stats(v, ln_1, core.XN, NB - 1)
                v.wait_ge(ln_1.normed, NT)

        @block.tensor
        def _(pe):
            for b in range(NB):
                for t in range(TT):
                    tr = pe.transpose(core.tiles(b)[:, t, :], XF[:, b * TT + t, :], core.ident[:])
                tr.then_inc(turned, 1)
            pe.wait_ge(gate_in, 32)
            for b in range(NB):
                pe.wait_ge(xT_ready, b + 1)
                for t in range(TT):
                    mm = pe.matmul(bank[:, 4 + b, t * NE:t * NE + NE], xT[:, b, t * P:t * P + P], gate_w[:],
                                   start=True, stop=True)
                mm.then_inc(score_ready, 1)
            pe.wait_ge(tables_in, 16 * TABLES)
            pe.wait_ge(members_ready, 1)
            pe.matmul(bank[:, 2, 0:NE * NT], below[:], memberb[:], start=True, stop=False)
            pe.matmul(bank[:, 2, 0:NE * NT], onesb[:], before[:], start=False, stop=True)
            pe.matmul(bank[:, 3, 0:NE], onesb[:], total[:], start=True, stop=True).then_inc(rank_ready, 1)
            pe.wait_ge(split_done, 1)
            pe.wait_ge(whose_ready, 2)
            pe.wait_ge(on_row_ready, 2)
            for k in range(TOPK):
                for i in range(NT):
                    mm = pe.matmul(bank[:, 2, 0:2 * SLOT_TILES], on_row[k][:, i, :],
                                   whose[:, k * NT + i, :, :].rearrange("p a j -> p (a j)"),
                                   start=(k == 0 and i == 0), stop=(k == TOPK - 1 and i == NT - 1))
            mm.then_inc(inverted, 1)
            pe.wait_ge(owner_ready, 1)
            pe.wait_ge(core.experts_in, 16 * 2 * (NE // LOAD_EXPERTS))
            pe.wait_ge(tables_ready, 2)

            def step(j, q, loop=False):
                if has(j, 0, loop):
                    pe.wait_ge(slot_in[q], counted + ((j - q) * 4 if loop else (j // 4) * 16) + 16)
                    pe.wait_ge(xsT_ready, LEAD + j - 1)
                    pe.transpose(core.tiles(q % 2)[:, 0, :], xs[:, q, :], core.ident[:]).then_inc(slot_turned, 1)
                if has(j, 1, loop):
                    m, mq = j - 1, (q + 3) % 4
                    pe.wait_ge(w1_ready, LEAD + m + 1)
                    pe.wait_ge(xsT_ready, LEAD + m + 1)
                    pe.wait_ge(gelu_done, LEAD + m - 1)
                    for f in range(FB):
                        mm = pe.matmul(core.tiles(2 + mq % 2)[:, f, :], w1b[:, mq, f * P:f * P + P],
                                       xsT[:, mq % 2, :], start=True, stop=True)
                    mm.then_inc(mm1_done, 1)
                if has(j, 2, loop):
                    m, mq = j - 2, (q + 2) % 4
                    e = pe.value_load(owner[0:1, bass.ds(m, 1)], min_val=0, max_val=NE - 1)
                    pe.wait_ge(y_ready, LEAD + m - 1)
                    pe.wait_ge(gelu_done, LEAD + m + 1)
                    for f in range(FB):
                        mm = pe.matmul(core.tiles(4 + mq % 2)[:, 0, :], hid[:, mq % 2, f * P:f * P + P],
                                       core.w2all[:, bass.ds(e, 1), f, :].rearrange("p a n -> p (a n)"), start=(f == 0), stop=(f == FB - 1))
                    mm.then_inc(mm2_done, 1)
            steps(pe, step)


def attention(core):
    nc, io, bank, X = core.nc, core.io, core.bank, core.X
    st = Stage(core, "t")
    UNITS = NB * NH // 4
    ROWS = 6 * HD
    MID = 32
    Q_PARTS = (0, 0, 1, 0, 2, 1)
    K_PARTS = (0, 1, 0, 2, 0, 1)
    PLACED = len(Q_PARTS)
    SCALE = 1.0 / float(np.sqrt(HD))
    ROT = (7, 0)
    stacks = nc.dram_tensor("stacks", (2, NB, NH, ROWS, T), BF16).ap()

    vec = st.sb("vec", [P, 6])
    LN1G, LN1B, LN2G, LN2B, BQ, BK = range(6)
    wqkv = st.sb("wqkv", [P, 3 * D])
    bv = st.sb("bv", [P, D])
    rot = st.sb("rot", [P, P])
    cos, sin = st.sb("cos", [P, T]), st.sb("sin", [P, T])
    wo = st.sb("wo", [P, D])
    bo, b2 = st.sb("bo", [P, D]), st.sb("b2", [P, D])
    w1, b1 = st.sb("w1", [P, FF]), st.sb("b1", [P, FB])
    w2 = st.sb("w2", [P, FB, D])
    identb = st.sb("identb", [P, P], BF16)
    hide_k = st.sb("hide_k", [P, P], BF16)
    hide_q = st.sb("hide_q", [P, P], BF16)

    XB = core.XN
    V = st.sb("V", [P, NT, D])
    A = st.sb("A", [P, NT, D])
    uT = [st.sb(f"uT{p}", [P, T]) for p in range(2)]
    qk = st.sb("qk", [P, 2, T])
    ropes = st.sb("ropes", [P, 4, T])
    side, turnedqk = ropes[:, 0:2, :], ropes[:, 2:4, :]
    va = [st.sb(f"va{p}", [P, TT, 4, 32]) for p in range(2)]
    peak = [st.sb(f"peak{p}", [P, TT, MID + 4]) for p in range(2)]
    low = [st.sb(f"low{p}", [P, T], BF16) for p in range(2)]
    spread = st.sb("spread", [P, 4, P], BF16)
    UN = core.UN
    pa = UN[:].rearrange("p t d -> p (t d)").rearrange("p (s n) -> p s n", s=2)
    pb = st.sb("pb", [P, 2, T])
    token_major = lambda x: x.rearrange("p b (t d) -> p (b t) d", d=D)
    oT = st.sb("oT", [P, T])
    rsum = st.sb("rsum", [P, TT, 4])
    aT = uT
    XA = V
    hT = [st.sb("hT0", [P, FB, T]), ropes]
    spaces = [st.sb("stacks_sb", [P, 8, T], BF16), hT[0][:].rearrange("p f n -> p (f n)").bitcast(BF16)
              .rearrange("p (s n) -> p s n", n=T)]
    QS, KS = ([spaces[q // 2][:, 4 * (q % 2) + 2 * x:4 * (q % 2) + 2 * x + 2, :] for q in range(4)] for x in range(2))
    parts = [st.sb("parts", [P, 2 * 3, T], BF16), hT[0][:].rearrange("p f n -> p (f n)").bitcast(BF16)
             .rearrange("p (i n) -> p i n", n=T)]
    part = [[[parts[p][:, 3 * x + i, :] for i in range(3)] for x in range(2)] for p in range(2)]

    qkv_in, rope_in, w_in = st.sem("qkv_in"), st.sem("rope_in"), st.sem("w_in")
    low_set, va_set = st.sem("low_set"), st.sem("va_set")
    ln_2, ln_next = Norm(st, "ln_2"), Norm(st, "ln_next")
    un_turned, uT_ready, q_ready, k_ready = map(st.lead, ("un_turned", "uT_ready", "q_ready", "k_ready"))
    qk_ready, rot_ready, v_ready, v_kept = map(st.lead, ("qk_ready", "rot_ready", "v_ready", "v_kept"))
    cos_ready, sin_ready, rope_ready = map(st.lead, ("cos_ready", "sin_ready", "rope_ready"))
    part_ready = [st.sem(f"part_ready{x}") for x in range(2)]
    part_out = [[st.sem(f"part_out{x}_{p}") for p in range(2)] for x in range(2)]
    unit_in = [st.sem(f"unit_in{q}") for q in range(4)]
    va_ready = st.lead("va_ready")
    peak_scored, peak_read = st.lead("peak_scored"), st.lead("peak_read")
    peak_whole, peak_turned = st.lead("peak_whole"), st.lead("peak_turned")
    low_hi_ready, low_ready = st.lead("low_hi_ready"), st.lead("low_ready")
    sa_ready, pa_ready, sb_ready, pb_ready = map(st.lead, ("sa_ready", "pa_ready", "sb_ready", "pb_ready"))
    pa_used, pb_used = map(st.lead, ("pa_used", "pb_used"))
    oT_ready, oT_turned, rsum_ready, a_ready = map(st.lead, ("oT_ready", "oT_turned", "rsum_ready", "a_ready"))
    at_turned, aT_ready, proj_ready, xa_ready, xa_added = map(st.sem, ("at_turned", "aT_ready", "proj_ready", "xa_ready", "xa_added"))
    xa_turned, xaT_ready, h1_ready, h1_gelu = map(st.lead, ("xa_turned", "xaT_ready", "h1_ready", "h1_gelu"))
    ffn_ready, x_done, bias_added = st.lead("ffn_ready"), st.lead("x_done"), st.sem("bias_added")
    part_copied, rest_ready = st.sem("part_copied"), st.sem("rest_ready")

    PEAKS = [(3, (j,)) for j in range(4)] + [(2, (j,)) for j in range(4)] + [(1, (0, 1)), (1, (2, 3)), (0, (0, 1)), (0, (2, 3))]
    NP = len(PEAKS)

    def sweep(eng, prepare, step):
        prepare(0, 0, 0)
        for q in range(4):
            step(q, 0, q, True, first=(q == 0))
        with eng.Fori(1, UNITS // 4 - 1) as i:
            for q in range(4):
                step(i * 4 + q, i, q, True)
        for q in range(4):
            step(UNITS - 4 + q, UNITS // 4 - 1, q, q < 3)

    def after(i, q):
        return (i, q + 1) if q < 3 else (i + 1, 0)

    W_LOADS = 10
    UT = A[:].rearrange("p (b t) d -> p b (t d)", t=TT)

    with st.ctx, nc.Block() as block:
        @block.sync
        def _(sp):
            for dst, name in ((vec, "vec_b"), (wqkv, "wqkv")):
                sp.dma_start(dst[:], io[name]).then_inc(qkv_in, 16)
            sp.dma_start(bv[:], io["bv"].partition_broadcast(P)).then_inc(qkv_in, 16)
            for dst, name in ((rot, "rot"), (cos, "cos"), (sin, "sin")):
                sp.dma_start(dst[:], io[name]).then_inc(rope_in, 16)
            for dst, name in ((identb, "identb"), (hide_k, "hide_k"), (hide_q, "hide_q"), (spread, "spread"),
                              (wo, "wo"), (w1, "b_w1"), (b1, "b_b1_t")):
                sp.dma_start(dst[:], io[name]).then_inc(w_in, 16)
            for dst, name in ((bo, "bo"), (b2, "b_b2")):
                sp.dma_start(dst[:], io[name].partition_broadcast(P)).then_inc(w_in, 16)
            sp.dma_start(w2[:], io["b_w2"].rearrange("(f p) n -> p f n", p=P)).then_inc(w_in, 16)
            def keep(b, p):
                for x, pairs in ((0, Q_PARTS), (1, K_PARTS)):
                    sp.wait_ge(part_ready[x], b + 1)
                    for r, i in enumerate(pairs):
                        sp.dma_start(stacks[x, bass.ds(b, 1), :, r * HD:r * HD + HD, :].rearrange("a h d n -> (a h) d n"),
                                     part[p][x][i]).then_inc(part_out[x][p], 16)

            flat = stacks.rearrange("x b h r n -> x (b h) r n")

            def load(u, q):
                for x, S in ((0, QS), (1, KS)):
                    src = flat[x, bass.ds(u * 4, 4)].rearrange("(a s) r n -> a r s n", a=2)
                    for a in range(2):
                        sp.dma_start(S[q][64 * a:64 * a + ROWS, :, :], src[a]).then_inc(unit_in[q], 16)

            keep(0, 0)
            keep(1, 1)
            for x in range(2):
                sp.wait_ge(part_out[x][0], 16 * PLACED)
            load(0, 0)
            load(1, 1)
            keep(2, 0)
            keep(3, 1)
            for x in range(2):
                for p in range(2):
                    sp.wait_ge(part_out[x][p], 16 * PLACED * 2)
            load(2, 2)
            load(3, 3)
            with sp.Fori(0, UNITS // 4 - 1) as i:
                for q in range(4):
                    u = i * 4 + q
                    sp.wait_ge(sb_ready, LEAD + 2 * u + 2)
                    load(u + 4, q)

        @block.gpsimd
        def _(g):
            st.set_leads(g)
            for p in range(2):
                g.memset(peak[p][:], 0.0).then_inc(low_set, 1)
                g.memset(low[p][:], 0.0).then_inc(low_set, 1)
                g.memset(va[p][:], 0.0).then_inc(va_set, 1)
            g.wait_ge(va_set, 2)
            for p in range(2):
                g.memset(va[p][:, :, :, HD:HD + 1], 1.0).then_inc(va_set, 1)
            g.wait_ge(rope_in, 16 * 3)
            for b in range(NB):
                g.wait_ge(qk_ready, LEAD + 2 * b + 2)
                for x in range(2):
                    g.wait_ge(rope_ready, LEAD + 2 * b + x - 1)
                    g.tensor_tensor(side[:, x, :], qk[:, x, :], cos[:], ALU.mult).then_inc(cos_ready, 1)
            g.wait_ge(va_set, 4)
            g.wait_ge(v_kept, LEAD + NB)

            def values(u, p):
                tile0, col0 = u // 4 * TT, u % 4 * 32
                g.wait_ge(pb_used, LEAD + 2 * u - 2)
                apart(g, core)
                g.tensor_copy(va[p][:, :, :, 0:HD],
                              V[:, bass.ds(tile0, TT), bass.ds(col0, 32)].rearrange("p t (h d) -> p t h d", d=HD))\
                    .then_inc(va_ready, 1)

            values(0, 0)
            values(1, 1)
            g.wait_ge(w_in, 16 * W_LOADS)
            for B, bias in ((XB, bo), (X, b2)):
                g.tensor_tensor(B[:], B[:], bias[:].unsqueeze(1).to_broadcast([P, NT, D]), ALU.add).then_inc(bias_added, 1)
            with g.Fori(1, UNITS // 2) as i:
                for p in range(2):
                    values(i * 2 + p, p)
            for b in range(NB):
                norm_pool(g, core, ln_2, b)
            g.wait_ge(bias_added, 2)
            for b in range(NB):
                g.tensor_tensor(X[:, b * TT:b * TT + TT, :], X[:, b * TT:b * TT + TT, :],
                                XA[:, b * TT:b * TT + TT, :], ALU.add).then_inc(xa_added, 1)
            for b in range(NB):
                norm_pool(g, core, ln_next, b)

        @block.scalar
        def _(act):
            act.wait_ge(qkv_in, 16 * 3)
            for b in range(NB + 1):
                if b < NB:
                    act.wait_ge(un_turned, LEAD + b + 1)
                    act.wait_ge(v_ready, LEAD + b - 1)
                    act.activation(uT[b % 2][:], bank[:, b, :], ACT.Identity, bias=vec[:, LN1B:LN1B + 1],
                                   scale=vec[:, LN1G:LN1G + 1]).then_inc(uT_ready, 1)
                for x in range(2):
                    if b < NB:
                        act.wait_ge((q_ready, k_ready)[x], LEAD + b + 1)
                        act.wait_ge(cos_ready, LEAD + 2 * b + x - 1)
                        act.wait_ge(rot_ready, LEAD + 2 * b + x - 1)
                        act.activation(qk[:, x, :], bank[:, 4 + x, :], ACT.Identity,
                                       bias=vec[:, BQ + x:BQ + x + 1]).then_inc(qk_ready, 1)
                if b >= 1:
                    for x in range(2):
                        k = 2 * (b - 1) + x
                        act.wait_ge(rope_ready, LEAD + k + 1)
                        if b >= 3:
                            act.wait_ge(part_out[x][(b - 1) % 2], 16 * PLACED)
                        act.activation(part[(b - 1) % 2][x][0], turnedqk[:, x, :], ACT.Identity).then_inc(part_copied, 1)
                        act.wait_ge(rest_ready, k + 1)
                        act.activation(part[(b - 1) % 2][x][1], turnedqk[:, x, :], ACT.Identity).then_inc(part_copied, 1)
            act.preload_act_table(ACT.Exp)

            act.wait_ge(low_set, 4)

            def prepare(u, i, q):
                p = q % 2
                act.wait_ge(peak_turned, LEAD + u + 1)
                act.activation(low[p][0:MID + 4, :], bank[0:MID + 4, 1, :], ACT.Identity, scale=-1.0)\
                    .then_inc(low_hi_ready, 1)

            def step(u, i, q, more, first=False):
                p = q % 2
                for j in range(4):
                    if j == 3 and more:
                        prepare(u + 1, *after(i, q))
                    act.wait_ge(sa_ready, LEAD + 4 * u + j + 1)
                    act.wait_ge(pa_used, LEAD + 4 * u + j - 1)
                    act.activation(pa[:, j % 2, :], bank[:, 2 + 2 * (j % 2):4 + 2 * (j % 2), :].rearrange("p a n -> p (a n)"),
                                   ACT.Exp, scale=SCALE).then_inc(pa_ready, 1)
                    if j % 2:
                        act.wait_ge(sb_ready, LEAD + 2 * u + j // 2 + 1)
                        act.wait_ge(pb_used, LEAD + 2 * u + j // 2 - 1)
                        act.activation(pb[:, j // 2, :], bank[:, 6, :], ACT.Exp, scale=SCALE).then_inc(pb_ready, 1)
            sweep(act, prepare, step)
            act.preload_act_table(ACT.Gelu)
            act.wait_ge(w_in, 16 * W_LOADS)
            for b in range(NB):
                act.wait_ge(at_turned, b + 1)
                if b >= 2:
                    act.wait_ge(proj_ready, b - 1)
                act.activation(aT[b % 2][:], bank[:, b, :], ACT.Identity).then_inc(aT_ready, 1)
            act.wait_ge(proj_ready, NB)
            for b in range(NB):
                norm_scalar(act, ln_2, XA, UN, b)
            for b in range(NB):
                act.wait_ge(xa_turned, LEAD + b + 1)
                act.wait_ge(a_ready, LEAD + UNITS)
                act.activation(UT[:, b, :], bank[:, b, :], ACT.Identity, bias=vec[:, LN2B:LN2B + 1],
                               scale=vec[:, LN2G:LN2G + 1]).then_inc(xaT_ready, 1)
            with act.Fori(0, NB // 2) as i:
                for p in range(2):
                    b = i * 2 + p
                    act.wait_ge(ffn_ready, LEAD + b - 1)
                    for f in range(FB):
                        act.wait_ge(h1_ready, LEAD + FB * b + f + 1)
                        act.activation(hT[p][:, f, :], bank[:, 4 + f, :], ACT.Gelu,
                                       bias=b1[:, f:f + 1]).then_inc(h1_gelu, 1)

        @block.vector
        def _(v):
            v.wait_ge(qkv_in, 16 * 3)
            v.wait_ge(rope_in, 16 * 3)
            for b in range(NB):
                v.wait_ge(v_ready, LEAD + b + 1)
                v.tensor_tensor(V[:, b * TT:b * TT + TT, :], core.tiles(6),
                                bv[:].unsqueeze(1).to_broadcast([P, TT, D]), ALU.add).then_inc(v_kept, 1)
                for x in range(2):
                    k = 2 * b + x
                    v.wait_ge(rot_ready, LEAD + k + 1)
                    if b >= 1:
                        v.wait_ge(part_ready[x], b)
                    v.tensor_tensor(turnedqk[:, x, :], core.bank[:, ROT[x], :], sin[:], ALU.mult).then_inc(sin_ready, 1)
                for x in range(2):
                    k = 2 * b + x
                    v.wait_ge(sin_ready, LEAD + k + 1)
                    v.wait_ge(cos_ready, LEAD + k + 1)
                    v.tensor_tensor(turnedqk[:, x, :], turnedqk[:, x, :], side[:, x, :], ALU.add).then_inc(rope_ready, 1)
                for x in range(2):
                    k = 2 * b + x
                    v.wait_ge(part_copied, 2 * k + 1)
                    v.tensor_tensor(turnedqk[:, x, :], turnedqk[:, x, :], part[b % 2][x][0], ALU.subtract).then_inc(rest_ready, 1)
                    v.wait_ge(part_copied, 2 * k + 2)
                    v.tensor_tensor(part[b % 2][x][2], turnedqk[:, x, :], part[b % 2][x][1], ALU.subtract).then_inc(part_ready[x], 1)

            v.wait_ge(low_set, 4)

            def prepare(u, i, q):
                p = q % 2
                for n, (qt, js) in enumerate(PEAKS):
                    v.wait_ge(peak_scored, LEAD + NP * u + n + 1)
                    w = (qt + 1) * P
                    v.tensor_reduce(peak[p][:, qt, js[0]:js[-1] + 1],
                                    bank[:, n % 2, 0:len(js) * w].rearrange("p (j n) -> p j n", n=w),
                                    AX_X, ALU.max).then_inc(peak_read, 1)
                v.wait_ge(peak_read, LEAD + NP * u + NP)
                apart(v, core)
                v.tensor_copy(peak[p][:, :, MID:MID + 4], peak[p][:, :, 0:4]).then_inc(peak_whole, 1)
                v.wait_ge(low_hi_ready, LEAD + u + 1)
                second = slice(MID, MID + 4)
                v.scalar_tensor_tensor(out=low[p][second, :], in0=bank[second, 1, :], scalar=-1.0,
                                       in1=low[p][second, :], op0=ALU.mult, op1=ALU.subtract).then_inc(low_ready, 1)

            def normalise(u):
                v.wait_ge(oT_turned, LEAD + u + 1)
                o = core.tiles(0).rearrange("p t (h c) -> p t h c", c=32)
                v.reciprocal(rsum[:], o[:, :, :, HD]).then_inc(rsum_ready, 1)
                v.wait_ge(rsum_ready, LEAD + u + 1)
                apart(v, core)
                v.tensor_tensor(A[:, bass.ds(u // 4 * TT, TT), bass.ds(u % 4 * 32, 32)]
                                .rearrange("p t (h d) -> p t h d", d=HD), o[:, :, :, 0:HD],
                                rsum[:].unsqueeze(3).to_broadcast([P, TT, 4, HD]), ALU.mult).then_inc(a_ready, 1)

            def step(u, i, q, more, first=False):
                if more:
                    prepare(u + 1, *after(i, q))
                if not first:
                    normalise(u - 1)
                v.wait_ge(pb_used, LEAD + 2 * u + 2)
                v.tensor_copy(oT[:], bank[:, 7, :]).then_inc(oT_ready, 1)

            sweep(v, prepare, step)
            normalise(UNITS - 1)
            v.wait_ge(bias_added, 2)
            for b in range(NB):
                v.wait_ge(proj_ready, b + 1)
                v.tensor_tensor(XA[:, b * TT:b * TT + TT, :], core.tiles(4 + b), XB[:, b * TT:b * TT + TT, :],
                                ALU.add).then_inc(xa_ready, 1)
                v.wait_ge(xa_ready, b + 1)
                norm_stats(v, ln_2, XA, b)
            v.wait_ge(xa_added, NB)
            for b in range(NB):
                v.wait_ge(ffn_ready, LEAD + b + 1)
                v.tensor_tensor(X[:, b * TT:b * TT + TT, :], X[:, b * TT:b * TT + TT, :], core.tiles(b % 2),
                                ALU.add).then_inc(x_done, 1)
                if b >= 1:
                    norm_apply(v, ln_next, X, core.XN, b - 1)
                v.wait_ge(x_done, LEAD + b + 1)
                norm_stats(v, ln_next, X, b)
            norm_apply(v, ln_next, X, core.XN, NB - 1)
            v.wait_ge(ln_next.normed, NT)

        @block.tensor
        def _(pe):
            for b in range(NB):
                for t in range(TT):
                    tr = pe.transpose(core.tiles(b)[:, t, :], UN[:, b * TT + t, :], core.ident[:])
                tr.then_inc(un_turned, 1)
            for b in range(NB):
                pe.wait_ge(uT_ready, LEAD + b + 1)
                if b == 0:
                    pe.wait_ge(qkv_in, 16 * 3)
                pe.wait_ge(qk_ready, LEAD + 2 * b)
                pe.matmul(bank[:, 4, :], wqkv[:, 0:D], uT[b % 2][:], start=True, stop=True).then_inc(q_ready, 1)
                pe.matmul(bank[:, 5, :], wqkv[:, D:2 * D], uT[b % 2][:], start=True, stop=True).then_inc(k_ready, 1)
                pe.wait_ge(v_kept, LEAD + b)
                for t in range(TT):
                    mm = pe.matmul(core.tiles(6)[:, t, :], uT[b % 2][:, t * P:t * P + P], wqkv[:, 2 * D:],
                                   start=True, stop=True)
                mm.then_inc(v_ready, 1)
                if b == 0:
                    pe.wait_ge(rope_in, 16 * 3)
                for x in range(2):
                    pe.wait_ge(sin_ready, LEAD + 2 * b + x - 1)
                    pe.wait_ge(qk_ready, LEAD + 2 * b + x + 1)
                    pe.matmul(bank[:, ROT[x], :], rot[:], qk[:, x, :], start=True, stop=True).then_inc(rot_ready, 1)

            pe.wait_ge(w_in, 16 * W_LOADS)
            pe.wait_ge(low_set, 4)
            pe.wait_ge(uT_ready, LEAD + NB)
            pe.wait_ge(qk_ready, LEAD + 2 * NB)
            pe.wait_ge(sin_ready, LEAD + 2 * NB)
            pe.wait_ge(v_kept, LEAD + NB)

            def peaks(u, q, turns):
                for n in turns:
                    qt, js = PEAKS[n]
                    if n == 0:
                        pe.wait_ge(a_ready, LEAD + u - 2)
                    elif n == 1:
                        pe.wait_ge(low_ready, LEAD + u)
                    else:
                        pe.wait_ge(peak_read, LEAD + NP * u + n - 1)
                    w = (qt + 1) * P
                    for i, j in enumerate(js):
                        r = slice(64 * (j // 2), 64 * (j // 2) + ROWS)
                        o = bank[:, n % 2, i * w:i * w + w]
                        pe.matmul(o, QS[q][r, j % 2, qt * P:qt * P + P], KS[q][r, j % 2, 0:w],
                                  start=True, stop=False, skip_group_check=True)
                        mm = pe.matmul(o[:, qt * P:], identb[:], hide_k[:], start=False, stop=True, skip_group_check=True)
                    mm.then_inc(peak_scored, 1)

            def turn_peaks(u, p):
                pe.wait_ge(peak_whole, LEAD + u + 1)
                apart(pe, core)
                for t in range(TT):
                    mm = pe.transpose(bank[0:MID + 4, 1, t * P:t * P + P], peak[p][:, t, :], core.ident[:])
                mm.then_inc(peak_turned, 1)

            def prepare(u, i, q):
                pe.wait_ge(unit_in[q], 64 * (i + 1))
                peaks(u, q, range(NP))
                turn_peaks(u, q % 2)

            def scores(u, q, j):
                r = slice(64 * (j // 2), 64 * (j // 2) + ROWS)
                first = 2 + 2 * (j % 2)
                pe.wait_ge(pa_ready, LEAD + 4 * u + j - 1)
                for kt, o in ((0, bank[:, first, :]), (1, bank[:, first + 1, 0:3 * P]), (3, bank[:, first + 1, 3 * P:])):
                    pe.matmul(o, KS[q][r, j % 2, kt * P:kt * P + P], QS[q][r, j % 2, kt * P:],
                              start=True, stop=False, skip_group_check=True)
                    pe.matmul(o, spread[:, j, :], low[q % 2][:, kt * P:], start=False, stop=False, skip_group_check=True)
                    mm = pe.matmul(o[:, 0:P], identb[:], hide_q[:], start=False, stop=True, skip_group_check=True)
                mm.then_inc(sa_ready, 1)
                if j % 2 == 0:
                    pe.wait_ge(pb_ready, LEAD + 2 * u + j // 2)
                o = bank[:, 6, 2 * P * (j % 2):2 * P * (j % 2) + 2 * P]
                pe.matmul(o, KS[q][r, j % 2, 2 * P:3 * P], QS[q][r, j % 2, 2 * P:], start=True, stop=False,
                          skip_group_check=True)
                pe.matmul(o, spread[:, j, :], low[q % 2][:, 2 * P:], start=False, stop=False, skip_group_check=True)
                mm = pe.matmul(o[:, 0:P], identb[:], hide_q[:], start=False, stop=True, skip_group_check=True)
                if j % 2:
                    mm.then_inc(sb_ready, 1)

            def outputs(u, p, j, tiles):
                if 0 in tiles:
                    pe.wait_ge(pa_ready, LEAD + 4 * u + j + 1)
                for kt in tiles:
                    at_col = (0, T, None, T + 3 * P)[kt]
                    mm = pe.matmul(bank[32 * j:32 * j + 32, 7, kt * P:], va[p][:, kt, j, :],
                                   pa[:, j % 2, at_col:at_col + T - kt * P], start=(kt == 0), stop=False,
                                   skip_group_check=True)
                if 3 in tiles:
                    mm.then_inc(pa_used, 1)

            def last_outputs(u, p, s):
                pe.wait_ge(pb_ready, LEAD + 2 * u + s + 1)
                for a in range(2):
                    j = 2 * s + a
                    mm = pe.matmul(bank[32 * j:32 * j + 32, 7, 2 * P:], va[p][:, 2, j, :],
                                   pb[:, s, 2 * P * a:2 * P * a + 2 * P], start=False, stop=True, skip_group_check=True)
                mm.then_inc(pb_used, 1)

            def turn_output(u):
                pe.wait_ge(oT_ready, LEAD + u + 1)
                for t in range(TT):
                    mm = pe.transpose(core.tiles(0)[:, t, :], oT[:, t * P:t * P + P], core.ident[:])
                mm.then_inc(oT_turned, 1)

            def step(u, i, q, more, first=False):
                p, (next_i, next_q) = q % 2, after(i, q)

                pe.wait_ge(low_ready, LEAD + u + 1)
                pe.wait_ge(va_ready, LEAD + u + 1)
                if more:
                    pe.wait_ge(unit_in[next_q], 64 * (next_i + 1))

                def peak_turns(k):
                    if more:
                        peaks(u + 1, next_q, range(2 * k, 2 * k + 2))

                peak_turns(0)
                scores(u, q, 0)
                peak_turns(1)
                scores(u, q, 1)
                peak_turns(2)
                pe.wait_ge(oT_ready, LEAD + u)
                outputs(u, p, 0, (0,))
                peak_turns(3)
                outputs(u, p, 0, (1, 3))
                peak_turns(4)
                scores(u, q, 2)
                outputs(u, p, 1, (0,))
                peak_turns(5)
                outputs(u, p, 1, (1, 3))
                scores(u, q, 3)
                if more:
                    turn_peaks(u + 1, 1 - p)
                last_outputs(u, p, 0)
                if not first:
                    turn_output(u - 1)
                outputs(u, p, 2, (0, 1, 3))
                outputs(u, p, 3, (0, 1, 3))
                last_outputs(u, p, 1)

            sweep(pe, prepare, step)
            turn_output(UNITS - 1)
            pe.wait_ge(a_ready, LEAD + UNITS)
            for b in range(NB):
                for t in range(TT):
                    tr = pe.transpose(core.tiles(b)[:, t, :], A[:, b * TT + t, :], core.ident[:])
                tr.then_inc(at_turned, 1)
            for b in range(NB):
                pe.wait_ge(aT_ready, b + 1)
                for t in range(TT):
                    mm = pe.matmul(core.tiles(4 + b)[:, t, :], aT[b % 2][:, t * P:t * P + P], wo[:], start=True, stop=True)
                mm.then_inc(proj_ready, 1)
            for b in range(NB):
                pe.wait_ge(ln_2.normed, b * TT + TT)
                for t in range(TT):
                    tr = pe.transpose(core.tiles(b)[:, t, :], UN[:, b * TT + t, :], core.ident[:])
                tr.then_inc(xa_turned, 1)
            pe.wait_ge(xaT_ready, LEAD + NB)

            def hidden(b):
                for f in range(FB):
                    pe.wait_ge(h1_gelu, LEAD + FB * b + f - FB + 1)
                    pe.matmul(bank[:, 4 + f, :], w1[:, f * P:f * P + P], row(UT, b),
                              start=True, stop=True).then_inc(h1_ready, 1)

            def feed_forward(b, p):
                pe.wait_ge(h1_gelu, LEAD + FB * b + FB)
                pe.wait_ge(x_done, LEAD + b - 1)
                for t in range(TT):
                    for f in range(FB):
                        mm = pe.matmul(core.tiles(p)[:, t, :], hT[p][:, f, t * P:t * P + P], w2[:, f, :],
                                       start=(f == 0), stop=(f == FB - 1))
                mm.then_inc(ffn_ready, 1)

            hidden(0)
            hidden(1)
            feed_forward(0, 0)
            with pe.Fori(1, NB // 2) as i:
                for p in range(2):
                    hidden(i * 2 + p)
                    feed_forward(i * 2 + p - 1, 1 - p)
            feed_forward(NB - 1, 1)


def build(nc, io, out):
    with ExitStack() as ctx:
        core = Core(nc, ctx, io, out)
        mamba(core)
        moe(core, 1)
        attention(core)
        moe(core, 2)


def constants():
    bf16 = mybir.dt.np(BF16)
    line = lambda x: np.ascontiguousarray(x, dtype=np.float32).reshape(-1)
    grid = np.zeros((NE, NT))
    inverse = (np.float32(1.0) / np.float32(10000.0) ** (np.arange(0, HD, 2, dtype=np.float32) / np.float32(HD))).astype(np.float32)
    angle = np.tile(np.arange(T, dtype=np.float32)[None, :] * np.tile(inverse, 2)[:, None], (NH, 1))
    swap = np.zeros((HD, HD), np.float32)
    for d in range(HD // 2):
        swap[d + HD // 2, d] = -1.0
        swap[d, d + HD // 2] = 1.0
    later = np.triu(np.full((P, P), FAR, np.float32), 1)
    eye = np.eye(P, dtype=np.float32)
    spread = np.zeros((P, 4, P), np.float32)
    for j in range(4):
        spread[[j, 32 + j], j, :] = 1.0
    return dict(cos=np.cos(angle), sin=np.sin(angle), rot=np.kron(np.eye(NH, dtype=np.float32), swap),
                hide_k=later.astype(bf16), hide_q=later.T.astype(bf16),
                spread=spread.astype(bf16), ident=eye, identb=eye.astype(bf16),
                pick=np.tile(np.eye(32, dtype=np.float32), (3, 1)),
                iota_e=line(grid + np.arange(NE)[:, None]), thresh=line(grid + P * np.arange(NT)),
                reset=line(grid + (np.arange(NT) > 0)),
                iota_j=line(np.zeros((SLOT_TILES, NE)) + np.arange(SLOT_TILES)[:, None]),
                iota_p=np.arange(P).astype(bf16), iota_s=np.arange(SLOT_TILES).astype(bf16),
                number=(1 + np.arange(TOPK * NT)).astype(bf16), partition=np.arange(P, dtype=np.float32)[:, None],
                spare=(P * (TOPK * NT + 1 + np.arange(SLOT_TILES))[None, :] + np.arange(P)[:, None]).astype(np.float32),
                below=np.triu(np.ones((P, P)), 1).astype(bf16),
                onesb=np.ones((P, P), bf16))


def layout(i):
    a = {k: np.asarray(v) for k, v in i.items()}
    A, B, E = "L0_attn_a_", "L0_attn_b_", "L0_ffn_"
    col = lambda x: x.reshape(-1, P).T
    return dict(
        x=a[A + "x"], in_proj_t=a[A + "in_proj_w"].T, conv_w=a[A + "conv_w"],
        vec_a=np.stack([a[A + n] for n in ("ln1_g", "ln1_b", "conv_b", "dt_proj_b", "D_param", "ln2_g", "ln2_b")], 1),
        x_proj_t=a[A + "x_proj_w"].T, dt_proj_t=a[A + "dt_proj_w"].T, a_log=a[A + "A_log"],
        out_proj_t=a[A + "out_proj_w"].T, a_w1_t=a[A + "w1"].T, a_b1_t=col(a[A + "b1"]),
        a_w2_t=a[A + "w2"].T, a_b2=a[A + "b2"],
        vec_b=np.stack([a[B + n] for n in ("ln1_g", "ln1_b", "ln2_g", "ln2_b")] +
                       [a[B + "bqkv"][0:D], a[B + "bqkv"][D:2 * D]], 1),
        wqkv=a[B + "Wqkv"], bv=a[B + "bqkv"][2 * D:], wo=a[B + "Wo"], bo=a[B + "bo"],
        b_w1=a[B + "W1"], b_b1_t=col(a[B + "b1"]), b_w2=a[B + "W2"], b_b2=a[B + "b2"],
        gate_w=a[E + "gate_w"], gate_b=a[E + "gate_b"], e_w1=a[E + "w1"], e_w2=a[E + "w2"],
        e_b1_t=a[E + "b1"].reshape(NE * FB, P).T, e_b2=a[E + "b2"].reshape(-1),
    )


def kernel(**inputs):
    import concourse.bacc as _bacc
    from concourse.bass_utils import run_bass_kernel_spmd as _run

    nc = _bacc.Bacc("TRN2", target_bir_lowering=False, num_devices=1)
    arrays = {k: np.ascontiguousarray(v) for k, v in {**layout(inputs), **constants()}.items()}
    io = {k: nc.dram_tensor(f"in_{k}", v.shape, mybir.dt.from_np(v.dtype), kind="ExternalInput").ap()
          for k, v in arrays.items()}
    out = nc.dram_tensor("out_x", (NB, T, D), F32, kind="ExternalOutput").ap()
    build(nc, io, out)
    r = _run(nc, [{f"in_{k}": v for k, v in arrays.items()}], core_ids=[0])
    return r.results[0]["out_x"]
```
